# Optimizing a Trainium2 kernel written in Bass

```python
import numpy as np
import jax
import jax.numpy as jnp

def _softmax(x, axis=-1):
    return jax.nn.softmax(x, axis=axis)

def _gelu(x):
    return jax.nn.gelu(x, approximate=True)

def _silu(x):
    return jax.nn.silu(x)

def _sigmoid(x):
    return jax.nn.sigmoid(x)

def _layernorm(x, axis=-1, eps=1e-05):
    m = jnp.mean(x, axis=axis, keepdims=True)
    v = jnp.var(x, axis=axis, keepdims=True)
    return (x - m) / jnp.sqrt(v + eps)

def _scatter_add(tgt, idx, src, axis=0):
    return tgt.at[idx].add(src)

def _segment_sum(src, seg, n):
    return jax.ops.segment_sum(src, seg, n)
kernel_name = 'mk_adaln_d1_jaxref_r4_f41749'

def setup_inputs(seed: int=0):
    np.random.seed(seed)
    _w = jnp.asarray

    def _L0_attn_setup():
        import jax, jax.numpy as jnp
        import numpy as np
        CHUNK = 32
        EPS_L2 = 1e-06
        EPS_RMS = 1e-05
        NUM_HEADS = 4

        def _causal_dwconv_silu(x, w):
            k = w.shape[1]
            l = x.shape[1]
            xp = jnp.pad(x, ((0, 0), (k - 1, 0), (0, 0)))
            out = sum((w[:, j] * xp[:, j:j + l, :] for j in range(k)))
            return jax.nn.silu(out)

        def _l2norm(x):
            return x * jax.lax.rsqrt(jnp.sum(x * x, -1, keepdims=True) + EPS_L2)

        def _delta_rule_chunkwise(q, k, v, beta, c=CHUNK):
            b, h, l, dk = q.shape
            dv = v.shape[-1]
            n = l // c
            q = _l2norm(q)
            k = _l2norm(k)
            v = v * beta[..., None]
            kb = k * beta[..., None]
            qc = q.reshape(b, h, n, c, dk)
            kc = k.reshape(b, h, n, c, dk)
            vc = v.reshape(b, h, n, c, dv)
            kbc = kb.reshape(b, h, n, c, dk)
            strict_lower = jnp.tril(jnp.ones((c, c), bool), -1)
            attn = -jnp.einsum('bhnik,bhnjk->bhnij', kbc, kc)
            attn = jnp.where(strict_lower, attn, 0.0)
            for i in range(1, c):
                upd = jnp.einsum('bhnj,bhnjm->bhnm', attn[..., i, :], attn[..., :, :i])
                attn = attn.at[..., i, :i].add(upd)
            attn = attn + jnp.eye(c, dtype=attn.dtype)
            u = attn @ vc
            w = attn @ kbc
            incl_lower = jnp.tril(jnp.ones((c, c), bool))

            def step(S, inp):
                q_i, k_i, u_i, w_i = inp
                a = jnp.where(incl_lower, jnp.einsum('bhik,bhjk->bhij', q_i, k_i), 0.0)
                u_new = u_i - w_i @ S
                o_i = q_i @ S + a @ u_new
                S = S + jnp.einsum('bhck,bhcv->bhkv', k_i, u_new)
                return (S, o_i)
            S0 = jnp.zeros((b, h, dk, dv), q.dtype)
            xs = tuple((jnp.moveaxis(x, 2, 0) for x in (qc, kc, u, w)))
            S, o = jax.lax.scan(step, S0, xs)
            o = jnp.moveaxis(o, 0, 2).reshape(b, h, l, dv)
            return (o, S)

        def _ema(v, gamma):
            vt = jnp.moveaxis(v, 2, 0)
            gt = jnp.moveaxis(gamma, 2, 0)[..., None]

            def step(s, xg):
                x, g = xg
                s = g * s + (1.0 - g) * x
                return (s, s)
            s0 = jnp.zeros(v.shape[:2] + v.shape[-1:], v.dtype)
            _, out = jax.lax.scan(step, s0, (vt, gt))
            return jnp.moveaxis(out, 0, 2)

        def _forward(hs, Wq, Wk, Wv, Wb, Wdec, Wmix, mix_bias, wq_conv, wk_conv, wv_conv, onorm_w, Wo):
            b, l, d = hs.shape
            h = NUM_HEADS
            q = _causal_dwconv_silu(hs @ Wq.T, wq_conv)
            k = _causal_dwconv_silu(hs @ Wk.T, wk_conv)
            v = _causal_dwconv_silu(hs @ Wv.T, wv_conv)
            dk = q.shape[-1] // h
            dv = v.shape[-1] // h
            q = q.reshape(b, l, h, dk)
            k = k.reshape(b, l, h, dk)
            v = v.reshape(b, l, h, dv)
            beta = jax.nn.sigmoid(hs @ Wb.T)
            qd = jnp.transpose(q, (0, 2, 1, 3))
            kd = jnp.transpose(k, (0, 2, 1, 3))
            vd = jnp.transpose(v, (0, 2, 1, 3))
            bd = jnp.transpose(beta, (0, 2, 1))
            o_d, _S = _delta_rule_chunkwise(qd, kd, vd, bd)
            o_d = jnp.transpose(o_d, (0, 2, 1, 3))
            gamma = jnp.transpose(jax.nn.sigmoid(hs @ Wdec.T), (0, 2, 1))
            ema_out = jnp.transpose(_ema(vd, gamma), (0, 2, 1, 3))
            mix = jax.nn.sigmoid(hs @ Wmix.T + mix_bias)[..., None]
            o = (1.0 - mix) * o_d + mix * ema_out
            o = o * jax.lax.rsqrt(jnp.mean(o * o, -1, keepdims=True) + EPS_RMS) * onorm_w
            return o.reshape(b, l, h * dv) @ Wo.T
        key = jax.random.key(seed)
        ks = jax.random.split(key, 12)
        B, L, D, H, K = (2, 1024, 256, 4, 4)
        s = 0.02
        f = jnp.float32
        return {'hidden_states': jax.random.normal(ks[0], (B, L, D), f), 'Wq': jax.random.normal(ks[1], (D, D), f) * s, 'Wk': jax.random.normal(ks[2], (D, D), f) * s, 'Wv': jax.random.normal(ks[3], (D, D), f) * s, 'Wb': jax.random.normal(ks[4], (H, D), f) * s, 'Wdec': jax.random.normal(ks[5], (H, D), f) * s, 'Wmix': jax.random.normal(ks[6], (H, D), f) * s, 'mix_bias': jnp.zeros((H,), f), 'wq_conv': jax.random.normal(ks[7], (D, K), f) * 0.3, 'wk_conv': jax.random.normal(ks[8], (D, K), f) * 0.3, 'wv_conv': jax.random.normal(ks[9], (D, K), f) * 0.3, 'onorm_w': jnp.ones((D // H,), f), 'Wo': jax.random.normal(ks[10], (D, D), f) * s}
    _L0_attn_in = _L0_attn_setup()

    def _L0_ffn_setup():
        import jax, jax.numpy as jnp
        import numpy as np
        EPS = 1e-05
        NUM_HEADS = 16
        NUM_KV_HEADS = 4
        NUM_EXPERTS = 8
        TOP_K = 2

        def _layernorm(x, w, b):
            mu = jnp.mean(x, axis=-1, keepdims=True)
            var = jnp.mean((x - mu) ** 2, axis=-1, keepdims=True)
            return (x - mu) * jax.lax.rsqrt(var + EPS) * w + b
        key = jax.random.key(seed)
        ks = jax.random.split(key, 8)
        S, B, H = (256, 4, 256)
        F = 512
        hd = H // NUM_HEADS
        qkv_out = (NUM_HEADS + 2 * NUM_KV_HEADS) * hd
        w_scale = 0.02
        return {'hidden_states': jax.random.normal(ks[0], (S, B, H), jnp.float32), 'ln1_weight': jnp.ones((H,), jnp.float32), 'ln1_bias': jnp.zeros((H,), jnp.float32), 'ln2_weight': jnp.ones((H,), jnp.float32), 'ln2_bias': jnp.zeros((H,), jnp.float32), 'qkv_weight': jax.random.normal(ks[1], (qkv_out, H), jnp.float32) * w_scale, 'proj_weight': jax.random.normal(ks[2], (H, H), jnp.float32) * w_scale, 'router_weight': jax.random.normal(ks[3], (NUM_EXPERTS, H), jnp.float32) * w_scale, 'moe_w1': jax.random.normal(ks[4], (NUM_EXPERTS, H, F), jnp.float32) * w_scale, 'moe_w2': jax.random.normal(ks[5], (NUM_EXPERTS, F, H), jnp.float32) * w_scale}
    _L0_ffn_in = _L0_ffn_setup()
    _L0_c = _w((lambda *s: np.random.randn(*s).astype(np.float32) * 0.05)(8, 256))
    _L0_wmod = _w((lambda *s: np.random.randn(*s).astype(np.float32) * 0.05)(256, 6 * 256) * 256 ** (-0.5))
    _d = {'L0_attn_hidden_states': _L0_attn_in['hidden_states'], 'L0_attn_Wq': _L0_attn_in['Wq'], 'L0_attn_Wk': _L0_attn_in['Wk'], 'L0_attn_Wv': _L0_attn_in['Wv'], 'L0_attn_Wb': _L0_attn_in['Wb'], 'L0_attn_Wdec': _L0_attn_in['Wdec'], 'L0_attn_Wmix': _L0_attn_in['Wmix'], 'L0_attn_mix_bias': _L0_attn_in['mix_bias'], 'L0_attn_wq_conv': _L0_attn_in['wq_conv'], 'L0_attn_wk_conv': _L0_attn_in['wk_conv'], 'L0_attn_wv_conv': _L0_attn_in['wv_conv'], 'L0_attn_onorm_w': _L0_attn_in['onorm_w'], 'L0_attn_Wo': _L0_attn_in['Wo'], 'L0_ffn_ln1_weight': _L0_ffn_in['ln1_weight'], 'L0_ffn_ln1_bias': _L0_ffn_in['ln1_bias'], 'L0_ffn_ln2_weight': _L0_ffn_in['ln2_weight'], 'L0_ffn_ln2_bias': _L0_ffn_in['ln2_bias'], 'L0_ffn_qkv_weight': _L0_ffn_in['qkv_weight'], 'L0_ffn_proj_weight': _L0_ffn_in['proj_weight'], 'L0_ffn_router_weight': _L0_ffn_in['router_weight'], 'L0_ffn_moe_w1': _L0_ffn_in['moe_w1'], 'L0_ffn_moe_w2': _L0_ffn_in['moe_w2'], 'L0_c': _L0_c, 'L0_wmod': _L0_wmod}
    _x0 = _d['L0_attn_hidden_states']
    _d['L0_attn_hidden_states'] = jax.random.normal(jax.random.fold_in(jax.random.key(seed), 1), (8, 1024, 256), dtype=_x0.dtype)
    del _x0
    return _d

def reference(L0_attn_hidden_states, L0_attn_Wq, L0_attn_Wk, L0_attn_Wv, L0_attn_Wb, L0_attn_Wdec, L0_attn_Wmix, L0_attn_mix_bias, L0_attn_wq_conv, L0_attn_wk_conv, L0_attn_wv_conv, L0_attn_onorm_w, L0_attn_Wo, L0_ffn_ln1_weight, L0_ffn_ln1_bias, L0_ffn_ln2_weight, L0_ffn_ln2_bias, L0_ffn_qkv_weight, L0_ffn_proj_weight, L0_ffn_router_weight, L0_ffn_moe_w1, L0_ffn_moe_w2, L0_c, L0_wmod):

    def _L0_attn_ref(hidden_states, Wq, Wk, Wv, Wb, Wdec, Wmix, mix_bias, wq_conv, wk_conv, wv_conv, onorm_w, Wo):
        import jax, jax.numpy as jnp
        import numpy as np
        CHUNK = 32
        EPS_L2 = 1e-06
        EPS_RMS = 1e-05
        NUM_HEADS = 4

        def _causal_dwconv_silu(x, w):
            k = w.shape[1]
            l = x.shape[1]
            xp = jnp.pad(x, ((0, 0), (k - 1, 0), (0, 0)))
            out = sum((w[:, j] * xp[:, j:j + l, :] for j in range(k)))
            return jax.nn.silu(out)

        def _l2norm(x):
            return x * jax.lax.rsqrt(jnp.sum(x * x, -1, keepdims=True) + EPS_L2)

        def _delta_rule_chunkwise(q, k, v, beta, c=CHUNK):
            b, h, l, dk = q.shape
            dv = v.shape[-1]
            n = l // c
            q = _l2norm(q)
            k = _l2norm(k)
            v = v * beta[..., None]
            kb = k * beta[..., None]
            qc = q.reshape(b, h, n, c, dk)
            kc = k.reshape(b, h, n, c, dk)
            vc = v.reshape(b, h, n, c, dv)
            kbc = kb.reshape(b, h, n, c, dk)
            strict_lower = jnp.tril(jnp.ones((c, c), bool), -1)
            attn = -jnp.einsum('bhnik,bhnjk->bhnij', kbc, kc)
            attn = jnp.where(strict_lower, attn, 0.0)
            for i in range(1, c):
                upd = jnp.einsum('bhnj,bhnjm->bhnm', attn[..., i, :], attn[..., :, :i])
                attn = attn.at[..., i, :i].add(upd)
            attn = attn + jnp.eye(c, dtype=attn.dtype)
            u = attn @ vc
            w = attn @ kbc
            incl_lower = jnp.tril(jnp.ones((c, c), bool))

            def step(S, inp):
                q_i, k_i, u_i, w_i = inp
                a = jnp.where(incl_lower, jnp.einsum('bhik,bhjk->bhij', q_i, k_i), 0.0)
                u_new = u_i - w_i @ S
                o_i = q_i @ S + a @ u_new
                S = S + jnp.einsum('bhck,bhcv->bhkv', k_i, u_new)
                return (S, o_i)
            S0 = jnp.zeros((b, h, dk, dv), q.dtype)
            xs = tuple((jnp.moveaxis(x, 2, 0) for x in (qc, kc, u, w)))
            S, o = jax.lax.scan(step, S0, xs)
            o = jnp.moveaxis(o, 0, 2).reshape(b, h, l, dv)
            return (o, S)

        def _ema(v, gamma):
            vt = jnp.moveaxis(v, 2, 0)
            gt = jnp.moveaxis(gamma, 2, 0)[..., None]

            def step(s, xg):
                x, g = xg
                s = g * s + (1.0 - g) * x
                return (s, s)
            s0 = jnp.zeros(v.shape[:2] + v.shape[-1:], v.dtype)
            _, out = jax.lax.scan(step, s0, (vt, gt))
            return jnp.moveaxis(out, 0, 2)

        def _forward(hs, Wq, Wk, Wv, Wb, Wdec, Wmix, mix_bias, wq_conv, wk_conv, wv_conv, onorm_w, Wo):
            b, l, d = hs.shape
            h = NUM_HEADS
            q = _causal_dwconv_silu(hs @ Wq.T, wq_conv)
            k = _causal_dwconv_silu(hs @ Wk.T, wk_conv)
            v = _causal_dwconv_silu(hs @ Wv.T, wv_conv)
            dk = q.shape[-1] // h
            dv = v.shape[-1] // h
            q = q.reshape(b, l, h, dk)
            k = k.reshape(b, l, h, dk)
            v = v.reshape(b, l, h, dv)
            beta = jax.nn.sigmoid(hs @ Wb.T)
            qd = jnp.transpose(q, (0, 2, 1, 3))
            kd = jnp.transpose(k, (0, 2, 1, 3))
            vd = jnp.transpose(v, (0, 2, 1, 3))
            bd = jnp.transpose(beta, (0, 2, 1))
            o_d, _S = _delta_rule_chunkwise(qd, kd, vd, bd)
            o_d = jnp.transpose(o_d, (0, 2, 1, 3))
            gamma = jnp.transpose(jax.nn.sigmoid(hs @ Wdec.T), (0, 2, 1))
            ema_out = jnp.transpose(_ema(vd, gamma), (0, 2, 1, 3))
            mix = jax.nn.sigmoid(hs @ Wmix.T + mix_bias)[..., None]
            o = (1.0 - mix) * o_d + mix * ema_out
            o = o * jax.lax.rsqrt(jnp.mean(o * o, -1, keepdims=True) + EPS_RMS) * onorm_w
            return o.reshape(b, l, h * dv) @ Wo.T
        return _forward(hidden_states, Wq, Wk, Wv, Wb, Wdec, Wmix, mix_bias, wq_conv, wk_conv, wv_conv, onorm_w, Wo)

    def _L0_ffn_ref(hidden_states, ln1_weight, ln1_bias, ln2_weight, ln2_bias, qkv_weight, proj_weight, router_weight, moe_w1, moe_w2):
        import jax, jax.numpy as jnp
        import numpy as np
        EPS = 1e-05
        NUM_HEADS = 16
        NUM_KV_HEADS = 4
        NUM_EXPERTS = 8
        TOP_K = 2

        def _layernorm(x, w, b):
            mu = jnp.mean(x, axis=-1, keepdims=True)
            var = jnp.mean((x - mu) ** 2, axis=-1, keepdims=True)
            return (x - mu) * jax.lax.rsqrt(var + EPS) * w + b
        S, B, H = hidden_states.shape
        hd = H // NUM_HEADS
        rep = NUM_HEADS // NUM_KV_HEADS
        scale = 1.0 / hd ** 0.5
        ln1_out = _layernorm(hidden_states, ln1_weight, ln1_bias)
        qkv = jnp.einsum('sbh,oh->sbo', ln1_out, qkv_weight)
        q = qkv[..., :NUM_HEADS * hd].reshape(S, B, NUM_HEADS, hd)
        k = qkv[..., NUM_HEADS * hd:(NUM_HEADS + NUM_KV_HEADS) * hd].reshape(S, B, NUM_KV_HEADS, hd)
        v = qkv[..., (NUM_HEADS + NUM_KV_HEADS) * hd:].reshape(S, B, NUM_KV_HEADS, hd)
        k = jnp.repeat(k, rep, axis=2)
        v = jnp.repeat(v, rep, axis=2)
        scores = jnp.einsum('sbhd,tbhd->bhst', q, k) * scale
        causal = jnp.tril(jnp.ones((S, S), bool))
        scores = jnp.where(causal, scores, jnp.finfo(scores.dtype).min)
        probs = jax.nn.softmax(scores, axis=-1)
        attn = jnp.einsum('bhst,tbhd->sbhd', probs, v).reshape(S, B, H)
        proj_out = jnp.einsum('sbh,oh->sbo', attn, proj_weight)
        hidden_after_attn = hidden_states + proj_out
        ln2_out = _layernorm(hidden_after_attn, ln2_weight, ln2_bias)
        x = ln2_out.reshape(-1, H)
        logits = jnp.einsum('th,eh->te', x, router_weight)
        gate = jax.nn.softmax(logits, axis=-1)
        top_probs, top_idx = jax.lax.top_k(gate, TOP_K)
        h_mid = jax.nn.gelu(jnp.einsum('th,ehf->etf', x, moe_w1))
        expert_out = jnp.einsum('etf,efh->eth', h_mid, moe_w2)
        e_ids = jnp.arange(NUM_EXPERTS)[:, None, None]
        weights = jnp.sum(jnp.where(top_idx[None] == e_ids, top_probs[None], 0.0), axis=-1)
        moe_out = jnp.einsum('eth,et->th', expert_out, weights).reshape(S, B, H)
        return hidden_after_attn + moe_out
    x = L0_attn_hidden_states
    mod = (_silu(L0_c) @ L0_wmod).reshape(L0_c.shape[0], 6, 1, -1)
    sa, ca, ga, sb, cb, gb = (mod[:, 0], mod[:, 1], mod[:, 2], mod[:, 3], mod[:, 4], mod[:, 5])
    ga = (2 * (ga >= 0) - 1) * jnp.maximum(jnp.abs(ga), 0.25)
    gb = (2 * (gb >= 0) - 1) * jnp.maximum(jnp.abs(gb), 0.25)
    h = _layernorm(x, axis=-1) * (1 + ca) + sa
    x = x + ga * _L0_attn_ref(h, L0_attn_Wq, L0_attn_Wk, L0_attn_Wv, L0_attn_Wb, L0_attn_Wdec, L0_attn_Wmix, L0_attn_mix_bias, L0_attn_wq_conv, L0_attn_wk_conv, L0_attn_wv_conv, L0_attn_onorm_w, L0_attn_Wo)
    h = _layernorm(x, axis=-1) * (1 + cb) + sb
    x = x + gb * _L0_ffn_ref(h, L0_ffn_ln1_weight, L0_ffn_ln1_bias, L0_ffn_ln2_weight, L0_ffn_ln2_bias, L0_ffn_qkv_weight, L0_ffn_proj_weight, L0_ffn_router_weight, L0_ffn_moe_w1, L0_ffn_moe_w2)
    return x

_drawn_inputs = setup_inputs


def setup_inputs(seed=0):
    import zlib

    import numpy as np

    out = dict(_drawn_inputs(seed))
    spreads = {'L0_attn_mix_bias': (0.0, 0.8),
     'L0_attn_onorm_w': (1.0, 0.6),
     'L0_ffn_ln1_weight': (1.0, 0.6),
     'L0_ffn_ln1_bias': (0.0, 0.8),
     'L0_ffn_ln2_weight': (1.0, 0.6),
     'L0_ffn_ln2_bias': (0.0, 0.8)}
    factors = {'L0_attn_Wb': 6.254,
     'L0_attn_Wdec': 5.507,
     'L0_attn_Wmix': 4.512,
     'L0_ffn_qkv_weight': 3.54,
     'L0_ffn_proj_weight': 3.443,
     'L0_ffn_router_weight': 8.0,
     'L0_ffn_moe_w1': 8.0,
     'L0_ffn_moe_w2': 8.0}
    for name, (base, spread) in spreads.items():
        noise = np.random.default_rng([zlib.crc32(name.encode()), seed]).standard_normal(out[name].shape)
        drawn = base * np.exp(spread * noise) if base else spread * noise
        out[name] = jnp.asarray(drawn.astype(out[name].dtype))
    for name, factor in factors.items():
        out[name] = (out[name] * factor).astype(out[name].dtype)
    return out
```

```python
from contextlib import ExitStack

import numpy as np
import concourse.bass as bass
from concourse import mybir

ALU = mybir.AluOpType
ACT = mybir.ActivationFunctionType
F32 = mybir.dt.float32
U32 = mybir.dt.uint32
AX_X = mybir.AxisListType.X

P = 128
B, L, D = 8, 1024, 256
KD = D // P
C = 32
STEPS = L // C
G = 2
QB = B // G
NH, DH = 4, 64
PAIRS = NH // 2
TAPS = 4
M = 3 * KD
LEVELS = 5
COLS = B * C
NEXP, FF = 8, 512
FT = FF // P
QH, KVH, HD = 16, 4, 16
REP = QH // KVH
QKV = (QH + 2 * KVH) * HD
PT = L // P
TOK = B * L
MT = 512
FMIN = float(np.finfo(np.float32).min)


def bc(ap, shape):
    return ap.broadcast_to(shape)


ONE = 1


def prime(eng, semaphores, dma_semaphores):
    for x in semaphores:
        eng.sem_inc(x, 1)
    for x in dma_semaphores:
        eng.sem_inc(x, 16)


def setup_constants(nc, ctx, dram, sbuf, psum, mod_b, zeroed):
    d, s = dram, sbuf
    sem = lambda name: ctx.enter_context(nc.semaphore(name))
    loaded, half_set, gates_in = sem("loaded"), sem("half_set"), sem("gates_in")
    sc_ready, mod_in_psum, mod_ready = sem("sc_ready"), sem("mod_in_psum"), sem("mod_ready")
    rows_in_psum, rows_out, wo_scaled = sem("rows_in_psum"), sem("rows_out"), sem("wo_scaled")
    gate_step = sem("gate_step")
    names = ["ident", "quad_mask", "eye32", "levels", "chunk_mask", "w_qkv", "w_beta_mix", "w_decay", "w_out", "conv_w",
             "onorm", "small_bias", "cT", "wmod", "iota8"]

    with nc.Block() as block:
        @block.sync
        def _(sp):
            for name in names:
                sp.dma_start(s[name][:], d[name]).then_inc(loaded, 16)

        @block.scalar
        def _(act):
            act.wait_ge(loaded, 16 * len(names))
            nc.scalar.activation(s["scT"][:], s["cT"][:], ACT.Silu).then_inc(sc_ready, 1)
            act.wait_ge(mod_in_psum, 1)
            nc.scalar.copy(s["mod"][:], psum[0:B, 0:3, :]).then_inc(mod_ready, 1)
            n = 0
            for dst in mod_b:
                act.wait_ge(rows_in_psum, n + 1)
                nc.scalar.copy(dst, psum[:, 4 + n % 4, 0:D]).then_inc(rows_out, 1)
                n += 1

        @block.tensor
        def _(pe):
            pe.wait_ge(sc_ready, 1)
            for c in range(3):
                for k in range(KD):
                    last = nc.tensor.matmul(psum[0:B, c, :], s["scT"][:, k, :],
                                            s["wmod"][:, k, c * 512:(c + 1) * 512], start=(k == 0), stop=(k == KD - 1))
            last.then_inc(mod_in_psum, 1)
            pe.wait_ge(gates_in, 1)
            n = 0
            for which in (1, 0, 2):
                for g in range(G):
                    if n >= 4:
                        pe.wait_ge(rows_out, n - 3)
                    nc.tensor.matmul(psum[:, 4 + n % 4, 0:D], s["sel_quad"][:, g, :],
                                     s["mod"][:, which * D:(which + 1) * D], start=True, stop=True).then_inc(rows_in_psum, 1)
                    n += 1
            for which in (4, 3, 5):
                for b in range(B):
                    pe.wait_ge(rows_out, n - 3)
                    nc.tensor.matmul(psum[:, 4 + n % 4, 0:D], s["sel_all"][:, b, :],
                                     s["mod"][:, which * D:(which + 1) * D], start=True, stop=True).then_inc(rows_in_psum, 1)
                    n += 1

        @block.vector
        def _(dve):
            steps = [0]

            def link(ins):
                steps[0] += 1
                ins.then_inc(gate_step, 1)
                dve.wait_ge(gate_step, steps[0])

            dve.wait_ge(loaded, 16 * len(names))
            for k in range(KD):
                nc.vector.tensor_scalar(s["w_out"][:, k, :], s["w_out"][:, k, :], s["onorm"][:, 0:1], None, ALU.mult)
            for g in range(G):
                nc.vector.tensor_copy(s["sel_quad"][:, g, :].rearrange("b (i t) -> b i t", t=C),
                                      bc(s["ident"][0:B, g * QB:(g + 1) * QB].unsqueeze(2), [B, QB, C]))
            nc.vector.tensor_copy(s["sel_all"][:], bc(s["ident"][0:B, 0:B].unsqueeze(2), [B, B, P]))
            dve.wait_ge(mod_ready, 1)
            mod = s["mod"]
            for which in (2, 5):
                gate = mod[:, which * D:(which + 1) * D]
                link(nc.vector.tensor_scalar(s["gate_sign"][:], gate, 0.0, 2.0, ALU.is_ge, ALU.mult))
                link(nc.vector.tensor_scalar(s["gate_sign"][:], s["gate_sign"][:], -1.0, None, ALU.add))
                link(nc.vector.tensor_tensor(gate, gate, s["gate_sign"][:], ALU.mult))
                link(nc.vector.scalar_tensor_tensor(gate, gate, 0.25, s["gate_sign"][:], ALU.max, ALU.mult))
            for which in (1, 4):
                row = mod[:, which * D:(which + 1) * D]
                last = nc.vector.tensor_scalar(row, row, 1.0, None, ALU.add)
            last.then_inc(gates_in, 1)

        @block.gpsimd
        def _(pool):
            nc.gpsimd.memset(s["minus_half"][:], -0.5)
            for name in ("state", "conv_in", "ema_out", "TTbd"):
                nc.gpsimd.memset(s[name][:], 0.0)
            nc.gpsimd.memset(s["conv_acc"][:], 0.0).then_inc(zeroed, 1)
            pool.wait_ge(zeroed, 1)


def pass_one(nc, ctx, x, x1, s, ps, zeroed):
    sem = lambda name: ctx.enter_context(nc.semaphore(name))
    x_in, xres_in, x1_out = sem("x_in"), sem("xres_in"), sem("x1_out")
    stats, rstd, rstd_a = sem("ln_stats"), sem("ln_rstd"), sem("ln_var_eps")
    normed, scaled, h_ready = sem("ln_normed"), sem("ln_scaled"), sem("h_ready")
    hT_ps, hT_ok = sem("hT_in_psum"), sem("hT_ready")
    proj_ps, decay_ps, small_ps = sem("proj_in_psum"), sem("decay_in_psum"), sem("small_in_psum")
    conv_in_ok, conv_tap, carried = sem("conv_in_ready"), sem("conv_tap"), sem("conv_carried")
    th_decay, small_sum, th_small, gates = sem("tanh_decay"), sem("small_sum"), sem("tanh_small"), sem("gates_ready")
    qkvT_ok, ema_step, ema_ok = sem("qkvT_ready"), sem("ema_step"), sem("ema_ready")
    qk_ps, v_ps, sq_ok, ssq_ok, r_a, r_ok = (sem("qk_rows_in_psum"), sem("v_rows_in_psum"), sem("squares"),
                                             sem("square_sums"), sem("norm_eps"), sem("norm_scale"))
    v_rows, ema_rows, qkn_ok, kb_ok = sem("v_rows"), sem("ema_rows"), sem("qk_normed"), sem("kb_ready")
    knT_ps, kqT_ps, knT_ok, kqT_ok = sem("knT_in_psum"), sem("kqT_in_psum"), sem("knT_ready"), sem("kqT_ready")
    kbd_ok, gram_ps, gram_ok = sem("k_blocks_ready"), sem("gram_in_psum"), sem("gram_masked")
    y_ps, y_ok, z_ps, t_ok, tt_ok = sem("LT_in_psum"), sem("LT_masked"), sem("TLT_in_psum"), sem("T_ready"), sem("Tt_ready")
    uw_ps, uw_ok, ws_ps, o_ps, un_ok = sem("uw_in_psum"), sem("uw_ready"), sem("wS_in_psum"), sem("o_in_psum"), sem("u_new")
    ds_ps, s_ok = sem("dS_in_psum"), sem("state_ready")
    mix_a, mix_b, o_ok, osq_ok, oss_ok, or_a, or_ok = (sem("mix_delta"), sem("mix_ema"), sem("o_ready"), sem("o_squares"),
                                                       sem("o_square_sums"), sem("o_norm_eps"), sem("o_norm_scale"))
    on_ok, onT_ps, onT_ok, wo_ps, gated, x1_ok = (sem("o_normed"), sem("onT_in_psum"), sem("onT_ready"),
                                                  sem("out_in_psum"), sem("gated"), sem("x1_ready"))

    def chunk_rows(a, n, g):
        return a[g * QB:(g + 1) * QB, bass.ds(n * C, C), :]

    v, gp, ac, te = nc.vector, nc.gpsimd, nc.scalar, nc.tensor
    heads = lambda ap: ap.rearrange("p (h d) -> p h d", d=DH)
    both = lambda ap: ap.rearrange("p a b -> p (a b)")

    with nc.Block() as block:
        @block.sync
        def _(sp):
            prime(sp, (normed, x1_ok, ds_ps, carried, s_ok), (x1_out,))
            with sp.Fori(0, STEPS) as n:
                sp.wait_ge(normed, ONE + n * G)
                for g in range(G):
                    for i in range(QB):
                        sp.dma_start(s["x_in"][i * C:(i + 1) * C, g, :],
                                     x[g * QB + i, bass.ds(n * C, C), :]).then_inc(x_in, 16)
                sp.wait_ge(x1_ok, ONE + n * G)
                for g in range(G):
                    for i in range(QB):
                        sp.dma_start(s["x_res"][i * C:(i + 1) * C, g, :],
                                     x[g * QB + i, bass.ds(n * C, C), :]).then_inc(xres_in, 16)
                for g in range(G):
                    sp.wait_ge(x1_ok, ONE + n * G + g + 1)
                    for i in range(QB):
                        sp.dma_start(x1[g * QB + i, bass.ds(n * C, C), :],
                                     s["x1_rows"][i * C:(i + 1) * C, g, :]).then_inc(x1_out, 16)
            sp.wait_ge(x1_out, 16 + 16 * B * STEPS)

        @block.gpsimd
        def _(pool):
            mh = s["minus_half"]
            with pool.Fori(0, STEPS) as n:
                pool.wait_ge(stats, n + 1)
                gp.tensor_tensor(s["ln_r"][:], s["ln_v"][:], mh[:, 0:G], ALU.pow).then_inc(rstd, 1)
                pool.wait_ge(scaled, n + 1)
                gp.tensor_tensor(s["h"][:], s["h"][:], s["shift1"][:], ALU.add).then_inc(h_ready, 1)
                for g in range(G):
                    pool.wait_ge(r_a, n * G + g + 1)
                    gp.tensor_tensor(s["rqk"][:, g, :], s["ss"][:, g, :], mh[:, 0:2 * NH], ALU.pow).then_inc(r_ok, 1)
                for g in range(G):
                    pool.wait_ge(qkn_ok, n * G + g + 1)
                    pool.wait_ge(ds_ps, ONE + n * G)
                    gp.tensor_tensor(s["k_bd"][:, g], bc(s["qkn"][:, g, 1, :].unsqueeze(1), [P, QB, D]),
                                     bc(s["quad_mask"][:].unsqueeze(2), [P, QB, D]), ALU.mult).then_inc(kbd_ok, 1)
                for g in range(G):
                    pool.wait_ge(ema_rows, n * G + g + 1)
                    pool.wait_ge(gates, n + 1)
                    gp.tensor_tensor(heads(s["mix_e"][:, g, :]), heads(s["ema_rows"][:, g, :]),
                                     bc(s["bm"][:, g, NH:2 * NH].unsqueeze(2), [P, NH, DH]), ALU.mult).then_inc(mix_b, 1)
                for g in range(G):
                    pool.wait_ge(or_a, n * G + g + 1)
                    gp.tensor_tensor(s["orr"][:, g, :], s["oss"][:, g, :], mh[:, 0:NH], ALU.pow).then_inc(or_ok, 1)
                for g in range(G):
                    pool.wait_ge(gated, n * G + g + 1)
                    pool.wait_ge(xres_in, (n + 1) * 16 * B)
                    pool.wait_ge(x1_out, 16 + n * 16 * B)
                    gp.tensor_tensor(s["x1_rows"][:, g, :], s["y"][:, g, :], s["x_res"][:, g, :], ALU.add).then_inc(x1_ok, 1)

        @block.scalar
        def _(act):
            with act.Fori(0, STEPS) as n:
                act.wait_ge(hT_ps, n + 1)
                ac.copy(both(s["hT"][:]), ps[:, 3, :]).then_inc(hT_ok, 1)
                act.wait_ge(proj_ps, n + 1)
                act.wait_ge(carried, ONE + n)
                for c in range(3):
                    last = ac.copy(s["conv_in"][:, 2 * c:2 * c + 2, :, TAPS - 1:],
                                   ps[:, c, :].rearrange("p (m b t) -> p m b t", m=2, t=C))
                last.then_inc(conv_in_ok, 1)
                act.wait_ge(decay_ps, n + 1)
                ac.activation(s["th_decay"][:], ps[:, 4, :], ACT.Tanh, scale=0.5).then_inc(th_decay, 1)
                act.wait_ge(small_sum, n + 1)
                ac.activation(s["th_small"][:], s["small"][:], ACT.Tanh, scale=0.5).then_inc(th_small, 1)
                act.wait_ge(conv_tap, (n + 1) * TAPS)
                ac.activation(s["qkvT"][:], s["conv_acc"][:], ACT.Silu).then_inc(qkvT_ok, 1)
                ac.copy(s["conv_in"][:, :, :, 0:TAPS - 1].rearrange("p m b t -> p (m b) t"),
                        s["conv_in"][:, :, :, C:C + TAPS - 1].rearrange("p m b t -> p (m b) t")).then_inc(carried, 1)
                for g in range(G):
                    act.wait_ge(qk_ps, n * G + g + 1)
                    ac.activation(s["sq"][:, g, :], ps[:, 4 * g, :], ACT.Square).then_inc(sq_ok, 1)
                    act.wait_ge(v_ps, n * G + g + 1)
                    ac.copy(s["ema_rows"][:, g, :], ps[:, 4 * g + 1, D:2 * D]).then_inc(ema_rows, 1)
                for g in range(G):
                    act.wait_ge(knT_ps, n * G + g + 1)
                    ac.copy(both(s["knT"][:, g]), ps[:, 4 * g + 2, 0:D]).then_inc(knT_ok, 1)
                    act.wait_ge(kqT_ps, n * G + g + 1)
                    ac.copy(s["kqT"][:, g].rearrange("p a b c -> p (a b c)"), ps[:, 4 * g + 3, :]).then_inc(kqT_ok, 1)
                for g in range(G):
                    act.wait_ge(uw_ps, n * G + g + 1)
                    ac.copy(s["u"][:, g, :], ps[:, 4 * g, 0:D])
                    ac.copy(both(s["wT"][:, g]), ps[:, 4 * g + 1, 0:D]).then_inc(uw_ok, 1)
                for g in range(G):
                    act.wait_ge(o_ok, n * G + g + 1)
                    ac.activation(s["osq"][:, g, :], s["o"][:, g, :], ACT.Square).then_inc(osq_ok, 1)
                for g in range(G):
                    act.wait_ge(onT_ps, n * G + g + 1)
                    ac.copy(both(s["onT"][:, g]), ps[:, 4 * g + 2, 0:D]).then_inc(onT_ok, 1)

        @block.tensor
        def _(pe):
            ident = s["ident"]
            with pe.Fori(0, STEPS) as n:
                pe.wait_ge(h_ready, n + 1)
                pe.wait_ge(x1_ok, ONE + n * G)
                for k in range(KD):
                    for g in range(G):
                        last = te.transpose(ps[:, 3, (k * G + g) * P:(k * G + g + 1) * P], s["h"][:, g, k * P:(k + 1) * P], ident[:])
                last.then_inc(hT_ps, 1)
                pe.wait_ge(hT_ok, n + 1)
                for m in range(M):
                    for k in range(KD):
                        last = te.matmul(ps[:, m // 2, (m % 2) * COLS:(m % 2 + 1) * COLS], s["w_qkv"][:, k, m * P:(m + 1) * P],
                                         s["hT"][:, k, :], start=(k == 0), stop=(k == KD - 1))
                last.then_inc(proj_ps, 1)
                for pair in range(PAIRS):
                    for k in range(KD):
                        last = te.matmul(ps[:, 4, pair * COLS:(pair + 1) * COLS], s["w_decay"][:, k, pair * P:(pair + 1) * P],
                                         s["hT"][:, k, :], start=(k == 0), stop=(k == KD - 1))
                last.then_inc(decay_ps, 1)
                for g in range(G):
                    for k in range(KD):
                        last = te.matmul(ps[:, 5, g * 2 * NH:(g + 1) * 2 * NH], s["hT"][:, k, g * P:(g + 1) * P],
                                         s["w_beta_mix"][:, k, :], start=(k == 0), stop=(k == KD - 1))
                last.then_inc(small_ps, 1)
                pe.wait_ge(qkvT_ok, n + 1)
                pe.wait_ge(th_decay, n + 1)
                for g in range(G):
                    if g == 1:
                        pe.wait_ge(small_sum, n + 1)
                    for m in range(4):
                        last = te.transpose(ps[:, 4 * g, m * P:(m + 1) * P], s["qkvT"][:, m, g * P:(g + 1) * P], ident[:])
                    last.then_inc(qk_ps, 1)
                pe.wait_ge(ema_ok, n + 1)
                for g in range(G):
                    for m in range(2):
                        te.transpose(ps[:, 4 * g + 1, m * P:(m + 1) * P], s["qkvT"][:, 4 + m, g * P:(g + 1) * P], ident[:])
                    for m in range(2):
                        last = te.transpose(ps[:, 4 * g + 1, (2 + m) * P:(3 + m) * P], s["ema_out"][:, m, g * P:(g + 1) * P], ident[:])
                    last.then_inc(v_ps, 1)
                for g in range(G):
                    pe.wait_ge(qkn_ok, n * G + g + 1)
                    for m in range(PAIRS):
                        last = te.transpose(ps[:, 4 * g + 2, m * P:(m + 1) * P], s["qkn"][:, g, 1, m * P:(m + 1) * P], ident[:])
                    last.then_inc(knT_ps, 1)
                    pe.wait_ge(kb_ok, n * G + g + 1)
                    for m in range(PAIRS):
                        te.transpose(ps[:, 4 * g + 3, 2 * m * P:(2 * m + 1) * P], s["kb"][:, g, m * P:(m + 1) * P], ident[:])
                        last = te.transpose(ps[:, 4 * g + 3, (2 * m + 1) * P:(2 * m + 2) * P], s["qkn"][:, g, 0, m * P:(m + 1) * P], ident[:])
                    last.then_inc(kqT_ps, 1)
                for g in range(G):
                    pe.wait_ge(knT_ok, n * G + g + 1)
                    pe.wait_ge(kqT_ok, n * G + g + 1)
                    pe.wait_ge(ema_rows, n * G + g + 1)
                    for par in range(2):
                        half = slice(par * DH, (par + 1) * DH)
                        for m in range(PAIRS):
                            last = te.matmul(ps[:, 4 * g + par, m * 2 * P:(m + 1) * 2 * P], s["knT"][half, g, m, :],
                                             both(s["kqT"][half, g, m]), start=True, stop=True)
                    last.then_inc(gram_ps, 1)
                for lev in range(LEVELS):
                    for g in range(G):
                        if lev == 0:
                            pe.wait_ge(gram_ok, n * G + g + 1)
                        else:
                            pe.wait_ge(t_ok, n * G * LEVELS + lev * G + g + 1 - G)
                        for h in range(NH):
                            rhs = s["eye32"][:] if lev == 0 else s["T"][:, g, h, :]
                            last = te.matmul(ps[:, 4 * g + 2, h * C:(h + 1) * C], s["LA"][:, g, h, 0, :], rhs, start=True, stop=True)
                        last.then_inc(y_ps, 1)
                    if lev == 0:
                        continue
                    for g in range(G):
                        pe.wait_ge(y_ok, n * G * LEVELS + lev * G + g + 1)
                        pe.wait_ge(tt_ok, n * G * LEVELS + lev * G + g + 1 - G)
                        for h in range(NH):
                            last = te.matmul(ps[:, 4 * g + 3, h * C:(h + 1) * C], s["TTbd"][:, g, h, :], s["Y"][:, g, h, :], start=True, stop=True)
                        last.then_inc(z_ps, 1)
                for g in range(G):
                    pe.wait_ge(tt_ok, (n * LEVELS + LEVELS - 1) * G + g + 1)
                    for h in range(NH):
                        te.matmul(ps[:, 4 * g, h * DH:(h + 1) * DH], s["TTbd"][:, g, h, :], s["vb"][:, g, h * DH:(h + 1) * DH], start=True, stop=True)
                    for h in range(NH):
                        last = te.matmul(ps[(h % 2) * DH:(h % 2 + 1) * DH, 4 * g + 1, (h // 2) * P:(h // 2 + 1) * P],
                                         s["kb"][:, g, h * DH:(h + 1) * DH], s["TTbd"][:, g, h, :], start=True, stop=True)
                    last.then_inc(uw_ps, 1)
                for g in range(G):
                    pe.wait_ge(uw_ok, n * G + g + 1)
                    pe.wait_ge(s_ok, ONE + n * G)
                    for pair in range(PAIRS):
                        for i in range(QB):
                            last = te.matmul(ps[i * C:(i + 1) * C, 4 * g + 2, pair * P:(pair + 1) * P], s["wT"][:, g, pair, i * C:(i + 1) * C],
                                             s["state"][:, g * QB + i, pair, :], start=True, stop=True)
                    last.then_inc(ws_ps, 1)
                    for pair in range(PAIRS):
                        for i in range(QB):
                            te.matmul(ps[i * C:(i + 1) * C, 4 * g + 3, pair * P:(pair + 1) * P], s["kqT"][:, g, pair, 1, i * C:(i + 1) * C],
                                      s["state"][:, g * QB + i, pair, :], start=(pair == 0), stop=False, skip_group_check=True)
                for g in range(G):
                    pe.wait_ge(un_ok, n * G + g + 1)
                    for h in range(NH):
                        last = te.matmul(ps[:, 4 * g + 3, h * DH:(h + 1) * DH], s["LA"][:, g, h, 1, :], s["un"][:, g, h * DH:(h + 1) * DH],
                                         start=False, stop=True, skip_group_check=True)
                    last.then_inc(o_ps, 1)
                    pe.wait_ge(kbd_ok, n * G + g + 1)
                    for pair in range(PAIRS):
                        for i in range(QB):
                            last = te.matmul(ps[:, 4 * g + pair, i * P:(i + 1) * P], s["k_bd"][:, g, i, pair * P:(pair + 1) * P],
                                             s["un"][:, g, pair * P:(pair + 1) * P], start=True, stop=True)
                    last.then_inc(ds_ps, 1)
                for g in range(G):
                    pe.wait_ge(on_ok, n * G + g + 1)
                    for m in range(KD):
                        last = te.transpose(ps[:, 4 * g + 2, m * P:(m + 1) * P], s["on"][:, g, m * P:(m + 1) * P], ident[:])
                    last.then_inc(onT_ps, 1)
                for g in range(G):
                    pe.wait_ge(onT_ok, n * G + g + 1)
                    for k in range(KD):
                        last = te.matmul(ps[:, 4 * g + 3, 0:D], s["onT"][:, g, k, :], s["w_out"][:, k, :], start=(k == 0), stop=(k == KD - 1))
                    last.then_inc(wo_ps, 1)

        @block.vector
        def _(dve):
            with dve.Fori(0, STEPS) as n:
                dve.wait_ge(x_in, (n + 1) * 16 * B)
                for g in range(G):
                    last = v.bn_stats(s["ln_st"][:, g, :], s["x_in"][:, g, :])
                last.then_inc(ema_step, 1)
                dve.wait_ge(ema_step, n * 4 + 1)
                v.tensor_copy(s["pad"][:], s["ln_st"][:, 0, 0:1])
                for g in range(G):
                    last = v.bn_aggr(s["ln_mv"][:, g, :], s["ln_st"][:, g, :])
                last.then_inc(rstd_a, 1)
                dve.wait_ge(rstd_a, n + 1)
                v.tensor_scalar(s["ln_v"][:], s["ln_mv"][:, :, 1], 1e-5, None, ALU.add).then_inc(stats, 1)
                dve.wait_ge(rstd, n + 1)
                for g in range(G):
                    v.tensor_scalar(s["h"][:, g, :], s["x_in"][:, g, :], s["ln_mv"][:, g, 0:1], s["ln_r"][:, g:g + 1],
                                    ALU.subtract, ALU.mult).then_inc(normed, 1)
                dve.wait_ge(normed, ONE + (n + 1) * G)
                v.tensor_tensor(s["h"][:], s["h"][:], s["scale1"][:], ALU.mult).then_inc(scaled, 1)
                dve.wait_ge(small_ps, n + 1)
                v.tensor_tensor(s["small"][:], ps[:, 5, 0:G * 2 * NH].rearrange("p (g e) -> p g e", g=G),
                                bc(s["small_bias"][:].unsqueeze(1), [P, G, 2 * NH]), ALU.add).then_inc(small_sum, 1)
                dve.wait_ge(conv_in_ok, n + 1)
                for j in range(TAPS):
                    if j:
                        dve.wait_ge(conv_tap, n * TAPS + j)
                    for m in range(M):
                        xin = s["conv_in"][:, m, :, j:j + C]
                        acc = s["conv_acc"][:, m, :].rearrange("p (b t) -> p b t", t=C)
                        if j == 0:
                            last = v.tensor_scalar(acc, xin, s["conv_w"][:, m, 0:1], None, ALU.mult)
                        else:
                            last = v.scalar_tensor_tensor(acc, xin, s["conv_w"][:, m, j:j + 1], acc, ALU.mult, ALU.add)
                    last.then_inc(conv_tap, 1)
                dve.wait_ge(th_small, n + 1)
                v.tensor_scalar(s["bm"][:], s["th_small"][:], 0.5, 0.5, ALU.mult, ALU.add)
                v.tensor_scalar(s["omm"][:], s["th_small"][:, :, NH:], -0.5, 0.5, ALU.mult, ALU.add).then_inc(gates, 1)
                dve.wait_ge(th_decay, n + 1)
                v.tensor_scalar(s["gam"][:], s["th_decay"][:], 0.5, 0.5, ALU.mult, ALU.add)
                v.tensor_scalar(s["omg"][:], s["th_decay"][:], -0.5, 0.5, ALU.mult, ALU.add).then_inc(ema_step, 1)
                dve.wait_ge(ema_step, n * 4 + 2)
                dve.wait_ge(qkvT_ok, n + 1)
                first = lambda t: t.rearrange("p (q t) -> p q t", t=C)
                v.tensor_tensor(s["omg"][:], s["omg"][:], both(s["qkvT"][:, 4:6, :]), ALU.mult)
                v.tensor_tensor(s["ema_hist"][:], first(s["gam"][:])[:, :, 0], first(both(s["ema_out"][:]))[:, :, C - 1],
                                ALU.mult).then_inc(ema_step, 1)
                dve.wait_ge(ema_step, n * 4 + 3)
                v.tensor_tensor(first(s["omg"][:])[:, :, 0], first(s["omg"][:])[:, :, 0], s["ema_hist"][:], ALU.add)
                v.memset(first(s["gam"][:])[:, :, 0], 0.0).then_inc(ema_step, 1)
                dve.wait_ge(ema_step, n * 4 + 4)
                v.tensor_tensor_scan(both(s["ema_out"][:]), s["gam"][:], s["omg"][:], 0.0, ALU.mult, ALU.add).then_inc(ema_ok, 1)
                for g in range(G):
                    dve.wait_ge(sq_ok, n * G + g + 1)
                    v.tensor_reduce(s["ss"][:, g, :], heads(s["sq"][:, g, :]), AX_X, ALU.add).then_inc(ssq_ok, 1)
                    dve.wait_ge(ssq_ok, n * G + g + 1)
                    v.tensor_scalar(s["ss"][:, g, :], s["ss"][:, g, :], 1e-6, None, ALU.add).then_inc(r_a, 1)
                dve.wait_ge(gates, n + 1)
                for g in range(G):
                    beta = bc(s["bm"][:, g, 0:NH].unsqueeze(2), [P, NH, DH])
                    dve.wait_ge(r_ok, n * G + g + 1)
                    v.tensor_tensor(heads(both(s["qkn"][:, g])), heads(ps[:, 4 * g, :]),
                                    bc(s["rqk"][:, g, :].unsqueeze(2), [P, 2 * NH, DH]), ALU.mult).then_inc(qkn_ok, 1)
                    dve.wait_ge(ema_rows, n * G + g + 1)
                    v.tensor_tensor(heads(s["vb"][:, g, :]), heads(ps[:, 4 * g + 1, 0:D]), beta, ALU.mult)
                    dve.wait_ge(qkn_ok, n * G + g + 1)
                    v.tensor_tensor(heads(s["kb"][:, g, :]), heads(s["qkn"][:, g, 1, :]), beta, ALU.mult).then_inc(kb_ok, 1)
                for g in range(G):
                    dve.wait_ge(gram_ps, n * G + g + 1)
                    mask = bc(both(s["chunk_mask"][:]).unsqueeze(1), [P, PAIRS, 2 * P])
                    for par in range(2):
                        dst = s["LA"][:, g, par::2].rearrange("p m a b -> p m (a b)")
                        last = v.tensor_tensor(dst, ps[:, 4 * g + par, :].rearrange("p (m c) -> p m c", m=PAIRS), mask, ALU.mult)
                    last.then_inc(gram_ok, 1)
                for lev in range(LEVELS):
                    for g in range(G):
                        dve.wait_ge(y_ps, (n * LEVELS + lev) * G + g + 1)
                        v.tensor_tensor(s["Y"][:, g], ps[:, 4 * g + 2, 0:P].rearrange("p (h c) -> p h c", h=NH),
                                        bc(s["levels"][:, lev, :].unsqueeze(1), [P, NH, C]), ALU.mult).then_inc(y_ok, 1)
                    for g in range(G):
                        dve.wait_ge(y_ok, (n * LEVELS + lev) * G + g + 1)
                        if lev == 0:
                            v.tensor_tensor(s["T"][:, g], bc(s["eye32"][:].unsqueeze(1), [P, NH, C]), s["Y"][:, g],
                                            ALU.subtract).then_inc(t_ok, 1)
                        else:
                            dve.wait_ge(z_ps, n * (LEVELS - 1) * G + (lev - 1) * G + g + 1)
                            v.tensor_tensor(s["T"][:, g], s["T"][:, g], ps[:, 4 * g + 3, 0:P].rearrange("p (h c) -> p h c", h=NH),
                                            ALU.subtract).then_inc(t_ok, 1)
                    for g in range(G):
                        dve.wait_ge(t_ok, (n * LEVELS + lev) * G + g + 1)
                        for i in range(QB):
                            q = slice(i * C, (i + 1) * C)
                            last = v.transpose(s["TTbd"][q, g, :, q], s["T"][q, g])
                        last.then_inc(tt_ok, 1)
                for g in range(G):
                    dve.wait_ge(ws_ps, n * G + g + 1)
                    v.tensor_tensor(s["un"][:, g, :], s["u"][:, g, :], ps[:, 4 * g + 2, 0:D], ALU.subtract).then_inc(un_ok, 1)
                for g in range(G):
                    dve.wait_ge(o_ps, n * G + g + 1)
                    v.tensor_tensor(heads(s["mix_d"][:, g, :]), heads(ps[:, 4 * g + 3, 0:D]),
                                    bc(s["omm"][:, g, :].unsqueeze(2), [P, NH, DH]), ALU.mult).then_inc(mix_a, 1)
                    dve.wait_ge(mix_a, n * G + g + 1)
                    dve.wait_ge(mix_b, n * G + g + 1)
                    v.tensor_tensor(s["o"][:, g, :], s["mix_d"][:, g, :], s["mix_e"][:, g, :], ALU.add).then_inc(o_ok, 1)
                    dve.wait_ge(ds_ps, ONE + n * G + g + 1)
                    for pair in range(PAIRS):
                        for par in range(2):
                            half = slice(par * DH, (par + 1) * DH)
                            st = s["state"][half, g * QB:(g + 1) * QB, pair, half]
                            last = v.tensor_tensor(st, st, ps[half, 4 * g + pair, :].rearrange("p (i c) -> p i c", i=QB)[:, :, half], ALU.add)
                    last.then_inc(s_ok, 1)
                for g in range(G):
                    dve.wait_ge(osq_ok, n * G + g + 1)
                    v.tensor_reduce(s["oss"][:, g, :], heads(s["osq"][:, g, :]), AX_X, ALU.add).then_inc(oss_ok, 1)
                    dve.wait_ge(oss_ok, n * G + g + 1)
                    v.tensor_scalar(s["oss"][:, g, :], s["oss"][:, g, :], 1.0 / DH, 1e-5, ALU.mult, ALU.add).then_inc(or_a, 1)
                for g in range(G):
                    dve.wait_ge(or_ok, n * G + g + 1)
                    v.tensor_tensor(heads(s["on"][:, g, :]), heads(s["o"][:, g, :]), bc(s["orr"][:, g, :].unsqueeze(2), [P, NH, DH]),
                                    ALU.mult).then_inc(on_ok, 1)
                for g in range(G):
                    dve.wait_ge(wo_ps, n * G + g + 1)
                    v.tensor_tensor(s["y"][:, g, :], ps[:, 4 * g + 3, 0:D], s["gate1"][:, g, :], ALU.mult).then_inc(gated, 1)


def setup_two(nc, ctx, d, s):
    sem = lambda name: ctx.enter_context(nc.semaphore(name))
    loaded, masked = sem("b_loaded"), sem("b_masked")
    names = ["w_qkv2", "w_proj", "w_router", "ln_wb"]
    with nc.Block() as block:
        @block.sync
        def _(sp):
            for name in names:
                sp.dma_start(s[name][:], d[name]).then_inc(loaded, 16)
            sp.wait_ge(loaded, 16 * len(names))

        @block.gpsimd
        def _(pool):
            nc.gpsimd.memset(s["scores"][:], FMIN).then_inc(masked, 1)
            pool.wait_ge(masked, 1)


def pass_two(nc, ctx, x1, xg, x2T, s, ps):
    sem = lambda name: ctx.enter_context(nc.semaphore(name))
    x1_in, st_ok, ag_ok, var_ok, r_ok = sem("b_x1_in"), sem("b_stats"), sem("b_aggregated"), sem("b_var"), sem("b_rstd")
    norm_ok, scaled_ok, h2_ok = sem("b_normed"), sem("b_scaled"), sem("b_h2_ready")
    nT_ps, nT_ok, qkv_ps, q_ok, kv_ok = (sem("b_nT_in_psum"), sem("b_nT_ready"), sem("b_qkv_in_psum"), sem("b_q_ready"),
                                         sem("b_kv_ready"))
    prod_ok, sc_ok, soft, exp_ok, attn_step = sem("b_products"), sem("b_scores"), sem("b_softmax"), sem("b_exp"), sem("b_attn_step")
    pv_prod, aT_ps, aT_ok, pr_ps, haa_ok = sem("b_pv_product"), sem("b_aT_in_psum"), sem("b_aT_ready"), sem("b_proj_in_psum"), sem("b_after_attn")
    lg_ps, route, gexp_ok, gate_ok, x2_out, xg_ok, xg_out = (sem("b_logits_in_psum"), sem("b_route"), sem("b_gate_exp"), sem("b_gated"),
                                                         sem("b_x2_out"), sem("b_xg_ready"), sem("b_xg_out"))
    v, gp, ac, te = nc.vector, nc.gpsimd, nc.scalar, nc.tensor
    LN, AT = 3, 2 * B
    ident = s["ident"]

    with nc.Block() as block:
        @block.sync
        def _(sp):
            prime(sp, (xg_ok,), (x2_out, xg_out))
            with sp.Fori(0, PT) as t:
                sp.wait_ge(xg_ok, ONE + t)
                for b in range(B):
                    sp.dma_start(s["b_x1"][:, b, :], x1[b, bass.ds(t * P, P), :]).then_inc(x1_in, 16)
                sp.wait_ge(xg_ok, ONE + t + 1)
                for b in range(B):
                    sp.dma_start(xg[b, bass.ds(t * P, P), :], s["b_xg"][:, b, :]).then_inc(xg_out, 16)
                sp.wait_ge(lg_ps, t + 1)
                for k in range(KD):
                    sp.dma_start(x2T[:, k, bass.ds(t * B * P, B * P)], s["b_nT"][:, k, :]).then_inc(x2_out, 16)
            sp.wait_ge(xg_out, 16 + 16 * B * PT)
            sp.wait_ge(x2_out, 16 + 16 * KD * PT)

        @block.gpsimd
        def _(pool):
            mh = s["minus_half"]
            with pool.Fori(0, PT) as t:
                for l in range(LN):
                    pool.wait_ge(var_ok, t * LN + l + 1)
                    gp.tensor_tensor(s["b_r"][:, l, :], s["b_var"][:], mh[:], ALU.pow).then_inc(r_ok, 1)
                    if l == 0:
                        pool.wait_ge(scaled_ok, t + 1)
                        gp.tensor_tensor(s["b_h2"][:], s["b_n"][:], s["shift2"][:], ALU.add).then_inc(h2_ok, 1)

        @block.scalar
        def _(act):
            with act.Fori(0, PT) as t:
                act.wait_ge(x2_out, 16 + t * 16 * KD)
                for half in range(2):
                    for k in range(KD):
                        for c in range(2):
                            act.wait_ge(nT_ps, ((t * 2 + half) * 2 + k) * 2 + c + 1)
                            ac.activation(s["b_nT"][:, k, c * 512:(c + 1) * 512], ps[:, 2 * k + c, :], ACT.Identity,
                                          bias=s["ln_wb"][:, k, 2 * half + 1:2 * half + 2],
                                          scale=s["ln_wb"][:, k, 2 * half:2 * half + 1]).then_inc(nT_ok, 1)
                    if half == 0:
                        for b in range(B):
                            act.wait_ge(qkv_ps, t * B + b + 1)
                            bank = 4 + b % 4
                            ac.copy(s["b_q"][:, b, :], ps[:, bank, 0:QH * HD]).then_inc(q_ok, 1)
                            for kv, name in enumerate(("b_k", "b_v")):
                                src = ps[:, bank, QH * HD + kv * KVH * HD:QH * HD + (kv + 1) * KVH * HD]
                                src = src.rearrange("p (j d) -> p j d", d=HD).unsqueeze(2)
                                last = ac.copy(s[name][:, b, :].rearrange("p (j r d) -> p j r d", j=KVH, r=REP),
                                               bc(src, [P, KVH, REP, HD]))
                            last.then_inc(kv_ok, 1)
                        act.wait_ge(soft, t * 5 + 2)
                        ac.activation(s["scores_x"][:], s["scores_x"][:], ACT.Exp, scale=HD ** -0.5).then_inc(exp_ok, 1)
                        for k in range(KD):
                            for c in range(2):
                                act.wait_ge(aT_ps, (t * 2 + k) * 2 + c + 1)
                                ac.copy(s["b_aT"][:, k, c * 512:(c + 1) * 512], ps[:, 2 * k + c, :]).then_inc(aT_ok, 1)
                act.wait_ge(route, t * 10 + 2)
                ac.activation(s["b_gate"][:], s["b_gate"][:], ACT.Exp).then_inc(gexp_ok, 1)

        @block.tensor
        def _(pe):
            with pe.Fori(0, PT) as t:
                for half in range(2):
                    pe.wait_ge(norm_ok, (t * LN + 1 + half + 1) * B)
                    for k in range(KD):
                        for c in range(2):
                            for b in range(4):
                                last = te.transpose(ps[:, 2 * k + c, b * P:(b + 1) * P], s["b_n"][:, 4 * c + b, k * P:(k + 1) * P], ident[:])
                            last.then_inc(nT_ps, 1)
                    pe.wait_ge(nT_ok, (t * 2 + half + 1) * 4)
                    if half == 0:
                        for b in range(B):
                            if b >= 4:
                                pe.wait_ge(kv_ok, t * B + b - 3)
                            for k in range(KD):
                                last = te.matmul(ps[:, 4 + b % 4, 0:QKV], s["b_nT"][:, k, b * P:(b + 1) * P], s["w_qkv2"][:, k, :],
                                                 start=(k == 0), stop=(k == KD - 1))
                            last.then_inc(qkv_ps, 1)
                        pe.wait_ge(attn_step, (t + 1) * (B - 1))
                        for k in range(KD):
                            for c in range(2):
                                for b in range(4):
                                    last = te.transpose(ps[:, 2 * k + c, b * P:(b + 1) * P], s["b_attn"][:, 4 * c + b, k * P:(k + 1) * P], ident[:])
                                last.then_inc(aT_ps, 1)
                        pe.wait_ge(aT_ok, (t + 1) * 4)
                        for b in range(B):
                            for k in range(KD):
                                last = te.matmul(ps[:, 4 + b // 2, (b % 2) * D:(b % 2 + 1) * D], s["b_aT"][:, k, b * P:(b + 1) * P],
                                                 s["w_proj"][:, k, :], start=(k == 0), stop=(k == KD - 1))
                            last.then_inc(pr_ps, 1)
                for b in range(B):
                    for k in range(KD):
                        last = te.matmul(ps[:, 4, b * NEXP:(b + 1) * NEXP], s["b_nT"][:, k, b * P:(b + 1) * P], s["w_router"][:, k, :],
                                         start=(k == 0), stop=(k == KD - 1))
                last.then_inc(lg_ps, 1)

        @block.vector
        def _(dve):
            def layernorm(t, l, src):
                for b in range(B):
                    last = v.bn_stats(s["b_st"][:, b, :], src[:, b, :])
                last.then_inc(st_ok, 1)
                dve.wait_ge(st_ok, t * LN + l + 1)
                v.tensor_copy(s["pad"][:], s["b_st"][:, 0, 0:1])
                for b in range(B):
                    last = v.bn_aggr(s["b_mv"][:, b, :], s["b_st"][:, b, :])
                last.then_inc(ag_ok, 1)
                dve.wait_ge(ag_ok, t * LN + l + 1)
                v.tensor_scalar(s["b_var"][:], s["b_mv"][:, :, 1], 1e-5, None, ALU.add).then_inc(var_ok, 1)
                dve.wait_ge(r_ok, t * LN + l + 1)
                for b in range(B):
                    v.tensor_scalar(s["b_n"][:, b, :], src[:, b, :], s["b_mv"][:, b, 0:1], s["b_r"][:, l, b:b + 1],
                                    ALU.subtract, ALU.mult).then_inc(norm_ok, 1)

            with dve.Fori(0, PT) as t:
                dve.wait_ge(x1_in, (t + 1) * 16 * B)
                layernorm(t, 0, s["b_x1"])
                dve.wait_ge(norm_ok, (t * LN + 1) * B)
                v.tensor_tensor(s["b_n"][:], s["b_n"][:], s["scale2"][:], ALU.mult).then_inc(scaled_ok, 1)
                dve.wait_ge(h2_ok, t + 1)
                layernorm(t, 1, s["b_h2"])
                dve.wait_ge(q_ok, (t + 1) * B)
                dve.wait_ge(kv_ok, (t + 1) * B)
                for u in range(B):
                    if u >= 2:
                        dve.wait_ge(sc_ok, t * B + u - 1)
                    prod = s["b_prod"][:, u % 2, 0:B - u, :]
                    v.tensor_tensor(prod, s["b_q"][:, u:, :], bc(s["b_k"][:, u, :].unsqueeze(1), [P, B - u, D]), ALU.mult).then_inc(prod_ok, 1)
                    dve.wait_ge(prod_ok, t * B + u + 1)
                    v.tensor_reduce(s["scores"][:, u:, :, u], prod.rearrange("p a (h d) -> p a h d", d=HD), AX_X, ALU.add).then_inc(sc_ok, 1)
                flat = s["scores"][:].rearrange("p a h u -> p (a h) u")
                sx = s["scores_x"][:].rearrange("p (q u) -> p q u", u=B)
                rows = [P, B * QH, B]
                dve.wait_ge(sc_ok, (t + 1) * B)
                v.tensor_reduce(s["b_mx"][:], flat, AX_X, ALU.max).then_inc(soft, 1)
                dve.wait_ge(soft, t * 5 + 1)
                v.tensor_tensor(sx, flat, bc(s["b_mx"][:].unsqueeze(2), rows), ALU.subtract).then_inc(soft, 1)
                dve.wait_ge(exp_ok, t + 1)
                v.tensor_reduce(s["b_mx"][:], sx, AX_X, ALU.add).then_inc(soft, 1)
                dve.wait_ge(soft, t * 5 + 3)
                v.reciprocal(s["b_den"][:], s["b_mx"][:]).then_inc(soft, 1)
                dve.wait_ge(soft, t * 5 + 4)
                v.tensor_tensor(sx, sx, bc(s["b_den"][:].unsqueeze(2), rows), ALU.mult).then_inc(soft, 1)
                dve.wait_ge(soft, t * 5 + 5)
                probs = s["scores_x"][:].rearrange("p (a h u) -> p a h u", a=B, h=QH)
                for u in range(B):
                    dst = s["b_attn"][:] if u == 0 else s["b_prod"][:, u % 2, 0:B - u, :]
                    if u >= 3:
                        dve.wait_ge(attn_step, t * (B - 1) + u - 2)
                    for a in range(u, B):
                        last = v.tensor_tensor(dst[:, a - u, :].rearrange("p (h d) -> p h d", d=HD),
                                               s["b_v"][:, u, :].rearrange("p (h d) -> p h d", d=HD),
                                               bc(probs[:, a, :, u].unsqueeze(2), [P, QH, HD]), ALU.mult)
                    last.then_inc(pv_prod, 1)
                    dve.wait_ge(pv_prod, t * B + u + 1)
                    if u:
                        v.tensor_tensor(s["b_attn"][:, u:, :], s["b_attn"][:, u:, :], dst, ALU.add).then_inc(attn_step, 1)
                for b in range(B):
                    dve.wait_ge(pr_ps, t * B + (b // 2) * 2 + 2)
                    last = v.tensor_tensor(s["b_haa"][:, b, :], ps[:, 4 + b // 2, (b % 2) * D:(b % 2 + 1) * D], s["b_h2"][:, b, :], ALU.add)
                last.then_inc(haa_ok, 1)
                dve.wait_ge(haa_ok, t + 1)
                layernorm(t, 2, s["b_haa"])
                dve.wait_ge(xg_out, 16 + t * 16 * B)
                v.tensor_tensor(s["b_xg"][:], s["b_haa"][:], s["gate2"][:], ALU.mult).then_inc(gate_ok, 1)
                dve.wait_ge(gate_ok, t + 1)
                v.tensor_tensor(s["b_xg"][:], s["b_xg"][:], s["b_x1"][:], ALU.add).then_inc(xg_ok, 1)
                dve.wait_ge(lg_ps, t + 1)
                ten = lambda c: dve.wait_ge(route, t * 10 + c)
                lg = ps[:, 4, 0:B * NEXP].rearrange("p (b e) -> p b e", e=NEXP)
                wide = [P, B, NEXP]
                v.tensor_reduce(s["b_gm"][:], lg, AX_X, ALU.max).then_inc(route, 1)
                ten(1)
                v.tensor_tensor(s["b_gate"][:], lg, bc(s["b_gm"][:].unsqueeze(2), wide), ALU.subtract).then_inc(route, 1)
                dve.wait_ge(gexp_ok, t + 1)
                v.tensor_reduce(s["b_gs"][:], s["b_gate"][:], AX_X, ALU.add).then_inc(route, 1)
                ten(3)
                v.reciprocal(s["b_gm"][:], s["b_gs"][:]).then_inc(route, 1)
                ten(4)
                v.tensor_tensor(s["b_gate"][:], s["b_gate"][:], bc(s["b_gm"][:].unsqueeze(2), wide), ALU.mult).then_inc(route, 1)
                ten(5)
                v.tensor_copy(s["pad"][:], s["b_gate"][:, 0, 0:1])
                for b in range(B):
                    last = v.max(s["b_top"][:, b, :], s["b_gate"][:, b, :])
                last.then_inc(route, 1)
                ten(6)
                v.tensor_copy(s["pad"][:], s["b_top"][:, 0, 0:1])
                for b in range(B):
                    last = v.max_index(s["b_idx"][:, b, :], s["b_top"][:, b, :], s["b_gate"][:, b, :])
                last.then_inc(route, 1)
                ten(7)
                v.tensor_copy(s["b_idf"][:], s["b_idx"][:, :, 0:2]).then_inc(route, 1)
                ten(8)
                iota = bc(s["iota8"][:].unsqueeze(1), wide)
                for r in range(2):
                    last = v.tensor_tensor(s["b_hot"][:, r], iota, bc(s["b_idf"][:, :, r:r + 1], wide), ALU.is_equal)
                last.then_inc(route, 1)
                ten(9)
                for r in range(2):
                    last = v.tensor_tensor(s["b_hot"][:, r], s["b_hot"][:, r], bc(s["b_top"][:, :, r:r + 1], wide), ALU.mult)
                last.then_inc(route, 1)
                ten(10)
                v.tensor_tensor(s["wts"][:, bass.ds(t * B, B), :], s["b_hot"][:, 0], s["b_hot"][:, 1], ALU.add)


def pass_three(nc, ctx, x2T, xg, out, d, s, ps):
    sem = lambda name: ctx.enter_context(nc.semaphore(name))
    w_in, x_in, xg_in, up_ps, gelu_ok, down_ps, acc_ok, gated, y_ok, y_out, w_row = (
        sem("c_w_in"), sem("c_x_in"), sem("c_xg_in"), sem("c_up_in_psum"), sem("c_gelu"), sem("c_down_in_psum"), sem("c_acc"),
        sem("c_gated"), sem("c_y_ready"), sem("c_y_out"), sem("c_weight_rows"))
    v, gp, ac, te = nc.vector, nc.gpsimd, nc.scalar, nc.tensor
    NT = MT // P
    NI = TOK // MT

    with nc.Block() as block:
        @block.sync
        def _(sp):
            prime(sp, (up_ps, y_ok, down_ps, acc_ok), (y_out,))
            for e in range(NEXP):
                sp.dma_start(s["w_up"][:, e], d["w_up"][:, e]).then_inc(w_in, 16)
                sp.dma_start(s["w_down"][:, e], d["w_down"][:, e]).then_inc(w_in, 16)
            with sp.Fori(0, PT) as t:
                for half in range(2):
                    i = t * 2 + half
                    sp.wait_ge(up_ps, ONE + i * NEXP * FT)
                    sp.dma_start(s["c_x"][:], x2T[:, :, bass.ds(i * MT, MT)]).then_inc(x_in, 16)
                    sp.wait_ge(y_ok, ONE + i)
                    for c in range(NT):
                        sp.dma_start(s["c_xg"][:, c, :], xg[half * NT + c, bass.ds(t * P, P), :]).then_inc(xg_in, 16)
                    sp.wait_ge(y_ok, ONE + i + 1)
                    for c in range(NT):
                        sp.dma_start(out[half * NT + c, bass.ds(t * P, P), :], s["c_y"][:, c, :]).then_inc(y_out, 16)
            sp.wait_ge(y_out, 16 + 16 * NT * NI)

        @block.gpsimd
        def _(pool):
            with pool.Fori(0, PT) as t:
                for half in range(2):
                    i = t * 2 + half
                    pool.wait_ge(gated, i + 1)
                    pool.wait_ge(xg_in, (i + 1) * 16 * NT)
                    pool.wait_ge(y_out, 16 + i * 16 * NT)
                    gp.tensor_tensor(s["c_y"][:], s["c_g"][:], s["c_xg"][:], ALU.add).then_inc(y_ok, 1)

        @block.scalar
        def _(act):
            with act.Fori(0, NI) as i:
                for e in range(NEXP):
                    for f in range(FT):
                        u = e * FT + f
                        act.wait_ge(up_ps, ONE + i * NEXP * FT + u + 1)
                        if f == 0 and e >= 2:
                            act.wait_ge(down_ps, ONE + i * NEXP + e - 1)
                        elif f == 0:
                            act.wait_ge(down_ps, ONE + i * NEXP)
                        ac.activation(s["c_h"][:, e % 2, f, :], ps[:, u % 4, :], ACT.Gelu_apprx_tanh).then_inc(gelu_ok, 1)

        @block.tensor
        def _(pe):
            pe.wait_ge(w_in, 2 * NEXP * 16)
            with pe.Fori(0, NI) as i:
                def up(e):
                    for f in range(FT):
                        u = e * FT + f
                        if u >= 4:
                            pe.wait_ge(gelu_ok, i * NEXP * FT + u - 3)
                        for k in range(KD):
                            last = te.matmul(ps[:, u % 4, :], s["w_up"][:, e, k, f * P:(f + 1) * P], s["c_x"][:, k, :],
                                             start=(k == 0), stop=(k == KD - 1))
                        last.then_inc(up_ps, 1)

                def down(e):
                    pe.wait_ge(gelu_ok, (i * NEXP + e + 1) * FT)
                    if e >= 2:
                        pe.wait_ge(acc_ok, ONE + i * NEXP + e - 1)
                    else:
                        pe.wait_ge(acc_ok, ONE + i * NEXP)
                    for c in range(NT):
                        for f in range(FT):
                            last = te.matmul(ps[:, 4 + 2 * (e % 2) + c // 2, (c % 2) * D:(c % 2 + 1) * D], s["c_h"][:, e % 2, f, c * P:(c + 1) * P],
                                             s["w_down"][:, e, f, :], start=(f == 0), stop=(f == FT - 1))
                    last.then_inc(down_ps, 1)

                pe.wait_ge(x_in, (i + 1) * 16)
                up(0)
                for e in range(NEXP):
                    if e + 1 < NEXP:
                        up(e + 1)
                    down(e)

        @block.vector
        def _(dve):
            with dve.Fori(0, PT) as t:
                for half in range(2):
                    i = t * 2 + half
                    v.tensor_copy(s["c_w"][:], s["wts"][:, bass.ds(i * NT, NT), :]).then_inc(w_row, 1)
                    dve.wait_ge(w_row, i + 1)
                    for e in range(NEXP):
                        dve.wait_ge(down_ps, ONE + i * NEXP + e + 1)
                        if e:
                            dve.wait_ge(acc_ok, ONE + i * NEXP + e)
                        for c in range(NT):
                            src = ps[:, 4 + 2 * (e % 2) + c // 2, (c % 2) * D:(c % 2 + 1) * D]
                            if e == 0:
                                last = v.tensor_scalar(s["c_acc"][:, c, :], src, s["c_w"][:, c, 0:1], None, ALU.mult)
                            else:
                                last = v.scalar_tensor_tensor(s["c_acc"][:, c, :], src, s["c_w"][:, c, e:e + 1], s["c_acc"][:, c, :],
                                                              ALU.mult, ALU.add)
                        last.then_inc(acc_ok, 1)
                    dve.wait_ge(acc_ok, ONE + (i + 1) * NEXP)
                    dve.wait_ge(y_ok, ONE + i)
                    v.tensor_tensor(s["c_g"][:], s["c_acc"][:], s["gate2"][:, half * NT:(half + 1) * NT, :], ALU.mult).then_inc(gated, 1)


SHAPES = {
    "quad_mask": [P, QB],    "eye32": [P, C], "levels": [P, LEVELS, C], "chunk_mask": [P, 2, P],
    "w_qkv": [P, KD, 3 * D], "w_beta_mix": [P, KD, 2 * NH], "w_decay": [P, KD, D], "w_out": [P, KD, D],
    "conv_w": [P, M, TAPS], "onorm": [P, 1], "small_bias": [P, 2 * NH], "cT": [P, KD, B], "wmod": [P, KD, 6 * D],
}
SHARED = dict(ident=[P, P], iota8=[P, NEXP], pad=[P, 1], wts=[P, PT * B, NEXP], minus_half=[P, 8], mod=[B, 6 * D], shift1=[P, G, D], scale1=[P, G, D], gate1=[P, G, D],
              shift2=[P, B, D], scale2=[P, B, D], gate2=[P, B, D])
PASS2 = dict(
    w_qkv2=[P, KD, QKV], w_proj=[P, KD, D], w_router=[P, KD, NEXP], ln_wb=[P, KD, 4],
    b_x1=[P, B, D], b_n=[P, B, D], b_h2=[P, B, D], b_nT=[P, KD, B * P], b_st=[P, B, 6], b_mv=[P, B, 2], b_var=[P, B], b_r=[P, 3, B],
    b_q=[P, B, D], b_k=[P, B, D], b_v=[P, B, D], b_prod=[P, 2, B, D], scores=[P, B, QH, B], scores_x=[P, B * QH * B],
    b_mx=[P, B * QH], b_den=[P, B * QH], b_attn=[P, B, D], b_aT=[P, KD, B * P], b_haa=[P, B, D], b_xg=[P, B, D],
    b_gate=[P, B, NEXP], b_gm=[P, B], b_gs=[P, B], b_top=[P, B, 8], b_idf=[P, B, 2], b_hot=[P, 2, B, NEXP])
PASS3 = dict(w_up=[P, NEXP, KD, FF], w_down=[P, NEXP, FT, D], c_x=[P, KD, MT], c_xg=[P, 4, D], c_y=[P, 4, D], c_g=[P, 4, D],
             c_acc=[P, 4, D], c_h=[P, 2, FT, MT], c_w=[P, 4, NEXP])
SETUP = dict(scT=[P, KD, B], gate_sign=[B, D], sel_quad=[B, G, P], sel_all=[B, B, P])
PASS1 = dict(
    state=[P, B, PAIRS, P], x_in=[P, G, D], x_res=[P, G, D], x1_rows=[P, G, D], y=[P, G, D], ln_st=[P, G, 6], ln_mv=[P, G, 2],
    ln_v=[P, G], ln_r=[P, G], h=[P, G, D], hT=[P, KD, COLS], conv_in=[P, M, B, C + TAPS - 1], conv_acc=[P, M, COLS],
    qkvT=[P, M, COLS], th_decay=[P, PAIRS * COLS], gam=[P, PAIRS * COLS], omg=[P, PAIRS * COLS], ema_hist=[P, PAIRS * B],
    ema_out=[P, PAIRS, COLS], small=[P, G, 2 * NH], th_small=[P, G, 2 * NH], bm=[P, G, 2 * NH], omm=[P, G, NH],
    sq=[P, G, 2 * D], ss=[P, G, 2 * NH], rqk=[P, G, 2 * NH], ema_rows=[P, G, D], mix_e=[P, G, D], mix_d=[P, G, D],
    qkn=[P, G, 2, D], kb=[P, G, D], vb=[P, G, D], k_bd=[P, G, QB, D], knT=[P, G, PAIRS, P], kqT=[P, G, PAIRS, 2, P],
    LA=[P, G, NH, 2, P], Y=[P, G, NH, C], T=[P, G, NH, C], TTbd=[P, G, NH, P], u=[P, G, D], wT=[P, G, PAIRS, P], un=[P, G, D],
    o=[P, G, D], osq=[P, G, D], oss=[P, G, NH], orr=[P, G, NH], on=[P, G, D], onT=[P, G, KD, P])


def program(nc, d, x, out):
    x1 = nc.dram_tensor("x1_rows_dram", (B, L, D), F32, kind="Internal").ap()
    xg = nc.dram_tensor("xg_rows_dram", (B, L, D), F32, kind="Internal").ap()
    x2T = nc.dram_tensor("x2T_dram", (P, KD, TOK), F32, kind="Internal").ap()
    with ExitStack() as ctx:
        ps = ctx.enter_context(nc.psum_tensor("ps", [P, 8, 512], F32))
        zeroed = ctx.enter_context(nc.semaphore("zeroed"))
        s = {k: ctx.enter_context(nc.sbuf_tensor(k, v, F32)) for k, v in SHARED.items()}
        with ExitStack() as c1:
            s |= {k: c1.enter_context(nc.sbuf_tensor(k, v, F32)) for k, v in {**SHAPES, **SETUP, **PASS1, }.items()}
            mod_b = [s[name][:, g, :] for name in ("scale1", "shift1", "gate1") for g in range(G)]
            mod_b += [s[name][:, b, :] for name in ("scale2", "shift2", "gate2") for b in range(B)]
            setup_constants(nc, ctx, d, s, ps, mod_b, zeroed)
            pass_one(nc, ctx, x, x1, s, ps, zeroed)
        with ExitStack() as c2:
            s |= {k: c2.enter_context(nc.sbuf_tensor(k, v, F32)) for k, v in PASS2.items()}
            s["b_idx"] = c2.enter_context(nc.sbuf_tensor("b_idx", [P, B, 8], U32))
            setup_two(nc, ctx, d, s)
            pass_two(nc, ctx, x1, xg, x2T, s, ps)
        with ExitStack() as c3:
            s |= {k: c3.enter_context(nc.sbuf_tensor(k, v, F32)) for k, v in PASS3.items()}
            pass_three(nc, ctx, x2T, xg, out, d, s, ps)
    return x1


def constants():
    p = np.arange(P)
    same = (p[:, None] // C) == (p[None, :] // C)
    row, col = (p % C)[:, None], np.arange(C)[None, :]
    levels = np.stack([((row >> k) & 1 == 1) & ((col >> k) == (row >> k) - 1) for k in range(LEVELS)], 1)
    mask = np.stack([same & (p[None, :] > p[:, None]), same & (p[None, :] >= p[:, None])], 1)
    f = np.float32
    return {"ident": np.eye(P, dtype=f), "eye32": np.tile(np.eye(C, dtype=f), (P // C, 1)), "levels": levels.astype(f),
            "chunk_mask": mask.astype(f),
            "quad_mask": (p[:, None] // C == np.arange(QB)[None, :]).astype(f), "iota8": np.tile(np.arange(NEXP, dtype=f), (P, 1))}


def tiles(a):
    a = np.asarray(a)
    return np.ascontiguousarray(a.reshape(-1, P, *a.shape[1:]).swapaxes(0, 1))


def lay_out(i):
    a = {k: np.asarray(v) for k, v in i.items()}
    d = constants()
    d["w_qkv"] = tiles(np.concatenate([a["L0_attn_Wq"], a["L0_attn_Wk"], a["L0_attn_Wv"]], 0).T)
    d["w_beta_mix"] = tiles(np.concatenate([a["L0_attn_Wb"], a["L0_attn_Wmix"]], 0).T)
    d["w_decay"] = tiles(np.repeat(a["L0_attn_Wdec"], DH, axis=0).T)
    d["w_out"] = tiles(a["L0_attn_Wo"].T)
    d["conv_w"] = tiles(np.concatenate([a["L0_attn_wq_conv"], a["L0_attn_wk_conv"], a["L0_attn_wv_conv"]], 0))
    d["onorm"] = np.ascontiguousarray(np.tile(a["L0_attn_onorm_w"], P // DH)[:, None])
    d["small_bias"] = np.ascontiguousarray(np.tile(np.concatenate([np.zeros(NH, np.float32), a["L0_attn_mix_bias"]])[None], (P, 1)))
    d["w_qkv2"] = tiles(a["L0_ffn_qkv_weight"].T)
    d["w_proj"] = tiles(a["L0_ffn_proj_weight"].T)
    d["w_router"] = tiles(a["L0_ffn_router_weight"].T)
    d["ln_wb"] = tiles(np.stack([a["L0_ffn_ln1_weight"], a["L0_ffn_ln1_bias"], a["L0_ffn_ln2_weight"], a["L0_ffn_ln2_bias"]], 1))
    d["w_up"] = np.ascontiguousarray(a["L0_ffn_moe_w1"].reshape(NEXP, KD, P, FF).transpose(2, 0, 1, 3))
    d["w_down"] = np.ascontiguousarray(a["L0_ffn_moe_w2"].reshape(NEXP, FT, P, D).transpose(2, 0, 1, 3))
    d["cT"] = tiles(a["L0_c"].T)
    d["wmod"] = tiles(a["L0_wmod"])
    return d, np.ascontiguousarray(a["L0_attn_hidden_states"])


def kernel(**inputs):
    import concourse.bacc as bacc
    from concourse.bass_utils import run_bass_kernel_spmd

    nc = bacc.Bacc("TRN2", target_bir_lowering=False, num_devices=1)
    d, x = lay_out(inputs)
    arrays = {f"{name}_dram": a for name, a in d.items()} | {"x_dram": x}
    aps = {name: nc.dram_tensor(f"{name}_dram", a.shape, mybir.dt.from_np(a.dtype), kind="ExternalInput").ap() for name, a in d.items()}
    x_ap = nc.dram_tensor("x_dram", x.shape, F32, kind="ExternalInput").ap()
    out = nc.dram_tensor("out_0_dram", (B, L, D), F32, kind="ExternalOutput").ap()
    program(nc, aps, x_ap, out)
    r = run_bass_kernel_spmd(nc, [arrays], core_ids=[0])
    return r.results[0]["out_0_dram"]
```

```python
from contextlib import ExitStack

import numpy as np
import concourse.bass as bass
from concourse import mybir

ALU = mybir.AluOpType
ACT = mybir.ActivationFunctionType
F32 = mybir.dt.float32
U32 = mybir.dt.uint32
AX_X = mybir.AxisListType.X

P = 128
B, L, D = 8, 1024, 256
KD = D // P
C = 32
STEPS = L // C
G = 2
QB = B // G
NH, DH = 4, 64
PAIRS = NH // 2
TAPS = 4
M = 3 * KD
LEVELS = 5
COLS = B * C
NEXP, FF = 8, 512
FT = FF // P
QH, KVH, HD = 16, 4, 16
REP = QH // KVH
QKV = (QH + 2 * KVH) * HD
PT = L // P
TOK = B * L
TOPK = 2
REGION = TOK
TILES = (TOPK * TOK) // P + NEXP
SLOTS = (NEXP - 1) * REGION + TILES * P
DEEP = 8
XDEEP = 4
FMIN = float(np.finfo(np.float32).min)


def bc(ap, shape):
    return ap.broadcast_to(shape)


ONE = 1


def prime(eng, semaphores, dma_semaphores):
    for x in semaphores:
        eng.sem_inc(x, 1)
    for x in dma_semaphores:
        eng.sem_inc(x, 16)


def setup_constants(nc, ctx, dram, sbuf, psum, mod_b, zeroed):
    d, s = dram, sbuf
    sem = lambda name: ctx.enter_context(nc.semaphore(name))
    loaded, half_set, gates_in = sem("loaded"), sem("half_set"), sem("gates_in")
    sc_ready, mod_in_psum, mod_ready = sem("sc_ready"), sem("mod_in_psum"), sem("mod_ready")
    rows_in_psum, rows_out, wo_scaled = sem("rows_in_psum"), sem("rows_out"), sem("wo_scaled")
    gate_step = sem("gate_step")
    names = ["ident", "quad_mask", "eye32", "levels", "chunk_mask", "w_qkv", "w_beta_mix", "w_decay", "w_out", "conv_w",
             "onorm", "small_bias", "cT", "wmod", "iota8"]

    with nc.Block() as block:
        @block.sync
        def _(sp):
            for name in names:
                sp.dma_start(s[name][:], d[name]).then_inc(loaded, 16)

        @block.scalar
        def _(act):
            act.wait_ge(loaded, 16 * len(names))
            nc.scalar.activation(s["scT"][:], s["cT"][:], ACT.Silu).then_inc(sc_ready, 1)
            act.wait_ge(mod_in_psum, 1)
            nc.scalar.copy(s["mod"][:], psum[0:B, 0:3, :]).then_inc(mod_ready, 1)
            n = 0
            for dst in mod_b:
                act.wait_ge(rows_in_psum, n + 1)
                nc.scalar.copy(dst, psum[:, 4 + n % 4, 0:D]).then_inc(rows_out, 1)
                n += 1

        @block.tensor
        def _(pe):
            pe.wait_ge(sc_ready, 1)
            for c in range(3):
                for k in range(KD):
                    last = nc.tensor.matmul(psum[0:B, c, :], s["scT"][:, k, :],
                                            s["wmod"][:, k, c * 512:(c + 1) * 512], start=(k == 0), stop=(k == KD - 1))
            last.then_inc(mod_in_psum, 1)
            pe.wait_ge(gates_in, 1)
            n = 0
            for which in (1, 0, 2):
                for g in range(G):
                    if n >= 4:
                        pe.wait_ge(rows_out, n - 3)
                    nc.tensor.matmul(psum[:, 4 + n % 4, 0:D], s["sel_quad"][:, g, :],
                                     s["mod"][:, which * D:(which + 1) * D], start=True, stop=True).then_inc(rows_in_psum, 1)
                    n += 1

        @block.vector
        def _(dve):
            steps = [0]

            def link(ins):
                steps[0] += 1
                ins.then_inc(gate_step, 1)
                dve.wait_ge(gate_step, steps[0])

            dve.wait_ge(loaded, 16 * len(names))
            for k in range(KD):
                nc.vector.tensor_scalar(s["w_out"][:, k, :], s["w_out"][:, k, :], s["onorm"][:, 0:1], None, ALU.mult)
            for g in range(G):
                nc.vector.tensor_copy(s["sel_quad"][:, g, :].rearrange("b (i t) -> b i t", t=C),
                                      bc(s["ident"][0:B, g * QB:(g + 1) * QB].unsqueeze(2), [B, QB, C]))
            dve.wait_ge(mod_ready, 1)
            mod = s["mod"]
            for which in (2, 5):
                gate = mod[:, which * D:(which + 1) * D]
                link(nc.vector.tensor_scalar(s["gate_sign"][:], gate, 0.0, 2.0, ALU.is_ge, ALU.mult))
                link(nc.vector.tensor_scalar(s["gate_sign"][:], s["gate_sign"][:], -1.0, None, ALU.add))
                link(nc.vector.tensor_tensor(gate, gate, s["gate_sign"][:], ALU.mult))
                link(nc.vector.scalar_tensor_tensor(gate, gate, 0.25, s["gate_sign"][:], ALU.max, ALU.mult))
            for which in (1, 4):
                row = mod[:, which * D:(which + 1) * D]
                last = nc.vector.tensor_scalar(row, row, 1.0, None, ALU.add)
            last.then_inc(gates_in, 1)

        @block.gpsimd
        def _(pool):
            nc.gpsimd.memset(s["minus_half"][:], -0.5)
            for name in ("state", "conv_in", "ema_out", "TTbd", "knT"):
                nc.gpsimd.memset(s[name][:], 0.0)
            nc.gpsimd.memset(s["conv_acc"][:], 0.0).then_inc(zeroed, 1)
            pool.wait_ge(zeroed, 1)


def in_tick_order(*phases):
    ahead = [[next(p), k, p] for k, p in enumerate(phases)]
    while ahead:
        first = min(ahead, key=lambda x: (x[0], x[1]))
        try:
            first[0] = next(first[2])
        except StopIteration:
            ahead.remove(first)


def over_steps(eng, phase_a, phase_b, phase_c):
    phases = [(phase_c, 2), (phase_b, 1), (phase_a, 0)]

    def together(m, parity):
        in_tick_order(*[f(m - lag, (parity + lag) % 2) for f, lag in phases
                        if not isinstance(m, int) or 0 <= m - lag < STEPS])

    for m in range(4):
        together(m, m % 2)
    with eng.Fori(2, STEPS // 2) as j:
        for r in range(2):
            together(j * 2 + r, r)
    together(STEPS, 0)
    together(STEPS + 1, 1)


def once_positive(eng, semaphore, value):
    if not isinstance(value, int) or value > 0:
        eng.wait_ge(semaphore, value)


def own(bank):
    return bass.AP(bank.tensor, bank.offset, [bank.ap[0], (P + C, NH), (1, C)])


def pass_one(nc, ctx, x, x1, s, ps):
    sem = lambda name: ctx.enter_context(nc.semaphore(name))
    x_in, xres_in, x1_out = [sem("x_in_even"), sem("x_in_odd")], sem("xres_in"), sem("x1_out")
    st_ok, ag_ok, stats, rstd = sem("ln_stats"), sem("ln_aggregated"), sem("ln_var_eps"), sem("ln_rstd")
    normed, scaled, h_ready = sem("ln_normed"), sem("ln_scaled"), sem("h_ready")
    hT_ps, hT_ok = sem("hT_in_psum"), sem("hT_ready")
    proj_ps, decay_ps, small_ps = sem("proj_in_psum"), sem("decay_in_psum"), sem("small_in_psum")
    conv_in_ok, conv_tap, carried = sem("conv_in_ready"), sem("conv_tap"), sem("conv_carried")
    th_decay, small_sum, th_small, beta_ok = sem("tanh_decay"), sem("small_sum"), sem("tanh_small"), sem("beta_mix_ready")
    qkvT_ok, ema_in, ema_hist, ema_first, ema_ok = (sem("qkvT_ready"), sem("ema_gamma"), sem("ema_history"), sem("ema_first"),
                                                    sem("ema_ready"))
    qk_ps, v_ps, sq_ok, ssq_ok, eps_ok, r_ok = (sem("qk_rows_in_psum"), sem("v_rows_in_psum"), sem("squares"),
                                                sem("square_sums"), sem("norm_eps"), sem("norm_scale"))
    ema_rows, qkn_ok, kb_ok, mix_b = sem("ema_rows"), sem("qk_normed"), sem("kb_ready"), sem("mix_ema")
    knT_ps, kqT_ps, knT_ok, kqT_ok = sem("knT_in_psum"), sem("kqT_in_psum"), sem("knT_ready"), sem("kqT_ready")
    kbd_ok, gram_ps, gram_ok, lc_ok = sem("k_blocks_ready"), sem("gram_in_psum"), sem("gram_masked"), sem("L_compact")
    y0_ok = sem("L_level_0")
    y_ps, y_ok, z_ps, t_ok, tt_ok = sem("LT_in_psum"), sem("LT_masked"), sem("TLT_in_psum"), sem("T_ready"), sem("Tt_ready")
    uw_ps, uw_ok, ws_ps, o_ps, un_ok = sem("uw_in_psum"), sem("uw_ready"), sem("wS_in_psum"), sem("o_in_psum"), sem("u_new")
    ds_ps, s_ok, mix_a = sem("dS_in_psum"), sem("state_ready"), sem("mix_delta")
    o_ok, osq_ok, oss_ok, oeps_ok, or_ok = (sem("o_ready"), sem("o_squares"), sem("o_square_sums"), sem("o_norm_eps"),
                                            sem("o_norm_scale"))
    on_ok, onT_ps, onT_ok, wo_ps, gated, x1_ok = (sem("o_normed"), sem("onT_in_psum"), sem("onT_ready"),
                                                  sem("out_in_psum"), sem("gated"), sem("x1_ready"))
    v, gp, ac, te = nc.vector, nc.gpsimd, nc.scalar, nc.tensor
    heads = lambda ap: ap.rearrange("p (h d) -> p h d", d=DH)
    both = lambda ap: ap.rearrange("p a b -> p (a b)")
    ident = s["ident"]
    A_BANK = (0, 1)
    b_bank = lambda g: (2 + 2 * g, 3 + 2 * g)
    C_BANK = (6, 7)
    HALVES = (slice(0, DH), slice(DH, P))
    level_tick = lambda lev: 10 + 4 * lev
    c_tick = lambda g: 15 * g

    with nc.Block() as block:
        @block.sync
        def _(sp):
            def load(n, parity):
                once_positive(sp, normed, (n - 1) * G)
                for g in range(G):
                    for i in range(QB):
                        sp.dma_start(s["x_in"][i * C:(i + 1) * C, parity, g, :],
                                     x[g * QB + i, bass.ds(n * C, C), :]).then_inc(x_in[parity], 16)

            def residual_and_store(n):
                once_positive(sp, x1_ok, n * G)
                for g in range(G):
                    for i in range(QB):
                        sp.dma_start(s["x_res"][i * C:(i + 1) * C, g, :],
                                     x[g * QB + i, bass.ds(n * C, C), :]).then_inc(xres_in, 16)
                for g in range(G):
                    sp.wait_ge(x1_ok, n * G + g + 1)
                    for i in range(QB):
                        sp.dma_start(x1[g * QB + i, bass.ds(n * C, C), :],
                                     s["x1_rows"][i * C:(i + 1) * C, g, :]).then_inc(x1_out, 16)

            for n in range(4):
                load(n, n % 2)
            residual_and_store(0)
            with sp.Fori(2, STEPS // 2) as j:
                for r in range(2):
                    load(j * 2 + r, r)
                    residual_and_store(j * 2 + r - 3)
            for n in (STEPS - 3, STEPS - 2, STEPS - 1):
                residual_and_store(n)
            sp.wait_ge(x1_out, 16 * B * STEPS)

        @block.gpsimd
        def _(pool):
            mh = s["minus_half"]

            def phase_a(n, r):
                yield 2
                pool.wait_ge(stats, n + 1)
                gp.tensor_tensor(s["ln_r"][:], s["ln_v"][:], mh[:, 0:G], ALU.pow).then_inc(rstd, 1)
                yield 5
                pool.wait_ge(scaled, n + 1)
                gp.tensor_tensor(s["h"][:], s["h"][:], s["shift1"][:], ALU.add).then_inc(h_ready, 1)

            def phase_b(n, r):
                for g in range(G):
                    yield 3 + g
                    pool.wait_ge(eps_ok, n * G + g + 1)
                    gp.tensor_tensor(s["rqk"][:, g, :], s["ss"][:, g, :], mh[:, 0:2 * NH], ALU.pow).then_inc(r_ok, 1)
                for g in range(G):
                    yield 8 + 4 * g
                    pool.wait_ge(qkn_ok, n * G + g + 1)
                    once_positive(pool, ds_ps, (n - 1) * G * PAIRS)
                    gp.tensor_tensor(s["k_bd"][:, r, g], bc(s["qkn"][:, g, 1, :].unsqueeze(1), [P, QB, D]),
                                     bc(s["quad_mask"][:].unsqueeze(2), [P, QB, D]), ALU.mult).then_inc(kbd_ok, 1)
                for g in range(G):
                    yield 16 + g
                    pool.wait_ge(ema_rows, n * G + g + 1)
                    pool.wait_ge(beta_ok, n + 1)
                    gp.tensor_tensor(heads(s["mix_e"][:, r, g, :]), heads(s["ema_rows"][:, g, :]),
                                     bc(s["bm"][:, g, NH:2 * NH].unsqueeze(2), [P, NH, DH]), ALU.mult).then_inc(mix_b, 1)

            def phase_c(n, r):
                for g in range(G):
                    yield c_tick(g) + 9
                    pool.wait_ge(oeps_ok, n * G + g + 1)
                    gp.tensor_tensor(s["orr"][:, g, :], s["oss"][:, g, :], mh[:, 0:NH], ALU.pow).then_inc(or_ok, 1)
                    yield c_tick(g) + 15
                    pool.wait_ge(gated, n * G + g + 1)
                    pool.wait_ge(xres_in, (n + 1) * 16 * B)
                    once_positive(pool, x1_out, n * 16 * B)
                    gp.tensor_tensor(s["x1_rows"][:, g, :], s["y"][:, g, :], s["x_res"][:, g, :], ALU.add).then_inc(x1_ok, 1)

            over_steps(pool, phase_a, phase_b, phase_c)

        @block.scalar
        def _(act):
            def phase_a(n, r):
                yield 7
                act.wait_ge(hT_ps, n + 1)
                ac.copy(both(s["hT"][:]), ps[:, A_BANK[1], :]).then_inc(hT_ok, 1)
                for c in range(3):
                    yield 9 + c
                    act.wait_ge(proj_ps, n * 3 + c + 1)
                    if c == 0:
                        once_positive(act, carried, n)
                    ac.copy(s["conv_in"][:, 2 * c:2 * c + 2, :, TAPS - 1:],
                            ps[:, A_BANK[c % 2], :].rearrange("p (m b t) -> p m b t", m=2, t=C)).then_inc(conv_in_ok, 1)
                yield 12
                act.wait_ge(decay_ps, n + 1)
                ac.activation(s["th_decay"][:], ps[:, A_BANK[1], :], ACT.Tanh, scale=0.5).then_inc(th_decay, 1)
                yield 14
                act.wait_ge(small_sum, n + 1)
                ac.activation(s["th_small"][:, r], s["small"][:], ACT.Tanh, scale=0.5).then_inc(th_small, 1)
                yield 20
                act.wait_ge(conv_tap, (n + 1) * TAPS)
                once_positive(act, v_ps, (n - 1) * G)
                ac.activation(s["qkvT"][:, r], s["conv_acc"][:], ACT.Silu).then_inc(qkvT_ok, 1)
                ac.copy(s["conv_in"][:, :, :, 0:TAPS - 1].rearrange("p m b t -> p (m b) t"),
                        s["conv_in"][:, :, :, C:C + TAPS - 1].rearrange("p m b t -> p (m b) t")).then_inc(carried, 1)

            def phase_b(n, r):
                for g in range(G):
                    yield 1
                    act.wait_ge(qk_ps, n * G + g + 1)
                    ac.activation(s["sq"][:, g, :], ps[:, b_bank(g)[0], :], ACT.Square).then_inc(sq_ok, 1)
                    act.wait_ge(v_ps, n * G + g + 1)
                    once_positive(act, mix_b, n * G)
                    ac.copy(s["ema_rows"][:, g, :], ps[:, b_bank(g)[1], D:2 * D]).then_inc(ema_rows, 1)
                for g in range(G):
                    yield 7
                    act.wait_ge(knT_ps, n * G + g + 1)
                    for par, half in enumerate(HALVES):
                        last = ac.copy(s["knT"][half, g, par], ps[half, b_bank(g)[0], 0:D].rearrange("p (m t) -> p m t", m=PAIRS))
                    last.then_inc(knT_ok, 1)
                    yield 8
                    act.wait_ge(kqT_ps, n * G + g + 1)
                    ac.copy(s["kqT"][:, r, g].rearrange("p a b c -> p (a b c)"), ps[:, b_bank(g)[1], :]).then_inc(kqT_ok, 1)

            def phase_c(n, r):
                for g in range(G):
                    t = c_tick(g)
                    yield t + 1
                    act.wait_ge(uw_ps, n * G + g + 1)
                    ac.copy(s["u"][:, g, :], ps[:, C_BANK[0], 0:D])
                    ac.copy(both(s["wT"][:, g]), ps[:, C_BANK[1], 0:D]).then_inc(uw_ok, 1)
                    yield t + 7
                    act.wait_ge(o_ok, n * G + g + 1)
                    ac.activation(s["osq"][:, g, :], s["o"][:, g, :], ACT.Square).then_inc(osq_ok, 1)
                    yield t + 12
                    act.wait_ge(onT_ps, n * G + g + 1)
                    ac.copy(both(s["onT"][:, g]), ps[:, C_BANK[0], 0:D]).then_inc(onT_ok, 1)

            over_steps(act, phase_a, phase_b, phase_c)

        @block.tensor
        def _(pe):
            def phase_a(n, r):
                yield 6
                pe.wait_ge(h_ready, n + 1)
                once_positive(pe, th_decay, n)
                for k in range(KD):
                    for g in range(G):
                        last = te.transpose(ps[:, A_BANK[1], (k * G + g) * P:(k * G + g + 1) * P], s["h"][:, g, k * P:(k + 1) * P], ident[:])
                last.then_inc(hT_ps, 1)
                for c in range(3):
                    yield 8 + c
                    pe.wait_ge(hT_ok, n + 1)
                    if c == 0:
                        once_positive(pe, small_sum, n)
                    if c == 2:
                        pe.wait_ge(conv_in_ok, n * 3 + 1)
                    for m in (2 * c, 2 * c + 1):
                        for k in range(KD):
                            last = te.matmul(ps[:, A_BANK[c % 2], (m % 2) * COLS:(m % 2 + 1) * COLS], s["w_qkv"][:, k, m * P:(m + 1) * P],
                                             s["hT"][:, k, :], start=(k == 0), stop=(k == KD - 1))
                    last.then_inc(proj_ps, 1)
                yield 11
                pe.wait_ge(conv_in_ok, n * 3 + 2)
                for pair in range(PAIRS):
                    for k in range(KD):
                        last = te.matmul(ps[:, A_BANK[1], pair * COLS:(pair + 1) * COLS], s["w_decay"][:, k, pair * P:(pair + 1) * P],
                                         s["hT"][:, k, :], start=(k == 0), stop=(k == KD - 1))
                last.then_inc(decay_ps, 1)
                yield 12
                pe.wait_ge(conv_in_ok, n * 3 + 3)
                for g in range(G):
                    for k in range(KD):
                        last = te.matmul(ps[:, A_BANK[0], g * P:(g + 1) * P], s["hT"][:, k, g * P:(g + 1) * P],
                                         s["w_beta_mix"][:, k, :], start=(k == 0), stop=(k == KD - 1))
                last.then_inc(small_ps, 1)

            def phase_b(n, r):
                for g in range(G):
                    yield 0
                    pe.wait_ge(qkvT_ok, n + 1)
                    once_positive(pe, tt_ok, n * LEVELS * G)
                    for m in range(4):
                        last = te.transpose(ps[:, b_bank(g)[0], m * P:(m + 1) * P], s["qkvT"][:, r, m, g * P:(g + 1) * P], ident[:])
                    last.then_inc(qk_ps, 1)
                    pe.wait_ge(ema_ok, n + 1)
                    for m in range(2):
                        te.transpose(ps[:, b_bank(g)[1], m * P:(m + 1) * P], s["qkvT"][:, r, 4 + m, g * P:(g + 1) * P], ident[:])
                    for m in range(2):
                        last = te.transpose(ps[:, b_bank(g)[1], (2 + m) * P:(3 + m) * P], s["ema_out"][:, r, m, g * P:(g + 1) * P], ident[:])
                    last.then_inc(v_ps, 1)
                for g in range(G):
                    yield 6
                    pe.wait_ge(qkn_ok, n * G + g + 1)
                    for m in range(PAIRS):
                        last = te.transpose(ps[:, b_bank(g)[0], m * P:(m + 1) * P], s["qkn"][:, g, 1, m * P:(m + 1) * P], ident[:])
                    last.then_inc(knT_ps, 1)
                    yield 7
                    pe.wait_ge(kb_ok, n * G + g + 1)
                    for m in range(PAIRS):
                        te.transpose(ps[:, b_bank(g)[1], 2 * m * P:(2 * m + 1) * P], s["kb"][:, r, g, m * P:(m + 1) * P], ident[:])
                        last = te.transpose(ps[:, b_bank(g)[1], (2 * m + 1) * P:(2 * m + 2) * P], s["qkn"][:, g, 0, m * P:(m + 1) * P], ident[:])
                    last.then_inc(kqT_ps, 1)
                for g in range(G):
                    yield 9
                    pe.wait_ge(knT_ok, n * G + g + 1)
                    pe.wait_ge(kqT_ok, n * G + g + 1)
                    for par in range(2):
                        for m in range(PAIRS):
                            last = te.matmul(ps[:, b_bank(g)[par], m * 2 * P:(m + 1) * 2 * P], s["knT"][:, g, par, m, :],
                                             both(s["kqT"][:, r, g, m]), start=True, stop=True)
                    last.then_inc(gram_ps, 1)
                for lev in range(1, LEVELS):
                    for g in range(G):
                        yield level_tick(lev)
                        pe.wait_ge(t_ok, (n * LEVELS + lev - 1) * G + g + 1)
                        for h in range(NH):
                            last = te.matmul(ps[:, b_bank(g)[0], h * P:(h + 1) * P], s["LA"][:, r, g, h, 0, :], both(s["T"][:, g]), start=True, stop=True)
                        last.then_inc(y_ps, 1)
                    for g in range(G):
                        yield level_tick(lev) + 2
                        pe.wait_ge(y_ok, (n * (LEVELS - 1) + lev - 1) * G + g + 1)
                        pe.wait_ge(tt_ok, (n * LEVELS + lev - 1) * G + g + 1)
                        for h in range(NH):
                            last = te.matmul(ps[:, b_bank(g)[1], h * P:(h + 1) * P], s["TTbd"][:, r, g, h, :], both(s["Y"][:, g]), start=True, stop=True)
                        last.then_inc(z_ps, 1)

            def phase_c(n, r):
                for g in range(G):
                    t = c_tick(g)
                    yield t
                    pe.wait_ge(tt_ok, (n * LEVELS + LEVELS - 1) * G + g + 1)
                    once_positive(pe, gated, n * G + g)
                    for h in range(NH):
                        te.matmul(ps[:, C_BANK[0], h * DH:(h + 1) * DH], s["TTbd"][:, r, g, h, :], s["vb"][:, r, g, h * DH:(h + 1) * DH], start=True, stop=True)
                        last = te.matmul(ps[(h % 2) * DH:(h % 2 + 1) * DH, C_BANK[1], (h // 2) * P:(h // 2 + 1) * P],
                                         s["kb"][:, r, g, h * DH:(h + 1) * DH], s["TTbd"][:, r, g, h, :], start=True, stop=True)
                    last.then_inc(uw_ps, 1)
                    yield t + 2
                    pe.wait_ge(uw_ok, n * G + g + 1)
                    once_positive(pe, s_ok, (n - 1) * G + g + 1)
                    for pair in range(PAIRS):
                        for i in range(QB):
                            last = te.matmul(ps[i * C:(i + 1) * C, C_BANK[0], pair * P:(pair + 1) * P], s["wT"][:, g, pair, i * C:(i + 1) * C],
                                             s["state"][:, g * QB + i, pair, :], start=True, stop=True)
                    last.then_inc(ws_ps, 1)
                    for pair in range(PAIRS):
                        for i in range(QB):
                            te.matmul(ps[i * C:(i + 1) * C, C_BANK[1], pair * P:(pair + 1) * P], s["kqT"][:, r, g, pair, 1, i * C:(i + 1) * C],
                                      s["state"][:, g * QB + i, pair, :], start=(pair == 0), stop=False, skip_group_check=True)
                    yield t + 4
                    pe.wait_ge(un_ok, n * G + g + 1)
                    pe.wait_ge(kbd_ok, n * G + g + 1)

                    def state_product(pair, i):
                        return te.matmul(ps[:, C_BANK[pair], i * P:(i + 1) * P], s["k_bd"][:, r, g, i, pair * P:(pair + 1) * P],
                                         s["un"][:, g, pair * P:(pair + 1) * P], start=True, stop=True)

                    for h in range(NH):
                        last = te.matmul(ps[:, C_BANK[1], h * DH:(h + 1) * DH], s["LA"][:, r, g, h, 1, :], s["un"][:, g, h * DH:(h + 1) * DH],
                                         start=False, stop=True, skip_group_check=True)
                        if h == NH - 1:
                            last.then_inc(o_ps, 1)
                        last = state_product(0, h)
                    last.then_inc(ds_ps, 1)
                    yield t + 6
                    pe.wait_ge(mix_a, n * G + g + 1)
                    for i in range(QB):
                        last = state_product(1, i)
                    last.then_inc(ds_ps, 1)
                    yield t + 11
                    pe.wait_ge(on_ok, n * G + g + 1)
                    for m in range(KD):
                        last = te.transpose(ps[:, C_BANK[0], m * P:(m + 1) * P], s["on"][:, g, m * P:(m + 1) * P], ident[:])
                    last.then_inc(onT_ps, 1)
                    yield t + 13
                    pe.wait_ge(onT_ok, n * G + g + 1)
                    for k in range(KD):
                        last = te.matmul(ps[:, C_BANK[1], 0:D], s["onT"][:, g, k, :], s["w_out"][:, k, :], start=(k == 0), stop=(k == KD - 1))
                    last.then_inc(wo_ps, 1)

            over_steps(pe, phase_a, phase_b, phase_c)

        @block.vector
        def _(dve):
            def phase_a(n, r):
                yield 0
                dve.wait_ge(x_in[r], (n - r) * (8 * B) + 16 * B)
                for g in range(G):
                    last = v.bn_stats(s["ln_st"][:, g, :], s["x_in"][:, r, g, :])
                last.then_inc(st_ok, 1)
                yield 1
                dve.wait_ge(st_ok, n + 1)
                v.tensor_copy(s["pad"][:], s["ln_st"][:, 0, 0:1])
                for g in range(G):
                    last = v.bn_aggr(s["ln_mv"][:, g, :], s["ln_st"][:, g, :])
                last.then_inc(ag_ok, 1)
                dve.wait_ge(ag_ok, n + 1)
                v.tensor_scalar(s["ln_v"][:], s["ln_mv"][:, :, 1], 1e-5, None, ALU.add).then_inc(stats, 1)
                yield 3
                dve.wait_ge(rstd, n + 1)
                for g in range(G):
                    v.tensor_scalar(s["h"][:, g, :], s["x_in"][:, r, g, :], s["ln_mv"][:, g, 0:1], s["ln_r"][:, g:g + 1],
                                    ALU.subtract, ALU.mult).then_inc(normed, 1)
                yield 4
                dve.wait_ge(normed, (n + 1) * G)
                v.tensor_tensor(s["h"][:], s["h"][:], s["scale1"][:], ALU.mult).then_inc(scaled, 1)
                for j in range(TAPS):
                    yield (11, 12, 14, 16)[j]
                    dve.wait_ge(conv_in_ok, n * 3 + 3)
                    if j:
                        dve.wait_ge(conv_tap, n * TAPS + j)
                    for m in range(M):
                        xin = s["conv_in"][:, m, :, j:j + C]
                        acc = s["conv_acc"][:, m, :].rearrange("p (b t) -> p b t", t=C)
                        if j == 0:
                            last = v.tensor_scalar(acc, xin, s["conv_w"][:, m, 0:1], None, ALU.mult)
                        else:
                            last = v.scalar_tensor_tensor(acc, xin, s["conv_w"][:, m, j:j + 1], acc, ALU.mult, ALU.add)
                    last.then_inc(conv_tap, 1)
                    if j == 1:
                        yield 13
                        dve.wait_ge(small_ps, n + 1)
                        v.tensor_tensor(s["small"][:], ps[:, A_BANK[0], 0:G * P].rearrange("p (g e) -> p g e", g=G)[:, :, 0:2 * NH],
                                        bc(s["small_bias"][:].unsqueeze(1), [P, G, 2 * NH]), ALU.add).then_inc(small_sum, 1)
                first = lambda t: t.rearrange("p (q t) -> p q t", t=C)
                yield 18
                dve.wait_ge(th_decay, n + 1)
                v.tensor_scalar(s["gam"][:], s["th_decay"][:], 0.5, 0.5, ALU.mult, ALU.add)
                v.tensor_scalar(s["omg"][:], s["th_decay"][:], -0.5, 0.5, ALU.mult, ALU.add).then_inc(ema_in, 1)
                yield 21
                dve.wait_ge(ema_in, n + 1)
                dve.wait_ge(qkvT_ok, n + 1)
                v.tensor_tensor(s["omg"][:], s["omg"][:], both(s["qkvT"][:, r, 4:6, :]), ALU.mult)
                v.tensor_tensor(s["ema_hist"][:], first(s["gam"][:])[:, :, 0], first(both(s["ema_out"][:, 1 - r]))[:, :, C - 1],
                                ALU.mult).then_inc(ema_hist, 1)
                yield 22
                dve.wait_ge(ema_hist, n + 1)
                v.tensor_tensor(first(s["omg"][:])[:, :, 0], first(s["omg"][:])[:, :, 0], s["ema_hist"][:], ALU.add)
                v.memset(first(s["gam"][:])[:, :, 0], 0.0).then_inc(ema_first, 1)
                yield 23
                dve.wait_ge(ema_first, n + 1)
                v.tensor_tensor_scan(both(s["ema_out"][:, r]), s["gam"][:], s["omg"][:], 0.0, ALU.mult, ALU.add).then_inc(ema_ok, 1)

            def phase_b(n, r):
                yield 1
                dve.wait_ge(th_small, n + 1)
                once_positive(dve, mix_b, n * G)
                v.tensor_scalar(s["bm"][:], s["th_small"][:, r], 0.5, 0.5, ALU.mult, ALU.add)
                v.tensor_scalar(s["omm"][:, r], s["th_small"][:, r, :, NH:], -0.5, 0.5, ALU.mult, ALU.add).then_inc(beta_ok, 1)
                for g in range(G):
                    yield 2 + g
                    dve.wait_ge(sq_ok, n * G + g + 1)
                    v.tensor_reduce(s["ss"][:, g, :], heads(s["sq"][:, g, :]), AX_X, ALU.add).then_inc(ssq_ok, 1)
                    dve.wait_ge(ssq_ok, n * G + g + 1)
                    v.tensor_scalar(s["ss"][:, g, :], s["ss"][:, g, :], 1e-6, None, ALU.add).then_inc(eps_ok, 1)
                for g in range(G):
                    yield 5 + g
                    beta = bc(s["bm"][:, g, 0:NH].unsqueeze(2), [P, NH, DH])
                    dve.wait_ge(r_ok, n * G + g + 1)
                    once_positive(dve, kbd_ok, (n - 1) * G + g + 1)
                    v.tensor_tensor(heads(both(s["qkn"][:, g])), heads(ps[:, b_bank(g)[0], :]),
                                    bc(s["rqk"][:, g, :].unsqueeze(2), [P, 2 * NH, DH]), ALU.mult).then_inc(qkn_ok, 1)
                    dve.wait_ge(ema_rows, n * G + g + 1)
                    dve.wait_ge(beta_ok, n + 1)
                    v.tensor_tensor(heads(s["vb"][:, r, g, :]), heads(ps[:, b_bank(g)[1], 0:D]), beta, ALU.mult)
                    dve.wait_ge(qkn_ok, n * G + g + 1)
                    v.tensor_tensor(heads(s["kb"][:, r, g, :]), heads(s["qkn"][:, g, 1, :]), beta, ALU.mult).then_inc(kb_ok, 1)
                for g in range(G):
                    yield 10
                    dve.wait_ge(gram_ps, n * G + g + 1)
                    mask = bc(both(s["chunk_mask"][:]).unsqueeze(1), [P, PAIRS, 2 * P])
                    for par in range(2):
                        dst = s["LA"][:, r, g, par::2].rearrange("p m a b -> p m (a b)")
                        last = v.tensor_tensor(dst, ps[:, b_bank(g)[par], :].rearrange("p (m c) -> p m c", m=PAIRS), mask, ALU.mult)
                    last.then_inc(gram_ok, 1)
                for g in range(G):
                    yield 11
                    dve.wait_ge(gram_ok, n * G + g + 1)
                    for i in range(QB):
                        q = slice(i * C, (i + 1) * C)
                        last = v.transpose(s["Y"][q, g], s["LA"][q, r, g, :, 0, q])
                    last.then_inc(lc_ok, 1)
                for g in range(G):
                    yield 12
                    dve.wait_ge(lc_ok, n * G + g + 1)
                    v.tensor_tensor(s["Y0"][:, g], s["Y"][:, g], bc(s["levels"][:, 0, :].unsqueeze(1), [P, NH, C]), ALU.mult).then_inc(y0_ok, 1)
                for lev in range(LEVELS):
                    if lev:
                        for g in range(G):
                            yield level_tick(lev) + 1
                            dve.wait_ge(y_ps, (n * (LEVELS - 1) + lev - 1) * G + g + 1)
                            v.tensor_tensor(s["Y"][:, g], own(ps[:, b_bank(g)[0], :]),
                                            bc(s["levels"][:, lev, :].unsqueeze(1), [P, NH, C]), ALU.mult).then_inc(y_ok, 1)
                    for g in range(G):
                        yield level_tick(lev) + 3
                        if lev == 0:
                            dve.wait_ge(y0_ok, n * G + g + 1)
                            v.tensor_tensor(s["T"][:, g], bc(s["eye32"][:].unsqueeze(1), [P, NH, C]), s["Y0"][:, g],
                                            ALU.subtract).then_inc(t_ok, 1)
                        else:
                            dve.wait_ge(z_ps, (n * (LEVELS - 1) + lev - 1) * G + g + 1)
                            v.tensor_tensor(s["T"][:, g], s["T"][:, g], own(ps[:, b_bank(g)[1], :]),
                                            ALU.subtract).then_inc(t_ok, 1)
                    for g in range(G):
                        yield level_tick(lev) + 3
                        dve.wait_ge(t_ok, (n * LEVELS + lev) * G + g + 1)
                        for i in range(QB):
                            q = slice(i * C, (i + 1) * C)
                            last = v.transpose(s["TTbd"][q, r, g, :, q], s["T"][q, g])
                        last.then_inc(tt_ok, 1)

            def phase_c(n, r):
                for g in range(G):
                    t = c_tick(g)
                    yield t + 3
                    dve.wait_ge(ws_ps, n * G + g + 1)
                    v.tensor_tensor(s["un"][:, g, :], s["u"][:, g, :], ps[:, C_BANK[0], 0:D], ALU.subtract).then_inc(un_ok, 1)
                    yield t + 5
                    dve.wait_ge(o_ps, n * G + g + 1)
                    v.tensor_tensor(heads(s["mix_d"][:, g, :]), heads(ps[:, C_BANK[1], 0:D]),
                                    bc(s["omm"][:, r, g, :].unsqueeze(2), [P, NH, DH]), ALU.mult).then_inc(mix_a, 1)
                    yield t + 6
                    dve.wait_ge(mix_a, n * G + g + 1)
                    dve.wait_ge(mix_b, n * G + g + 1)
                    v.tensor_tensor(s["o"][:, g, :], s["mix_d"][:, g, :], s["mix_e"][:, r, g, :], ALU.add).then_inc(o_ok, 1)
                    for pair in range(PAIRS):
                        yield t + 6 + pair
                        dve.wait_ge(ds_ps, (n * G + g) * PAIRS + pair + 1)
                        for par, half in enumerate(HALVES):
                            st = s["state"][half, g * QB:(g + 1) * QB, pair, half]
                            last = v.tensor_tensor(st, st, ps[half, C_BANK[pair], :].rearrange("p (i c) -> p i c", i=QB)[:, :, half], ALU.add)
                    last.then_inc(s_ok, 1)
                    yield t + 8
                    dve.wait_ge(osq_ok, n * G + g + 1)
                    v.tensor_reduce(s["oss"][:, g, :], heads(s["osq"][:, g, :]), AX_X, ALU.add).then_inc(oss_ok, 1)
                    dve.wait_ge(oss_ok, n * G + g + 1)
                    v.tensor_scalar(s["oss"][:, g, :], s["oss"][:, g, :], 1.0 / DH, 1e-5, ALU.mult, ALU.add).then_inc(oeps_ok, 1)
                    yield t + 10
                    dve.wait_ge(or_ok, n * G + g + 1)
                    v.tensor_tensor(heads(s["on"][:, g, :]), heads(s["o"][:, g, :]), bc(s["orr"][:, g, :].unsqueeze(2), [P, NH, DH]),
                                    ALU.mult).then_inc(on_ok, 1)
                    yield t + 14
                    dve.wait_ge(wo_ps, n * G + g + 1)
                    v.tensor_tensor(s["y"][:, g, :], ps[:, C_BANK[1], 0:D], s["gate1"][:, g, :], ALU.mult).then_inc(gated, 1)

            over_steps(dve, phase_a, phase_b, phase_c)


def setup_two(nc, ctx, d, s, ps, table, weights_in):
    sem = lambda name: ctx.enter_context(nc.semaphore(name))
    loaded, masked, sel_ok = sem("b_loaded"), sem("b_masked"), sem("b_selection")
    rows_in_psum, rows_out = sem("b_rows_in_psum"), sem("b_rows_out")
    rows = [(s[name][:, b, :], which, b) for name, which in (("scale2", 4), ("shift2", 3), ("gate2", 5)) for b in range(B)]
    names = ["w_qkv2", "w_proj", "w_router", "ln_wb", "region", "next_slot", "slot_steps", "earlier", "b_ids_f", "scan_reset"]
    with nc.Block() as block:
        @block.sync
        def _(sp):
            for name in names:
                sp.dma_start(s[name][:], d[name]).then_inc(loaded, 16)
            sp.dma_start(table, d["empty_slots"]).then_inc(loaded, 16)
            for name in ("w_up", "w_down"):
                sp.dma_start(s[name][:], d[name]).then_inc(weights_in, 16)
            sp.wait_ge(loaded, 16 * (len(names) + 1))

        @block.vector
        def _(dve):
            nc.vector.tensor_copy(s["sel_all"][:], bc(s["ident"][0:B, 0:B].unsqueeze(2), [B, B, P])).then_inc(sel_ok, 1)

        @block.tensor
        def _(pe):
            pe.wait_ge(sel_ok, 1)
            for n, (_, which, b) in enumerate(rows):
                if n >= 4:
                    pe.wait_ge(rows_out, n - 3)
                nc.tensor.matmul(ps[:, n % 4, 0:D], s["sel_all"][:, b, :], s["mod"][:, which * D:(which + 1) * D],
                                 start=True, stop=True).then_inc(rows_in_psum, 1)

        @block.scalar
        def _(act):
            for n, (row, _, _) in enumerate(rows):
                act.wait_ge(rows_in_psum, n + 1)
                nc.scalar.copy(row, ps[:, n % 4, 0:D]).then_inc(rows_out, 1)
            act.wait_ge(rows_out, len(rows))

        @block.gpsimd
        def _(pool):
            nc.gpsimd.memset(s["ones"][:], 1.0).then_inc(masked, 1)
            nc.gpsimd.memset(s["scores"][:], FMIN).then_inc(masked, 1)
            pool.wait_ge(masked, 2)


def pass_two(nc, ctx, x1, xg, x2n, table, s, ps):
    sem = lambda name: ctx.enter_context(nc.semaphore(name))
    x1_in, st_ok, ag_ok, var_ok, r_ok = sem("b_x1_in"), sem("b_stats"), sem("b_aggregated"), sem("b_var"), sem("b_rstd")
    norm_ok, scaled_ok, h2_ok = sem("b_normed"), sem("b_scaled"), sem("b_h2_ready")
    nT_ps, nT_ok, qkv_ps, q_ok, kv_ok = (sem("b_nT_in_psum"), sem("b_nT_ready"), sem("b_qkv_in_psum"), sem("b_q_ready"),
                                         sem("b_kv_ready"))
    prod_ok, sc_ok, soft, exp_ok, attn_step = sem("b_products"), sem("b_scores"), sem("b_softmax"), sem("b_exp"), sem("b_attn_step")
    pv_prod, aT_ps, aT_ok, pr_ps, haa_ok = sem("b_pv_product"), sem("b_aT_in_psum"), sem("b_aT_ready"), sem("b_proj_in_psum"), sem("b_after_attn")
    lg_ps, route, gexp_ok, gate_ok, x2_out, xg_ok, xg_out = (sem("b_logits_in_psum"), sem("b_route"), sem("b_gate_exp"), sem("b_gated"),
                                                         sem("b_x2_out"), sem("b_xg_ready"), sem("b_xg_out"))
    ids_free = sem("b_ids_free")
    held = sem("b_wait_held")
    hot_ok, count_ps, place, ids_ok, slot_ok, listed = (sem("b_chosen"), sem("b_counts_in_psum"), sem("b_place"), sem("b_ids_ready"),
                                                      sem("b_slots_ready"), sem("b_listed"))
    v, gp, ac, te = nc.vector, nc.gpsimd, nc.scalar, nc.tensor
    LN = 3
    ROUTE = 9
    ident = s["ident"]
    aT = s["b_q"][:].rearrange("p b d -> p (b d)").rearrange("p (k t) -> p k t", k=KD)

    with nc.Block() as block:
        @block.sync
        def _(sp):
            prime(sp, (xg_ok, ids_free), (x2_out, xg_out))
            with sp.Fori(0, PT) as t:
                sp.wait_ge(xg_ok, ONE + t)
                for b in range(B):
                    sp.dma_start(s["b_x1"][:, b, :], x1[b, bass.ds(t * P, P), :]).then_inc(x1_in, 16)
                sp.wait_ge(xg_ok, ONE + t + 1)
                for b in range(B):
                    sp.dma_start(xg[b, bass.ds(t * P, P), :], s["b_h2"][:, b, :]).then_inc(xg_out, 16)
                for b in range(B):
                    sp.dma_start(x2n[b, bass.ds(t * P, P), :], s["b_n"][:, b, :]).then_inc(x2_out, 16)
            sp.wait_ge(xg_out, 16 + 16 * B * PT)
            sp.wait_ge(x2_out, 16 + 16 * B * PT)

        @block.gpsimd
        def _(pool):
            mh = s["minus_half"]
            with pool.Fori(0, PT) as t:
                for l in range(LN):
                    pool.wait_ge(var_ok, t * LN + l + 1)
                    gp.tensor_tensor(s["b_r"][:, l, :], s["b_var"][:], mh[:], ALU.pow).then_inc(r_ok, 1)
                    if l == 0:
                        pool.wait_ge(scaled_ok, t + 1)
                        pool.wait_ge(xg_out, 16 + t * 16 * B)
                        gp.tensor_tensor(s["b_h2"][:], s["b_n"][:], s["shift2"][:], ALU.add).then_inc(h2_ok, 1)
                pool.wait_ge(ids_ok, t + 1)
                pool.wait_ge(slot_ok, t + 1)
                for r in range(TOPK):
                    for b in range(B):
                        c = r * B + b
                        if c == 0:
                            pool.sem_inc(held, 1)
                        gp.indirect_dma_start(table, bass.IndirectOffsetOnAxis(ap=s["b_slot"][:, c:c + 1], axis=0),
                                              s["b_ids"][:, r, b, :], None).then_inc(listed, 16)
            pool.wait_ge(listed, PT * 16 * TOPK * B)

        @block.scalar
        def _(act):
            with act.Fori(0, PT) as t:
                for half in range(2):
                    for k in range(KD):
                        for c in range(2):
                            act.wait_ge(nT_ps, ((t * 2 + half) * 2 + k) * 2 + c + 1)
                            ac.activation(s["b_nT"][:, k, c * 512:(c + 1) * 512], ps[:, 2 * k + c, :], ACT.Identity,
                                          bias=s["ln_wb"][:, k, 2 * half + 1:2 * half + 2],
                                          scale=s["ln_wb"][:, k, 2 * half:2 * half + 1]).then_inc(nT_ok, 1)
                    if half == 0:
                        for b in range(B):
                            act.wait_ge(qkv_ps, t * B + b + 1)
                            bank = 4 + b % 4
                            ac.copy(s["b_q"][:, b, :], ps[:, bank, 0:QH * HD]).then_inc(q_ok, 1)
                            for kv, name in enumerate(("b_k", "b_v")):
                                src = ps[:, bank, QH * HD + kv * KVH * HD:QH * HD + (kv + 1) * KVH * HD]
                                src = src.rearrange("p (j d) -> p j d", d=HD).unsqueeze(2)
                                last = ac.copy(s[name][:, b, :].rearrange("p (j r d) -> p j r d", j=KVH, r=REP),
                                               bc(src, [P, KVH, REP, HD]))
                            last.then_inc(kv_ok, 1)
                        act.wait_ge(soft, t * 5 + 2)
                        ac.activation(s["scores_x"][:], s["scores_x"][:], ACT.Exp, scale=HD ** -0.5).then_inc(exp_ok, 1)
                        for k in range(KD):
                            for c in range(2):
                                act.wait_ge(aT_ps, (t * 2 + k) * 2 + c + 1)
                                ac.copy(aT[:, k, c * 512:(c + 1) * 512], ps[:, 2 * k + c, :]).then_inc(aT_ok, 1)
                act.wait_ge(route, t * ROUTE + 2)
                ac.activation(s["b_gate"][:], s["b_gate"][:], ACT.Exp).then_inc(gexp_ok, 1)

        @block.tensor
        def _(pe):
            with pe.Fori(0, PT) as t:
                for half in range(2):
                    pe.wait_ge(norm_ok, (t * LN + 1 + half + 1) * B)
                    for k in range(KD):
                        for c in range(2):
                            for b in range(4):
                                last = te.transpose(ps[:, 2 * k + c, b * P:(b + 1) * P], s["b_n"][:, 4 * c + b, k * P:(k + 1) * P], ident[:])
                            last.then_inc(nT_ps, 1)
                    pe.wait_ge(nT_ok, (t * 2 + half + 1) * 4)
                    if half == 0:
                        for b in range(B):
                            if b >= 4:
                                pe.wait_ge(kv_ok, t * B + b - 3)
                            for k in range(KD):
                                last = te.matmul(ps[:, 4 + b % 4, 0:QKV], s["b_nT"][:, k, b * P:(b + 1) * P], s["w_qkv2"][:, k, :],
                                                 start=(k == 0), stop=(k == KD - 1))
                            last.then_inc(qkv_ps, 1)
                        pe.wait_ge(attn_step, (t + 1) * (B - 1))
                        for k in range(KD):
                            for c in range(2):
                                for b in range(4):
                                    last = te.transpose(ps[:, 2 * k + c, b * P:(b + 1) * P], s["b_attn"][:, 4 * c + b, k * P:(k + 1) * P], ident[:])
                                last.then_inc(aT_ps, 1)
                        pe.wait_ge(aT_ok, (t + 1) * 4)
                        for b in range(B):
                            for k in range(KD):
                                last = te.matmul(ps[:, 4 + b // 2, (b % 2) * D:(b % 2 + 1) * D], aT[:, k, b * P:(b + 1) * P],
                                                 s["w_proj"][:, k, :], start=(k == 0), stop=(k == KD - 1))
                            last.then_inc(pr_ps, 1)
                for b in range(B):
                    for k in range(KD):
                        last = te.matmul(ps[:, 4, b * NEXP:(b + 1) * NEXP], s["b_nT"][:, k, b * P:(b + 1) * P], s["w_router"][:, k, :],
                                         start=(k == 0), stop=(k == KD - 1))
                last.then_inc(lg_ps, 1)
                pe.wait_ge(hot_ok, t + 1)
                te.matmul(ps[:, 5, 0:B * NEXP], s["ones"][:], s["b_chosen"][:], start=True, stop=True)
                te.matmul(ps[:, 5, B * NEXP:2 * B * NEXP], s["earlier"][:], s["b_chosen"][:], start=True, stop=True).then_inc(count_ps, 1)
                pe.wait_ge(listed, (t + 1) * (16 * TOPK * B))
                pe.sem_inc(ids_free, 1)

        @block.vector
        def _(dve):
            def layernorm(t, l, src):
                for b in range(B):
                    last = v.bn_stats(s["b_st"][:, b, :], src[:, b, :])
                last.then_inc(st_ok, 1)
                dve.wait_ge(st_ok, t * LN + l + 1)
                v.tensor_copy(s["pad"][:], s["b_st"][:, 0, 0:1])
                for b in range(B):
                    last = v.bn_aggr(s["b_mv"][:, b, :], s["b_st"][:, b, :])
                last.then_inc(ag_ok, 1)
                dve.wait_ge(ag_ok, t * LN + l + 1)
                v.tensor_scalar(s["b_var"][:], s["b_mv"][:, :, 1], 1e-5, None, ALU.add).then_inc(var_ok, 1)
                dve.wait_ge(r_ok, t * LN + l + 1)
                for b in range(B):
                    v.tensor_scalar(s["b_n"][:, b, :], src[:, b, :], s["b_mv"][:, b, 0:1], s["b_r"][:, l, b:b + 1],
                                    ALU.subtract, ALU.mult).then_inc(norm_ok, 1)

            with dve.Fori(0, PT) as t:
                dve.wait_ge(x1_in, (t + 1) * 16 * B)
                dve.wait_ge(x2_out, 16 + t * 16 * B)
                layernorm(t, 0, s["b_x1"])
                dve.wait_ge(norm_ok, (t * LN + 1) * B)
                v.tensor_tensor(s["b_n"][:], s["b_n"][:], s["scale2"][:], ALU.mult).then_inc(scaled_ok, 1)
                dve.wait_ge(h2_ok, t + 1)
                layernorm(t, 1, s["b_h2"])
                dve.wait_ge(q_ok, (t + 1) * B)
                dve.wait_ge(kv_ok, (t + 1) * B)
                for u in range(B):
                    if u >= 2:
                        dve.wait_ge(sc_ok, t * B + u - 1)
                    prod = s["b_prod"][:, u % 2, 0:B - u, :]
                    v.tensor_tensor(prod, s["b_q"][:, u:, :], bc(s["b_k"][:, u, :].unsqueeze(1), [P, B - u, D]), ALU.mult).then_inc(prod_ok, 1)
                    dve.wait_ge(prod_ok, t * B + u + 1)
                    v.tensor_reduce(s["scores"][:, u:, :, u], prod.rearrange("p a (h d) -> p a h d", d=HD), AX_X, ALU.add).then_inc(sc_ok, 1)
                flat = s["scores"][:].rearrange("p a h u -> p (a h) u")
                sx = s["scores_x"][:].rearrange("p (q u) -> p q u", u=B)
                rows = [P, B * QH, B]
                dve.wait_ge(sc_ok, (t + 1) * B)
                v.tensor_reduce(s["b_mx"][:], flat, AX_X, ALU.max).then_inc(soft, 1)
                dve.wait_ge(soft, t * 5 + 1)
                v.tensor_tensor(sx, flat, bc(s["b_mx"][:].unsqueeze(2), rows), ALU.subtract).then_inc(soft, 1)
                dve.wait_ge(exp_ok, t + 1)
                v.tensor_reduce(s["b_mx"][:], sx, AX_X, ALU.add).then_inc(soft, 1)
                dve.wait_ge(soft, t * 5 + 3)
                v.reciprocal(s["b_den"][:], s["b_mx"][:]).then_inc(soft, 1)
                dve.wait_ge(soft, t * 5 + 4)
                v.tensor_tensor(sx, sx, bc(s["b_den"][:].unsqueeze(2), rows), ALU.mult).then_inc(soft, 1)
                dve.wait_ge(soft, t * 5 + 5)
                probs = s["scores_x"][:].rearrange("p (a h u) -> p a h u", a=B, h=QH)
                for u in range(B):
                    dst = s["b_attn"][:] if u == 0 else s["b_prod"][:, u % 2, 0:B - u, :]
                    if u >= 3:
                        dve.wait_ge(attn_step, t * (B - 1) + u - 2)
                    for a in range(u, B):
                        last = v.tensor_tensor(dst[:, a - u, :].rearrange("p (h d) -> p h d", d=HD),
                                               s["b_v"][:, u, :].rearrange("p (h d) -> p h d", d=HD),
                                               bc(probs[:, a, :, u].unsqueeze(2), [P, QH, HD]), ALU.mult)
                    last.then_inc(pv_prod, 1)
                    dve.wait_ge(pv_prod, t * B + u + 1)
                    if u:
                        v.tensor_tensor(s["b_attn"][:, u:, :], s["b_attn"][:, u:, :], dst, ALU.add).then_inc(attn_step, 1)
                for b in range(B):
                    dve.wait_ge(pr_ps, t * B + (b // 2) * 2 + 2)
                    last = v.tensor_tensor(s["b_h2"][:, b, :], ps[:, 4 + b // 2, (b % 2) * D:(b % 2 + 1) * D], s["b_h2"][:, b, :], ALU.add)
                last.then_inc(haa_ok, 1)
                dve.wait_ge(haa_ok, t + 1)
                layernorm(t, 2, s["b_h2"])
                dve.wait_ge(norm_ok, (t + 1) * LN * B)
                v.tensor_tensor(s["b_h2"][:], s["b_h2"][:], s["gate2"][:], ALU.mult).then_inc(gate_ok, 1)
                dve.wait_ge(gate_ok, t + 1)
                v.tensor_tensor(s["b_h2"][:], s["b_h2"][:], s["b_x1"][:], ALU.add).then_inc(xg_ok, 1)
                dve.wait_ge(lg_ps, t + 1)
                routed = lambda c: dve.wait_ge(route, t * ROUTE + c)
                lg = ps[:, 4, 0:B * NEXP].rearrange("p (b e) -> p b e", e=NEXP)
                wide = [P, B, NEXP]
                v.tensor_reduce(s["b_gm"][:], lg, AX_X, ALU.max).then_inc(route, 1)
                routed(1)
                v.tensor_tensor(s["b_gate"][:], lg, bc(s["b_gm"][:].unsqueeze(2), wide), ALU.subtract).then_inc(route, 1)
                dve.wait_ge(gexp_ok, t + 1)
                v.tensor_reduce(s["b_gs"][:], s["b_gate"][:], AX_X, ALU.add).then_inc(route, 1)
                routed(3)
                v.reciprocal(s["b_gm"][:], s["b_gs"][:]).then_inc(route, 1)
                routed(4)
                v.tensor_tensor(s["b_gate"][:], s["b_gate"][:], bc(s["b_gm"][:].unsqueeze(2), wide), ALU.mult).then_inc(route, 1)
                routed(5)
                v.tensor_copy(s["pad"][:], s["b_gate"][:, 0, 0:1])
                for b in range(B):
                    last = v.max(s["b_top"][:, b, :], s["b_gate"][:, b, :])
                last.then_inc(route, 1)
                routed(6)
                v.tensor_copy(s["pad"][:], s["b_top"][:, 0, 0:1])
                for b in range(B):
                    last = v.max_index(s["b_idx"][:, b, :], s["b_top"][:, b, :], s["b_gate"][:, b, :])
                last.then_inc(route, 1)
                routed(7)
                v.tensor_copy(s["b_idf"][:], s["b_idx"][:, :, 0:2]).then_inc(route, 1)
                routed(8)
                iota = bc(s["iota8"][:].unsqueeze(1), wide)
                for r in range(2):
                    last = v.tensor_tensor(s["b_hot"][:, r], iota, bc(s["b_idf"][:, :, r:r + 1], wide), ALU.is_equal)
                last.then_inc(route, 1)
                routed(ROUTE)
                v.tensor_tensor(s["b_chosen"][:].rearrange("p (b e) -> p b e", e=NEXP), s["b_hot"][:, 0], s["b_hot"][:, 1], ALU.add).then_inc(hot_ok, 1)
                v.tensor_copy(s["wts"][:, bass.ds(t * B, B), :], s["b_top"][:, :, 0:TOPK])
                dve.wait_ge(ids_free, ONE + t)
                v.tensor_copy(s["b_ids"][:], s["b_ids_f"][:]).then_inc(ids_ok, 1)
                v.tensor_scalar(s["b_ids_f"][:], s["b_ids_f"][:], float(P), None, ALU.add)
                placed = lambda c: dve.wait_ge(place, t * 5 + c)
                dve.wait_ge(count_ps, t + 1)
                total = ps[:, 5, 0:B * NEXP].rearrange("p (b e) -> p e b", e=NEXP)
                before = ps[:, 5, B * NEXP:2 * B * NEXP].rearrange("p (b e) -> p b e", e=NEXP)
                v.tensor_copy(s["b_scan_in"][:, :, 0], s["next_slot"][:])
                v.tensor_copy(s["b_scan_in"][:, :, 1:], total[:, :, 0:B - 1]).then_inc(place, 1)
                placed(1)
                v.tensor_tensor_scan(s["b_scan"][:].rearrange("p e b -> p (e b)"), s["scan_reset"][:],
                                     s["b_scan_in"][:].rearrange("p e b -> p (e b)"), 0.0, ALU.mult, ALU.add).then_inc(place, 1)
                placed(2)
                v.tensor_tensor(s["next_slot"][:], s["b_scan"][:, :, B - 1], total[:, :, B - 1], ALU.add)
                v.tensor_tensor(s["b_pos"][:], before, s["b_scan"][:].rearrange("p e b -> p b e"), ALU.add).then_inc(place, 1)
                placed(3)
                v.tensor_tensor(s["b_hot"][:], s["b_hot"][:], bc(s["b_pos"][:].unsqueeze(1), [P, TOPK, B, NEXP]), ALU.mult).then_inc(place, 1)
                placed(4)
                v.tensor_reduce(s["b_slot_f"][:], s["b_hot"][:].rearrange("p r b e -> p (r b) e"), AX_X, ALU.add).then_inc(place, 1)
                placed(5)
                v.tensor_copy(s["b_slot"][:], s["b_slot_f"][:]).then_inc(slot_ok, 1)


def plan_tiles(nc, ctx, s):
    sem = lambda name: ctx.enter_context(nc.semaphore(name))
    planned = sem("planned")
    v = nc.vector
    with nc.Block() as block:
        @block.vector
        def _(dve):
            steps = [0]

            def link(ins):
                steps[0] += 1
                ins.then_inc(planned, 1)
                dve.wait_ge(planned, steps[0])

            most = TOK // P
            link(v.tensor_tensor(s["p_count"][:], s["next_slot"][:], s["region"][:], ALU.subtract))
            link(v.tensor_tensor(s["p_under"][:], bc(s["p_count"][:].unsqueeze(2), [P, NEXP, most]),
                                 bc(s["slot_steps"][:, 0:most].unsqueeze(1), [P, NEXP, most]), ALU.is_gt))
            link(v.tensor_reduce(s["p_tiles"][:], s["p_under"][:], AX_X, ALU.add))
            link(v.tensor_tensor_scan(s["p_until"][:], s["ones"][:, 0:NEXP], s["p_tiles"][:], 0.0, ALU.mult, ALU.add))
            past = [P, TILES, NEXP - 1]
            link(v.tensor_scalar(s["p_tile"][:], s["slot_steps"][:], 1.0 / P, None, ALU.mult))
            link(v.tensor_tensor(s["p_past"][:], bc(s["p_tile"][:].unsqueeze(2), past),
                                 bc(s["p_until"][:, 0:NEXP - 1].unsqueeze(1), past), ALU.is_ge))
            link(v.tensor_reduce(s["p_expert"][:], s["p_past"][:], AX_X, ALU.add))
            link(v.tensor_tensor(s["p_past"][:], s["p_past"][:], bc(s["p_tiles"][:, 0:NEXP - 1].unsqueeze(1), past), ALU.mult))
            link(v.tensor_reduce(s["p_first"][:], s["p_past"][:], AX_X, ALU.add))
            link(v.tensor_tensor(s["p_first"][:], s["p_tile"][:], s["p_first"][:], ALU.subtract))
            link(v.tensor_scalar(s["p_first"][:], s["p_first"][:], float(P), None, ALU.mult))
            link(v.tensor_copy(s["tile_expert"][:], s["p_expert"][:]))
            link(v.tensor_scalar(s["p_expert"][:], s["p_expert"][:], float(REGION), None, ALU.mult))
            link(v.tensor_tensor(s["p_first"][:], s["p_first"][:], s["p_expert"][:], ALU.add))
            link(v.tensor_copy(s["tile_slot"][:], s["p_first"][:]))


def over_tiles(eng, body):
    for i in range(DEEP):
        body(i, i)
    with eng.Fori(1, TILES // DEEP - 1) as j:
        for r in range(DEEP):
            body(j * DEEP + r, r)
    for i in range(TILES - DEEP, TILES):
        body(i, i % DEEP)


def exists(i):
    return not isinstance(i, int) or i < TILES


def pass_three(nc, ctx, x2n, table, y_rows, weights_in, s, ps):
    sem = lambda name: ctx.enter_context(nc.semaphore(name))
    ids_in, turn_loaded, ids_ok, x_in = sem("c_ids_in"), sem("c_turn_loaded"), sem("c_ids_ready"), [sem(f"c_x_in_{r}") for r in range(XDEEP)]
    loads = lambda i, r: (i - r % XDEEP) * (16 // XDEEP) + 16
    AHEAD = 5
    xT_ps, xT_ok, up_ps, gelu_ok, hT_ps, hT_ok, y_ps, y_ok, y_out = (
        sem("c_xT_in_psum"), sem("c_xT_ready"), sem("c_up_in_psum"), sem("c_gelu"),
        sem("c_hT_in_psum"), sem("c_hT_ready"), sem("c_y_in_psum"), sem("c_y_ready"), sem("c_y_out"))
    v, gp, ac, te = nc.vector, nc.gpsimd, nc.scalar, nc.tensor
    held = sem("c_wait_held")
    ident = s["ident"]
    X_BANK = 0
    UP_BANK, HT_BANK, Y_BANK = (1, 2), (3, 4), (5, 6)
    w_up = s["w_up"][:].rearrange("p e k f -> p (e k f)")
    w_down = s["w_down"][:].rearrange("p e f d -> p (e f d)")

    with nc.Block() as block:
        @block.sync
        def _(sp):
            with sp.Fori(0, TILES // DEEP) as j:
                for r in range(DEEP):
                    i = j * DEEP + r
                    first = sp.value_load(s["tile_slot"][0:1, bass.ds(i, 1)], min_val=0, max_val=SLOTS - P)
                    sp.dma_start(s["c_all_ids"][:, bass.ds(i, 1), :], table[bass.ds(first, P), :].unsqueeze(1)).then_inc(ids_in, 16)
                sp.wait_ge(ids_in, (j + 1) * (16 * DEEP))
                sp.sem_inc(turn_loaded, 1)

        @block.gpsimd
        def _(pool):
            def gather(i, r):
                pool.wait_ge(ids_ok, i + 1)
                once_positive(pool, xT_ps, i - XDEEP + 1)
                pool.sem_inc(held, 1)
                gp.indirect_dma_start(s["c_x"][:, r % XDEEP, :], None, x2n, bass.IndirectOffsetOnAxis(ap=s["c_ids"][:, r, 0:1], axis=0)).then_inc(x_in[r % XDEEP], 16)

            def step(i, r):
                if exists(i + 3):
                    gather(i + 3, (r + 3) % DEEP)
                pool.wait_ge(y_ok, i + 1)
                once_positive(pool, y_out, i * 16)
                pool.sem_inc(held, 1)
                gp.indirect_dma_start(y_rows, bass.IndirectOffsetOnAxis(ap=s["c_ids"][:, r, 1:2], axis=0), s["c_y"][:, r % XDEEP, :], None).then_inc(y_out, 16)

            gather(0, 0)
            gather(1, 1)
            gather(2, 2)
            over_tiles(pool, step)
            pool.wait_ge(y_out, TILES * 16)

        @block.scalar
        def _(act):
            def turned(i, r):
                act.wait_ge(xT_ps, i + 1)
                once_positive(act, up_ps, i - 1)
                for k in range(KD):
                    last = ac.activation(s["c_xT"][:, r % 2, k, :], ps[:, X_BANK, k * P:(k + 1) * P], ACT.Identity,
                                         bias=s["ln_wb"][:, k, 3:4], scale=s["ln_wb"][:, k, 2:3])
                last.then_inc(xT_ok, 1)

            def gelu(i, r):
                act.wait_ge(up_ps, i + 1)
                once_positive(act, hT_ps, i - 1)
                ac.activation(s["c_h"][:, r % 2, :], ps[:, UP_BANK[r % 2], :], ACT.Gelu_apprx_tanh).then_inc(gelu_ok, 1)

            def step(i, r):
                if exists(i + 1):
                    gelu(i + 1, r + 1)
                if exists(i + 2):
                    turned(i + 2, r)

            turned(0, 0)
            gelu(0, 0)
            turned(1, 1)
            over_tiles(act, step)

        @block.tensor
        def _(pe):
            def turn_x(i, r):
                pe.wait_ge(x_in[r % XDEEP], loads(i, r))
                once_positive(pe, xT_ok, i)
                for k in range(KD):
                    last = te.transpose(ps[:, X_BANK, k * P:(k + 1) * P], s["c_x"][:, r % XDEEP, k * P:(k + 1) * P], ident[:])
                last.then_inc(xT_ps, 1)

            def up(i, r):
                expert = pe.value_load(s["tile_expert"][0:1, bass.ds(i, 1)], min_val=0, max_val=NEXP - 1)
                pe.wait_ge(xT_ok, i + 1)
                once_positive(pe, gelu_ok, i - 1)
                for k in range(KD):
                    last = te.matmul(ps[:, UP_BANK[r % 2], :], s["c_xT"][:, r % 2, k, :], w_up[:, bass.ds(expert * (KD * FF) + k * FF, FF)],
                                     start=(k == 0), stop=(k == KD - 1))
                last.then_inc(up_ps, 1)

            def turn_h(i, r):
                pe.wait_ge(gelu_ok, i + 1)
                once_positive(pe, hT_ok, i - 1)
                for f in range(FT):
                    last = te.transpose(ps[:, HT_BANK[r % 2], f * P:(f + 1) * P], s["c_h"][:, r % 2, f * P:(f + 1) * P], ident[:])
                last.then_inc(hT_ps, 1)

            def down(i, r):
                expert = pe.value_load(s["tile_expert"][0:1, bass.ds(i, 1)], min_val=0, max_val=NEXP - 1)
                pe.wait_ge(hT_ok, i + 1)
                once_positive(pe, y_ok, i - 1)
                for f in range(FT):
                    last = te.matmul(ps[:, Y_BANK[r % 2], 0:D], s["c_hT"][:, r % 2, f, :], w_down[:, bass.ds(expert * (FT * D) + f * D, D)],
                                     start=(f == 0), stop=(f == FT - 1))
                last.then_inc(y_ps, 1)

            def step(i, r):
                turn_h(i, r)
                if exists(i + 1):
                    up(i + 1, r + 1)
                if exists(i + 2):
                    turn_x(i + 2, (r + 2) % DEEP)
                down(i, r)

            pe.wait_ge(weights_in, 16 * 2)
            turn_x(0, 0)
            up(0, 0)
            turn_x(1, 1)
            over_tiles(pe, step)

        @block.vector
        def _(dve):
            def step(i, r):
                dve.wait_ge(hT_ps, i + 1)
                once_positive(dve, y_ps, i - 1)
                v.tensor_copy(s["c_hT"][:, r % 2].rearrange("p f t -> p (f t)"), ps[:, HT_BANK[r % 2], :]).then_inc(hT_ok, 1)
                dve.wait_ge(y_ps, i + 1)
                once_positive(dve, y_out, (i - XDEEP + 1) * 16)
                v.tensor_copy(s["c_y"][:, r % XDEEP, :], ps[:, Y_BANK[r % 2], 0:D]).then_inc(y_ok, 1)
                if exists(i + AHEAD):
                    hand_out(i + AHEAD, (r + AHEAD) % DEEP)

            def hand_out(i, r):
                if r == 0:
                    dve.wait_ge(ids_in, (i + DEEP) * 16)
                once_positive(dve, y_out, (i - DEEP + 1) * 16)
                v.tensor_copy(s["c_ids"][:, r, :], s["c_all_ids"][:, bass.ds(i, 1), :].rearrange("p i c -> p (i c)")).then_inc(ids_ok, 1)

            for i in range(AHEAD):
                hand_out(i, i)
            over_tiles(dve, step)


def pass_four(nc, ctx, xg, y_rows, out, s):
    sem = lambda name: ctx.enter_context(nc.semaphore(name))
    by_parity = lambda name: [sem(name + "_even"), sem(name + "_odd")]
    y_in, xg_in, stored = by_parity("d_y_in"), by_parity("d_xg_in"), by_parity("d_stored")
    first_ok, weights_ok, both_ok, gated, out_ok = sem("d_first"), sem("d_weights"), sem("d_both"), sem("d_gated"), sem("d_out_ready")
    v, gp, ac = nc.vector, nc.gpsimd, nc.scalar

    y_of, xg_of, out_of = y_rows[0:TOPK * TOK].rearrange("(n l) d -> l n d", l=L), xg.rearrange("b l d -> l b d"), out.rearrange("b l d -> l b d")

    with nc.Block() as block:
        @block.sync
        def _(sp):
            def load(t, r):
                sp.dma_start(s["d_y"][:, r], y_of[bass.ds(t * P, P)]).then_inc(y_in[r], 16)
                sp.dma_start(s["d_xg"][:, r], xg_of[bass.ds(t * P, P)]).then_inc(xg_in[r], 16)

            def store(t, r):
                sp.wait_ge(out_ok, t + 1)
                sp.dma_start(out_of[bass.ds(t * P, P)], s["d_xg"][:, r]).then_inc(stored[r], 16)

            for t in range(2):
                load(t, t)
            with sp.Fori(0, PT // 2 - 1) as j:
                for r in range(2):
                    store(j * 2 + r, r)
                    sp.wait_ge(stored[r], (j + 1) * 16)
                    load(j * 2 + 2 + r, r)
            for t in (PT - 2, PT - 1):
                store(t, t % 2)
            for r in range(2):
                sp.wait_ge(stored[r], PT // 2 * 16)

        @block.scalar
        def _(act):
            with act.Fori(0, PT // 2) as j:
                for r in range(2):
                    t = j * 2 + r
                    act.wait_ge(y_in[r], (j + 1) * 16)
                    act.wait_ge(weights_ok, t + 1)
                    for b in range(B):
                        last = ac.activation(s["d_y"][:, r, b, :], s["d_y"][:, r, b, :], ACT.Identity, scale=s["d_w"][:, r, b, 0:1])
                    last.then_inc(first_ok, 1)

        @block.vector
        def _(dve):
            with dve.Fori(0, PT // 2) as j:
                for r in range(2):
                    t = j * 2 + r
                    v.tensor_copy(s["d_w"][:, r], s["wts"][:, bass.ds(t * B, B), :]).then_inc(weights_ok, 1)
                    dve.wait_ge(weights_ok, t + 1)
                    dve.wait_ge(first_ok, t + 1)
                    for b in range(B):
                        last = v.scalar_tensor_tensor(s["d_y"][:, r, b, :], s["d_y"][:, r, B + b, :], s["d_w"][:, r, b, 1:2],
                                                      s["d_y"][:, r, b, :], ALU.mult, ALU.add)
                    last.then_inc(both_ok, 1)
                    dve.wait_ge(both_ok, t + 1)
                    v.tensor_tensor(s["d_y"][:, r, 0:B, :], s["d_y"][:, r, 0:B, :], s["gate2"][:], ALU.mult).then_inc(gated, 1)

        @block.gpsimd
        def _(pool):
            with pool.Fori(0, PT // 2) as j:
                for r in range(2):
                    t = j * 2 + r
                    pool.wait_ge(gated, t + 1)
                    pool.wait_ge(xg_in[r], (j + 1) * 16)
                    gp.tensor_tensor(s["d_xg"][:, r], s["d_xg"][:, r], s["d_y"][:, r, 0:B, :], ALU.add).then_inc(out_ok, 1)


SHAPES = {
    "quad_mask": [P, QB],    "eye32": [P, C], "levels": [P, LEVELS, C], "chunk_mask": [P, 2, P],
    "w_qkv": [P, KD, 3 * D], "w_beta_mix": [P, KD, P], "w_decay": [P, KD, D], "w_out": [P, KD, D],
    "conv_w": [P, M, TAPS], "onorm": [P, 1], "small_bias": [P, 2 * NH], "cT": [P, KD, B], "wmod": [P, KD, 6 * D],
}
SHARED = dict(ident=[P, P], iota8=[P, NEXP], pad=[P, 1], wts=[P, PT * B, TOPK], minus_half=[P, 8], mod=[B, 6 * D], shift1=[P, G, D], scale1=[P, G, D], gate1=[P, G, D])
SHARED2 = dict(
    next_slot=[P, NEXP], region=[P, NEXP], slot_steps=[P, TILES], ones=[P, P], ln_wb=[P, KD, 4], w_up=[P, NEXP, KD, FF], w_down=[P, NEXP, FT, D],
    shift2=[P, B, D], scale2=[P, B, D], gate2=[P, B, D])
PASS2 = dict(
    sel_all=[B, B, P],
    w_qkv2=[P, KD, QKV], w_proj=[P, KD, D], w_router=[P, KD, NEXP],
    b_x1=[P, B, D], b_n=[P, B, D], b_h2=[P, B, D], b_nT=[P, KD, B * P], b_st=[P, B, 6], b_mv=[P, B, 2], b_var=[P, B], b_r=[P, 3, B],
    b_q=[P, B, D], b_k=[P, B, D], b_v=[P, B, D], b_prod=[P, 2, B, D], scores=[P, B, QH, B], scores_x=[P, B * QH * B],
    b_mx=[P, B * QH], b_den=[P, B * QH], b_attn=[P, B, D],
    b_gate=[P, B, NEXP], b_gm=[P, B], b_gs=[P, B], b_top=[P, B, 8], b_idf=[P, B, 2], b_hot=[P, TOPK, B, NEXP],
    b_chosen=[P, B * NEXP], earlier=[P, P], b_ids_f=[P, TOPK, B, 2], b_scan_in=[P, NEXP, B], b_scan=[P, NEXP, B], scan_reset=[P, NEXP * B],
    b_pos=[P, B, NEXP], b_slot_f=[P, TOPK * B])
PLAN = dict(p_count=[P, NEXP], p_under=[P, NEXP, TOK // P], p_tiles=[P, NEXP], p_until=[P, NEXP], p_tile=[P, TILES],
            p_past=[P, TILES, NEXP - 1], p_expert=[P, TILES], p_first=[P, TILES])
PASS3 = dict(c_x=[P, XDEEP, D], c_xT=[P, 2, KD, P], c_h=[P, 2, FF], c_hT=[P, 2, FT, P], c_y=[P, XDEEP, D])
PASS4 = dict(d_y=[P, 2, TOPK * B, D], d_xg=[P, 2, B, D], d_w=[P, 2, B, TOPK])
INTEGERS = dict(tile_expert=[P, TILES], tile_slot=[P, TILES])
SETUP = dict(scT=[P, KD, B], gate_sign=[B, D], sel_quad=[B, G, P])
PASS1 = dict(
    state=[P, B, PAIRS, P], x_in=[P, 2, G, D], x_res=[P, G, D], x1_rows=[P, G, D], y=[P, G, D], ln_st=[P, G, 6], ln_mv=[P, G, 2],
    ln_v=[P, G], ln_r=[P, G], h=[P, G, D], hT=[P, KD, COLS], conv_in=[P, M, B, C + TAPS - 1], conv_acc=[P, M, COLS],
    qkvT=[P, 2, M, COLS], th_decay=[P, PAIRS * COLS], gam=[P, PAIRS * COLS], omg=[P, PAIRS * COLS], ema_hist=[P, PAIRS * B],
    ema_out=[P, 2, PAIRS, COLS], small=[P, G, 2 * NH], th_small=[P, 2, G, 2 * NH], bm=[P, G, 2 * NH], omm=[P, 2, G, NH],
    sq=[P, G, 2 * D], ss=[P, G, 2 * NH], rqk=[P, G, 2 * NH], ema_rows=[P, G, D], mix_e=[P, 2, G, D], mix_d=[P, G, D],
    qkn=[P, G, 2, D], kb=[P, 2, G, D], vb=[P, 2, G, D], k_bd=[P, 2, G, QB, D], knT=[P, G, 2, PAIRS, P], kqT=[P, 2, G, PAIRS, 2, P],
    LA=[P, 2, G, NH, 2, P], Y=[P, G, NH, C], Y0=[P, G, NH, C], T=[P, G, NH, C], TTbd=[P, 2, G, NH, P], u=[P, G, D],
    wT=[P, G, PAIRS, P], un=[P, G, D], o=[P, G, D], osq=[P, G, D], oss=[P, G, NH], orr=[P, G, NH], on=[P, G, D], onT=[P, G, KD, P])


def program(nc, d, x, out):
    x1 = nc.dram_tensor("x1_rows_dram", (B, L, D), F32, kind="Internal").ap()
    xg = nc.dram_tensor("xg_rows_dram", (B, L, D), F32, kind="Internal").ap()
    x2n = nc.dram_tensor("x2n_dram", (TOK, D), F32, kind="Internal").ap()
    y_rows = nc.dram_tensor("y_rows_dram", (TOPK * TOK + P, D), F32, kind="Internal").ap()
    table = nc.dram_tensor("table_dram", (SLOTS, 2), U32, kind="Internal").ap()
    with ExitStack() as ctx:
        ps = ctx.enter_context(nc.psum_tensor("ps", [P, 8, 512], F32))
        zeroed = ctx.enter_context(nc.semaphore("zeroed"))
        s = {k: ctx.enter_context(nc.sbuf_tensor(k, v, F32)) for k, v in SHARED.items()}
        with ExitStack() as c1:
            s |= {k: c1.enter_context(nc.sbuf_tensor(k, v, F32)) for k, v in {**SHAPES, **SETUP, **PASS1, }.items()}
            mod_b = [s[name][:, g, :] for name in ("scale1", "shift1", "gate1") for g in range(G)]
            setup_constants(nc, ctx, d, s, ps, mod_b, zeroed)
            pass_one(nc, ctx, x, x1, s, ps)
        s |= {k: ctx.enter_context(nc.sbuf_tensor(k, v, F32)) for k, v in SHARED2.items()}
        s |= {k: ctx.enter_context(nc.sbuf_tensor(k, v, U32)) for k, v in INTEGERS.items()}
        weights_in = ctx.enter_context(nc.semaphore("c_weights_in"))
        with ExitStack() as c2:
            s |= {k: c2.enter_context(nc.sbuf_tensor(k, v, F32)) for k, v in PASS2.items()}
            s["b_idx"] = c2.enter_context(nc.sbuf_tensor("b_idx", [P, B, 8], U32))
            s["b_ids"] = c2.enter_context(nc.sbuf_tensor("b_ids", [P, TOPK, B, 2], U32))
            s["b_slot"] = c2.enter_context(nc.sbuf_tensor("b_slot", [P, TOPK * B], U32))
            setup_two(nc, ctx, d, s, ps, table, weights_in)
            pass_two(nc, ctx, x1, xg, x2n.rearrange("(b l) d -> b l d", b=B), table, s, ps)
        with ExitStack() as c3:
            s |= {k: c3.enter_context(nc.sbuf_tensor(k, v, F32)) for k, v in PLAN.items()}
            plan_tiles(nc, ctx, s)
        with ExitStack() as c4:
            s |= {k: c4.enter_context(nc.sbuf_tensor(k, v, F32)) for k, v in PASS3.items()}
            s["c_all_ids"] = c4.enter_context(nc.sbuf_tensor("c_all_ids", [P, TILES, 2], U32))
            s["c_ids"] = c4.enter_context(nc.sbuf_tensor("c_ids", [P, DEEP, 2], U32))
            pass_three(nc, ctx, x2n, table, y_rows, weights_in, s, ps)
        with ExitStack() as c5:
            s |= {k: c5.enter_context(nc.sbuf_tensor(k, v, F32)) for k, v in PASS4.items()}
            pass_four(nc, ctx, xg, y_rows, out, s)
    return x1


def constants():
    p = np.arange(P)
    same = (p[:, None] // C) == (p[None, :] // C)
    row, col = (p % C)[:, None], np.arange(C)[None, :]
    levels = np.stack([((row >> k) & 1 == 1) & ((col >> k) == (row >> k) - 1) for k in range(LEVELS)], 1)
    mask = np.stack([same & (p[None, :] > p[:, None]), same & (p[None, :] >= p[:, None])], 1)
    f = np.float32
    slot, token = np.arange(SLOTS), np.arange(B)[None, None, :] * L + p[:, None, None]
    region = np.tile(np.arange(NEXP, dtype=f) * REGION, (P, 1))
    number = np.stack([np.broadcast_to(token, (P, TOPK, B)), token + np.arange(TOPK)[None, :, None] * TOK], 3)
    return {
            "empty_slots": np.stack([slot % P, TOPK * TOK + slot % P], 1).astype(np.uint32),
            "region": region, "next_slot": region.copy(), "slot_steps": np.tile(np.arange(TILES, dtype=f) * P, (P, 1)),
            "earlier": (p[:, None] < p[None, :]).astype(f), "b_ids_f": np.ascontiguousarray(number.astype(f)),
            "scan_reset": np.tile((np.arange(NEXP * B) % B > 0).astype(f), (P, 1)),
            "ident": np.eye(P, dtype=f), "eye32": np.tile(np.eye(C, dtype=f), (P // C, 1)), "levels": levels.astype(f),
            "chunk_mask": mask.astype(f),
            "quad_mask": (p[:, None] // C == np.arange(QB)[None, :]).astype(f), "iota8": np.tile(np.arange(NEXP, dtype=f), (P, 1))}


def tiles(a):
    a = np.asarray(a)
    return np.ascontiguousarray(a.reshape(-1, P, *a.shape[1:]).swapaxes(0, 1))


def lay_out(i):
    a = {k: np.asarray(v) for k, v in i.items()}
    d = constants()
    d["w_qkv"] = tiles(np.concatenate([a["L0_attn_Wq"], a["L0_attn_Wk"], a["L0_attn_Wv"]], 0).T)
    pad = np.zeros((P - 2 * NH, D), np.float32)
    d["w_beta_mix"] = tiles(np.concatenate([a["L0_attn_Wb"], a["L0_attn_Wmix"], pad], 0).T)
    d["w_decay"] = tiles(np.repeat(a["L0_attn_Wdec"], DH, axis=0).T)
    d["w_out"] = tiles(a["L0_attn_Wo"].T)
    d["conv_w"] = tiles(np.concatenate([a["L0_attn_wq_conv"], a["L0_attn_wk_conv"], a["L0_attn_wv_conv"]], 0))
    d["onorm"] = np.ascontiguousarray(np.tile(a["L0_attn_onorm_w"], P // DH)[:, None])
    d["small_bias"] = np.ascontiguousarray(np.tile(np.concatenate([np.zeros(NH, np.float32), a["L0_attn_mix_bias"]])[None], (P, 1)))
    d["w_qkv2"] = tiles(a["L0_ffn_qkv_weight"].T)
    d["w_proj"] = tiles(a["L0_ffn_proj_weight"].T)
    d["w_router"] = tiles(a["L0_ffn_router_weight"].T)
    d["ln_wb"] = tiles(np.stack([a["L0_ffn_ln1_weight"], a["L0_ffn_ln1_bias"], a["L0_ffn_ln2_weight"], a["L0_ffn_ln2_bias"]], 1))
    d["w_up"] = np.ascontiguousarray(a["L0_ffn_moe_w1"].reshape(NEXP, KD, P, FF).transpose(2, 0, 1, 3))
    d["w_down"] = np.ascontiguousarray(a["L0_ffn_moe_w2"].reshape(NEXP, FT, P, D).transpose(2, 0, 1, 3))
    d["cT"] = tiles(a["L0_c"].T)
    d["wmod"] = tiles(a["L0_wmod"])
    return d, np.ascontiguousarray(a["L0_attn_hidden_states"])


def kernel(**inputs):
    import concourse.bacc as bacc
    from concourse.bass_utils import run_bass_kernel_spmd

    nc = bacc.Bacc("TRN2", target_bir_lowering=False, num_devices=1)
    d, x = lay_out(inputs)
    arrays = {f"{name}_dram": a for name, a in d.items()} | {"x_dram": x}
    aps = {name: nc.dram_tensor(f"{name}_dram", a.shape, mybir.dt.from_np(a.dtype), kind="ExternalInput").ap() for name, a in d.items()}
    x_ap = nc.dram_tensor("x_dram", x.shape, F32, kind="ExternalInput").ap()
    out = nc.dram_tensor("out_0_dram", (B, L, D), F32, kind="ExternalOutput").ap()
    program(nc, aps, x_ap, out)
    r = run_bass_kernel_spmd(nc, [arrays], core_ids=[0])
    return r.results[0]["out_0_dram"]
```

```python
from contextlib import ExitStack

import numpy as np
import concourse.bass as bass
from concourse import mybir

ALU = mybir.AluOpType
ACT = mybir.ActivationFunctionType
F32 = mybir.dt.float32
U32 = mybir.dt.uint32
AX_X = mybir.AxisListType.X

P = 128
B, L, D = 8, 1024, 256
KD = D // P
C = 32
STEPS = L // C
G = 2
QB = B // G
NH, DH = 4, 64
PAIRS = NH // 2
TAPS = 4
M = 3 * KD
LEVELS = 5
COLS = B * C
NEXP, FF = 8, 512
FT = FF // P
QH, KVH, HD = 16, 4, 16
REP = QH // KVH
QKV = (QH + 2 * KVH) * HD
PT = L // P
TOK = B * L
TOPK = 2
REGION = TOK
TILES = (TOPK * TOK) // P + NEXP
SLOTS = (NEXP - 1) * REGION + TILES * P
DEEP = 8
XDEEP = 4
FMIN = float(np.finfo(np.float32).min)


def bc(ap, shape):
    return ap.broadcast_to(shape)


ONE = 1


def prime(eng, semaphores, dma_semaphores):
    for x in semaphores:
        eng.sem_inc(x, 1)
    for x in dma_semaphores:
        eng.sem_inc(x, 16)


def setup_constants(nc, ctx, dram, sbuf, psum, mod_rows, zeroed):
    d, s = dram, sbuf
    sem = lambda name: ctx.enter_context(nc.semaphore(name))
    loaded, half_set, gates_in = sem("loaded"), sem("half_set"), sem("gates_in")
    sc_ready, mod_in_psum, mod_ready = sem("sc_ready"), sem("mod_in_psum"), sem("mod_ready")
    rows_stored, rows_in = sem("rows_stored"), sem("rows_in")
    gate_step = sem("gate_step")
    mod = s["mod"][:]
    names = ["ident", "quad_mask", "eye32", "levels", "chunk_mask", "w_qkv", "w_beta_mix", "w_decay", "w_out", "conv_w",
             "onorm", "small_bias", "cT", "wmod", "iota8"]

    with nc.Block() as block:
        @block.sync
        def _(sp):
            for name in names:
                sp.dma_start(s[name][:], d[name]).then_inc(loaded, 16)
            sp.wait_ge(gates_in, 1)
            sp.dma_start(mod_rows, mod).then_inc(rows_stored, 16)
            sp.wait_ge(rows_stored, 16)
            for name, which in (("shift1", 0), ("scale1", 1), ("gate1", 2)):
                for g in range(G):
                    rows = mod_rows[g * QB:(g + 1) * QB, which * D:(which + 1) * D].unsqueeze(1)
                    sp.dma_start(s[name][:, g, :], bc(rows, [QB, C, D])).then_inc(rows_in, 16)
            sp.wait_ge(rows_in, 3 * G * 16)

        @block.scalar
        def _(act):
            act.wait_ge(loaded, 16 * len(names))
            nc.scalar.activation(s["scT"][:], s["cT"][:], ACT.Silu).then_inc(sc_ready, 1)
            act.wait_ge(mod_in_psum, 1)
            nc.scalar.copy(mod, psum[0:B, 0:3, :]).then_inc(mod_ready, 1)

        @block.tensor
        def _(pe):
            pe.wait_ge(sc_ready, 1)
            for c in range(3):
                for k in range(KD):
                    last = nc.tensor.matmul(psum[0:B, c, :], s["scT"][:, k, :],
                                            s["wmod"][:, k, c * 512:(c + 1) * 512], start=(k == 0), stop=(k == KD - 1))
            last.then_inc(mod_in_psum, 1)

        @block.vector
        def _(dve):
            steps = [0]

            def link(ins):
                steps[0] += 1
                ins.then_inc(gate_step, 1)
                dve.wait_ge(gate_step, steps[0])

            dve.wait_ge(loaded, 16 * len(names))
            for k in range(KD):
                nc.vector.tensor_scalar(s["w_out"][:, k, :], s["w_out"][:, k, :], s["onorm"][:, 0:1], None, ALU.mult)
            dve.wait_ge(mod_ready, 1)
            for which in (2, 5):
                gate = mod[:, which * D:(which + 1) * D]
                link(nc.vector.tensor_scalar(s["gate_sign"][:], gate, 0.0, 2.0, ALU.is_ge, ALU.mult))
                link(nc.vector.tensor_scalar(s["gate_sign"][:], s["gate_sign"][:], -1.0, None, ALU.add))
                link(nc.vector.tensor_tensor(gate, gate, s["gate_sign"][:], ALU.mult))
                link(nc.vector.scalar_tensor_tensor(gate, gate, 0.25, s["gate_sign"][:], ALU.max, ALU.mult))
            for which in (1, 4):
                row = mod[:, which * D:(which + 1) * D]
                last = nc.vector.tensor_scalar(row, row, 1.0, None, ALU.add)
            last.then_inc(gates_in, 1)

        @block.gpsimd
        def _(pool):
            nc.gpsimd.memset(s["minus_half"][:], -0.5)
            for name in ("state", "conv_in", "ema_out", "TTbd", "knT"):
                nc.gpsimd.memset(s[name][:], 0.0)
            nc.gpsimd.memset(s["conv_acc"][:], 0.0).then_inc(zeroed, 1)
            pool.wait_ge(zeroed, 1)


def in_tick_order(*phases):
    ahead = [[next(p), k, p] for k, p in enumerate(phases)]
    while ahead:
        first = min(ahead, key=lambda x: (x[0], x[1]))
        try:
            first[0] = next(first[2])
        except StopIteration:
            ahead.remove(first)


def over_steps(eng, phase_a, phase_b, phase_c, steps):
    phases = [(phase_c, 2), (phase_b, 1), (phase_a, 0)]

    def together(m, parity):
        in_tick_order(*[f(m - lag, (parity + lag) % 2) for f, lag in phases
                        if not isinstance(m, int) or 0 <= m - lag < steps])

    for m in range(4):
        together(m, m % 2)
    with eng.Fori(2, steps // 2) as j:
        for r in range(2):
            together(j * 2 + r, r)
    together(steps, 0)
    together(steps + 1, 1)


def once_positive(eng, semaphore, value):
    if not isinstance(value, int) or value > 0:
        eng.wait_ge(semaphore, value)


def own(bank):
    return bass.AP(bank.tensor, bank.offset, [bank.ap[0], (P + C, NH), (1, C)])


def pass_one(nc, ctx, x, x1, s, ps):
    sem = lambda name: ctx.enter_context(nc.semaphore(name))
    x_in, xres_in, x1_out = [sem("x_in_even"), sem("x_in_odd")], sem("xres_in"), sem("x1_out")
    st_ok, ag_ok, stats, rstd = sem("ln_stats"), sem("ln_aggregated"), sem("ln_var_eps"), sem("ln_rstd")
    normed, scaled, h_ready = sem("ln_normed"), sem("ln_scaled"), sem("h_ready")
    hT_ps, hT_ok = sem("hT_in_psum"), sem("hT_ready")
    proj_ps, decay_ps, small_ps = sem("proj_in_psum"), sem("decay_in_psum"), sem("small_in_psum")
    conv_in_ok, conv_tap, carried = sem("conv_in_ready"), sem("conv_tap"), sem("conv_carried")
    th_decay, small_sum, th_small, beta_ok = sem("tanh_decay"), sem("small_sum"), sem("tanh_small"), sem("beta_mix_ready")
    qkvT_ok, ema_in, ema_hist, ema_first, ema_ok = (sem("qkvT_ready"), sem("ema_gamma"), sem("ema_history"), sem("ema_first"),
                                                    sem("ema_ready"))
    qk_ps, v_ps, sq_ok, ssq_ok, eps_ok, r_ok = (sem("qk_rows_in_psum"), sem("v_rows_in_psum"), sem("squares"),
                                                sem("square_sums"), sem("norm_eps"), sem("norm_scale"))
    ema_rows, qkn_ok, kb_ok, mix_b = sem("ema_rows"), sem("qk_normed"), sem("kb_ready"), sem("mix_ema")
    knT_ps, kqT_ps, knT_ok, kqT_ok = sem("knT_in_psum"), sem("kqT_in_psum"), sem("knT_ready"), sem("kqT_ready")
    kbd_ok, gram_ps, gram_ok, lc_ok = sem("k_blocks_ready"), sem("gram_in_psum"), sem("gram_masked"), sem("L_compact")
    y0_ok = sem("L_level_0")
    y_ps, y_ok, z_ps, t_ok, tt_ok = sem("LT_in_psum"), sem("LT_masked"), sem("TLT_in_psum"), sem("T_ready"), sem("Tt_ready")
    uw_ps, uw_ok, ws_ps, o_ps, un_ok = sem("uw_in_psum"), sem("uw_ready"), sem("wS_in_psum"), sem("o_in_psum"), sem("u_new")
    ds_ps, s_ok, mix_a = sem("dS_in_psum"), sem("state_ready"), sem("mix_delta")
    o_ok, osq_ok, oss_ok, oeps_ok, or_ok = (sem("o_ready"), sem("o_squares"), sem("o_square_sums"), sem("o_norm_eps"),
                                            sem("o_norm_scale"))
    on_ok, onT_ps, onT_ok, wo_ps, gated, x1_ok = (sem("o_normed"), sem("onT_in_psum"), sem("onT_ready"),
                                                  sem("out_in_psum"), sem("gated"), sem("x1_ready"))
    v, gp, ac, te = nc.vector, nc.gpsimd, nc.scalar, nc.tensor
    heads = lambda ap: ap.rearrange("p (h d) -> p h d", d=DH)
    both = lambda ap: ap.rearrange("p a b -> p (a b)")
    ident = s["ident"]
    A_BANK = (0, 1)
    b_bank = lambda g: (2 + 2 * g, 3 + 2 * g)
    C_BANK = (6, 7)
    HALVES = (slice(0, DH), slice(DH, P))
    level_tick = lambda lev: 10 + 4 * lev
    c_tick = lambda g: 15 * g

    with nc.Block() as block:
        @block.sync
        def _(sp):
            def load(n, parity):
                once_positive(sp, normed, (n - 1) * G)
                for g in range(G):
                    for i in range(QB):
                        sp.dma_start(s["x_in"][i * C:(i + 1) * C, parity, g, :],
                                     x[g * QB + i, bass.ds(n * C, C), :]).then_inc(x_in[parity], 16)

            def residual_and_store(n):
                once_positive(sp, x1_ok, n * G)
                for g in range(G):
                    for i in range(QB):
                        sp.dma_start(s["x_res"][i * C:(i + 1) * C, g, :],
                                     x[g * QB + i, bass.ds(n * C, C), :]).then_inc(xres_in, 16)
                for g in range(G):
                    sp.wait_ge(x1_ok, n * G + g + 1)
                    for i in range(QB):
                        sp.dma_start(x1[g * QB + i, bass.ds(n * C, C), :],
                                     s["x1_rows"][i * C:(i + 1) * C, g, :]).then_inc(x1_out, 16)

            for n in range(4):
                load(n, n % 2)
            residual_and_store(0)
            with sp.Fori(2, STEPS // 2) as j:
                for r in range(2):
                    load(j * 2 + r, r)
                    residual_and_store(j * 2 + r - 3)
            for n in (STEPS - 3, STEPS - 2, STEPS - 1):
                residual_and_store(n)
            sp.wait_ge(x1_out, 16 * B * STEPS)

        @block.gpsimd
        def _(pool):
            mh = s["minus_half"]

            def phase_a(n, r):
                yield 2
                pool.wait_ge(stats, n + 1)
                gp.tensor_tensor(s["ln_r"][:], s["ln_v"][:], mh[:, 0:G], ALU.pow).then_inc(rstd, 1)
                yield 5
                pool.wait_ge(scaled, n + 1)
                gp.tensor_tensor(s["h"][:], s["h"][:], s["shift1"][:], ALU.add).then_inc(h_ready, 1)

            def phase_b(n, r):
                for g in range(G):
                    yield 3 + g
                    pool.wait_ge(eps_ok, n * G + g + 1)
                    gp.tensor_tensor(s["rqk"][:, g, :], s["ss"][:, g, :], mh[:, 0:2 * NH], ALU.pow).then_inc(r_ok, 1)
                for g in range(G):
                    yield 8 + 4 * g
                    pool.wait_ge(qkn_ok, n * G + g + 1)
                    once_positive(pool, ds_ps, (n - 1) * G * PAIRS)
                    gp.tensor_tensor(s["k_bd"][:, r, g], bc(s["qkn"][:, g, 1, :].unsqueeze(1), [P, QB, D]),
                                     bc(s["quad_mask"][:].unsqueeze(2), [P, QB, D]), ALU.mult).then_inc(kbd_ok, 1)
                for g in range(G):
                    yield 16 + g
                    pool.wait_ge(ema_rows, n * G + g + 1)
                    pool.wait_ge(beta_ok, n + 1)
                    gp.tensor_tensor(heads(s["mix_e"][:, r, g, :]), heads(s["ema_rows"][:, g, :]),
                                     bc(s["bm"][:, g, NH:2 * NH].unsqueeze(2), [P, NH, DH]), ALU.mult).then_inc(mix_b, 1)

            def phase_c(n, r):
                for g in range(G):
                    yield c_tick(g) + 9
                    pool.wait_ge(oeps_ok, n * G + g + 1)
                    gp.tensor_tensor(s["orr"][:, g, :], s["oss"][:, g, :], mh[:, 0:NH], ALU.pow).then_inc(or_ok, 1)
                    yield c_tick(g) + 15
                    pool.wait_ge(gated, n * G + g + 1)
                    pool.wait_ge(xres_in, (n + 1) * 16 * B)
                    once_positive(pool, x1_out, n * 16 * B)
                    gp.tensor_tensor(s["x1_rows"][:, g, :], s["y"][:, g, :], s["x_res"][:, g, :], ALU.add).then_inc(x1_ok, 1)

            over_steps(pool, phase_a, phase_b, phase_c, STEPS)

        @block.scalar
        def _(act):
            def phase_a(n, r):
                yield 7
                act.wait_ge(hT_ps, n + 1)
                ac.copy(both(s["hT"][:]), ps[:, A_BANK[1], :]).then_inc(hT_ok, 1)
                for c in range(3):
                    yield 9 + c
                    act.wait_ge(proj_ps, n * 3 + c + 1)
                    if c == 0:
                        once_positive(act, carried, n)
                    ac.copy(s["conv_in"][:, 2 * c:2 * c + 2, :, TAPS - 1:],
                            ps[:, A_BANK[c % 2], :].rearrange("p (m b t) -> p m b t", m=2, t=C)).then_inc(conv_in_ok, 1)
                yield 11.5
                act.wait_ge(conv_in_ok, n * 3 + 3)
                for m in range(M):
                    last = ac.activation(s["conv_acc"][:, m, :].rearrange("p (b t) -> p b t", t=C), s["conv_in"][:, m, :, 0:C],
                                         ACT.Identity, scale=s["conv_w"][:, m, 0:1])
                last.then_inc(conv_tap, 1)
                yield 12
                act.wait_ge(decay_ps, n + 1)
                ac.activation(s["th_decay"][:], ps[:, A_BANK[1], :], ACT.Tanh, scale=0.5).then_inc(th_decay, 1)
                yield 14
                act.wait_ge(small_sum, n + 1)
                ac.activation(s["th_small"][:, r], s["small"][:], ACT.Tanh, scale=0.5).then_inc(th_small, 1)
                yield 20
                act.wait_ge(conv_tap, (n + 1) * TAPS)
                once_positive(act, v_ps, (n - 1) * G)
                ac.activation(s["qkvT"][:, r], s["conv_acc"][:], ACT.Silu).then_inc(qkvT_ok, 1)
                ac.copy(s["conv_in"][:, :, :, 0:TAPS - 1].rearrange("p m b t -> p (m b) t"),
                        s["conv_in"][:, :, :, C:C + TAPS - 1].rearrange("p m b t -> p (m b) t")).then_inc(carried, 1)

            def phase_b(n, r):
                for g in range(G):
                    yield 1
                    act.wait_ge(qk_ps, n * G + g + 1)
                    ac.activation(s["sq"][:, g, :], ps[:, b_bank(g)[0], :], ACT.Square).then_inc(sq_ok, 1)
                    act.wait_ge(v_ps, n * G + g + 1)
                    once_positive(act, mix_b, n * G)
                    ac.copy(s["ema_rows"][:, g, :], ps[:, b_bank(g)[1], D:2 * D]).then_inc(ema_rows, 1)
                for g in range(G):
                    yield 7
                    act.wait_ge(knT_ps, n * G + g + 1)
                    for par, half in enumerate(HALVES):
                        last = ac.copy(s["knT"][half, g, par], ps[half, b_bank(g)[0], 0:D].rearrange("p (m t) -> p m t", m=PAIRS))
                    last.then_inc(knT_ok, 1)
                    yield 8
                    act.wait_ge(kqT_ps, n * G + g + 1)
                    ac.copy(s["kqT"][:, r, g].rearrange("p a b c -> p (a b c)"), ps[:, b_bank(g)[1], :]).then_inc(kqT_ok, 1)

            def phase_c(n, r):
                for g in range(G):
                    t = c_tick(g)
                    yield t + 1
                    act.wait_ge(uw_ps, n * G + g + 1)
                    ac.activation(both(s["wT"][:, g]), ps[:, C_BANK[1], 0:D], ACT.Identity, scale=-1.0).then_inc(uw_ok, 1)
                    yield t + 3
                    act.wait_ge(ws_ps, n * G + g + 1)
                    ac.copy(s["un"][:, g, :], ps[:, C_BANK[0], 0:D]).then_inc(un_ok, 1)
                    yield t + 7
                    act.wait_ge(o_ok, n * G + g + 1)
                    ac.activation(s["osq"][:, g, :], s["o"][:, g, :], ACT.Square).then_inc(osq_ok, 1)
                    yield t + 10
                    act.wait_ge(or_ok, n * G + g + 1)
                    for h in range(NH):
                        last = ac.activation(s["on"][:, g, h * DH:(h + 1) * DH], s["o"][:, g, h * DH:(h + 1) * DH], ACT.Identity,
                                             scale=s["orr"][:, g, h:h + 1])
                    last.then_inc(on_ok, 1)
                    yield t + 12
                    act.wait_ge(onT_ps, n * G + g + 1)
                    ac.copy(both(s["onT"][:, g]), ps[:, C_BANK[0], 0:D]).then_inc(onT_ok, 1)

            over_steps(act, phase_a, phase_b, phase_c, STEPS)

        @block.tensor
        def _(pe):
            def phase_a(n, r):
                yield 6
                pe.wait_ge(h_ready, n + 1)
                once_positive(pe, th_decay, n)
                for k in range(KD):
                    for g in range(G):
                        last = te.transpose(ps[:, A_BANK[1], (k * G + g) * P:(k * G + g + 1) * P], s["h"][:, g, k * P:(k + 1) * P], ident[:])
                last.then_inc(hT_ps, 1)
                for c in range(3):
                    yield 8 + c
                    pe.wait_ge(hT_ok, n + 1)
                    if c == 0:
                        once_positive(pe, small_sum, n)
                    if c == 2:
                        pe.wait_ge(conv_in_ok, n * 3 + 1)
                    for m in (2 * c, 2 * c + 1):
                        for k in range(KD):
                            last = te.matmul(ps[:, A_BANK[c % 2], (m % 2) * COLS:(m % 2 + 1) * COLS], s["w_qkv"][:, k, m * P:(m + 1) * P],
                                             s["hT"][:, k, :], start=(k == 0), stop=(k == KD - 1))
                    last.then_inc(proj_ps, 1)
                yield 11
                pe.wait_ge(conv_in_ok, n * 3 + 2)
                for pair in range(PAIRS):
                    for k in range(KD):
                        last = te.matmul(ps[:, A_BANK[1], pair * COLS:(pair + 1) * COLS], s["w_decay"][:, k, pair * P:(pair + 1) * P],
                                         s["hT"][:, k, :], start=(k == 0), stop=(k == KD - 1))
                last.then_inc(decay_ps, 1)
                yield 12
                pe.wait_ge(conv_in_ok, n * 3 + 3)
                for g in range(G):
                    for k in range(KD):
                        last = te.matmul(ps[:, A_BANK[0], g * P:(g + 1) * P], s["hT"][:, k, g * P:(g + 1) * P],
                                         s["w_beta_mix"][:, k, :], start=(k == 0), stop=(k == KD - 1))
                last.then_inc(small_ps, 1)

            def phase_b(n, r):
                for g in range(G):
                    yield 0
                    pe.wait_ge(qkvT_ok, n + 1)
                    once_positive(pe, tt_ok, n * LEVELS * G)
                    for m in range(4):
                        last = te.transpose(ps[:, b_bank(g)[0], m * P:(m + 1) * P], s["qkvT"][:, r, m, g * P:(g + 1) * P], ident[:])
                    last.then_inc(qk_ps, 1)
                    pe.wait_ge(ema_ok, n + 1)
                    for m in range(2):
                        te.transpose(ps[:, b_bank(g)[1], m * P:(m + 1) * P], s["qkvT"][:, r, 4 + m, g * P:(g + 1) * P], ident[:])
                    for m in range(2):
                        last = te.transpose(ps[:, b_bank(g)[1], (2 + m) * P:(3 + m) * P], s["ema_out"][:, r, m, g * P:(g + 1) * P], ident[:])
                    last.then_inc(v_ps, 1)
                for g in range(G):
                    yield 6
                    pe.wait_ge(qkn_ok, n * G + g + 1)
                    for m in range(PAIRS):
                        last = te.transpose(ps[:, b_bank(g)[0], m * P:(m + 1) * P], s["qkn"][:, g, 1, m * P:(m + 1) * P], ident[:])
                    last.then_inc(knT_ps, 1)
                    yield 7
                    pe.wait_ge(kb_ok, n * G + g + 1)
                    for m in range(PAIRS):
                        te.transpose(ps[:, b_bank(g)[1], 2 * m * P:(2 * m + 1) * P], s["kb"][:, r, g, m * P:(m + 1) * P], ident[:])
                        last = te.transpose(ps[:, b_bank(g)[1], (2 * m + 1) * P:(2 * m + 2) * P], s["qkn"][:, g, 0, m * P:(m + 1) * P], ident[:])
                    last.then_inc(kqT_ps, 1)
                for g in range(G):
                    yield 9
                    pe.wait_ge(knT_ok, n * G + g + 1)
                    pe.wait_ge(kqT_ok, n * G + g + 1)
                    for par in range(2):
                        for m in range(PAIRS):
                            last = te.matmul(ps[:, b_bank(g)[par], m * 2 * P:(m + 1) * 2 * P], s["knT"][:, g, par, m, :],
                                             both(s["kqT"][:, r, g, m]), start=True, stop=True)
                    last.then_inc(gram_ps, 1)
                for lev in range(1, LEVELS):
                    for g in range(G):
                        yield level_tick(lev)
                        pe.wait_ge(t_ok, (n * LEVELS + lev - 1) * G + g + 1)
                        for h in range(NH):
                            last = te.matmul(ps[:, b_bank(g)[0], h * P:(h + 1) * P], s["LA"][:, r, g, h, 0, :], both(s["T"][:, g]), start=True, stop=True)
                        last.then_inc(y_ps, 1)
                    for g in range(G):
                        yield level_tick(lev) + 2
                        pe.wait_ge(y_ok, (n * (LEVELS - 1) + lev - 1) * G + g + 1)
                        pe.wait_ge(tt_ok, (n * LEVELS + lev - 1) * G + g + 1)
                        for h in range(NH):
                            last = te.matmul(ps[:, b_bank(g)[1], h * P:(h + 1) * P], s["TTbd"][:, r, g, h, :], both(s["Y"][:, g]), start=True, stop=True)
                        last.then_inc(z_ps, 1)

            def phase_c(n, r):
                for g in range(G):
                    t = c_tick(g)
                    yield t
                    pe.wait_ge(tt_ok, (n * LEVELS + LEVELS - 1) * G + g + 1)
                    once_positive(pe, gated, n * G + g)
                    for h in range(NH):
                        te.matmul(ps[:, C_BANK[0], h * DH:(h + 1) * DH], s["TTbd"][:, r, g, h, :], s["vb"][:, r, g, h * DH:(h + 1) * DH],
                                  start=(h == 0), stop=False, skip_group_check=True)
                        last = te.matmul(ps[(h % 2) * DH:(h % 2 + 1) * DH, C_BANK[1], (h // 2) * P:(h // 2 + 1) * P],
                                         s["kb"][:, r, g, h * DH:(h + 1) * DH], s["TTbd"][:, r, g, h, :], start=True, stop=True)
                    last.then_inc(uw_ps, 1)
                    yield t + 2
                    pe.wait_ge(uw_ok, n * G + g + 1)
                    once_positive(pe, s_ok, (n - 1) * G + g + 1)
                    for pair in range(PAIRS):
                        for i in range(QB):
                            last = te.matmul(ps[i * C:(i + 1) * C, C_BANK[0], pair * P:(pair + 1) * P], s["wT"][:, g, pair, i * C:(i + 1) * C],
                                             s["state"][:, g * QB + i, pair, :], start=False, stop=True, skip_group_check=True)
                    last.then_inc(ws_ps, 1)
                    for pair in range(PAIRS):
                        for i in range(QB):
                            te.matmul(ps[i * C:(i + 1) * C, C_BANK[1], pair * P:(pair + 1) * P], s["kqT"][:, r, g, pair, 1, i * C:(i + 1) * C],
                                      s["state"][:, g * QB + i, pair, :], start=(pair == 0), stop=False, skip_group_check=True)
                    yield t + 4
                    pe.wait_ge(un_ok, n * G + g + 1)
                    pe.wait_ge(kbd_ok, n * G + g + 1)

                    def state_product(pair, i):
                        return te.matmul(ps[:, C_BANK[pair], i * P:(i + 1) * P], s["k_bd"][:, r, g, i, pair * P:(pair + 1) * P],
                                         s["un"][:, g, pair * P:(pair + 1) * P], start=True, stop=True)

                    for h in range(NH):
                        last = te.matmul(ps[:, C_BANK[1], h * DH:(h + 1) * DH], s["LA"][:, r, g, h, 1, :], s["un"][:, g, h * DH:(h + 1) * DH],
                                         start=False, stop=True, skip_group_check=True)
                        if h == NH - 1:
                            last.then_inc(o_ps, 1)
                        last = state_product(0, h)
                    last.then_inc(ds_ps, 1)
                    yield t + 6
                    pe.wait_ge(mix_a, n * G + g + 1)
                    for i in range(QB):
                        last = state_product(1, i)
                    last.then_inc(ds_ps, 1)
                    yield t + 11
                    pe.wait_ge(on_ok, n * G + g + 1)
                    for m in range(KD):
                        last = te.transpose(ps[:, C_BANK[0], m * P:(m + 1) * P], s["on"][:, g, m * P:(m + 1) * P], ident[:])
                    last.then_inc(onT_ps, 1)
                    yield t + 13
                    pe.wait_ge(onT_ok, n * G + g + 1)
                    for k in range(KD):
                        last = te.matmul(ps[:, C_BANK[1], 0:D], s["onT"][:, g, k, :], s["w_out"][:, k, :], start=(k == 0), stop=(k == KD - 1))
                    last.then_inc(wo_ps, 1)

            over_steps(pe, phase_a, phase_b, phase_c, STEPS)

        @block.vector
        def _(dve):
            def phase_a(n, r):
                yield 0
                dve.wait_ge(x_in[r], (n - r) * (8 * B) + 16 * B)
                for g in range(G):
                    last = v.bn_stats(s["ln_st"][:, g, :], s["x_in"][:, r, g, :])
                last.then_inc(st_ok, 1)
                yield 1
                dve.wait_ge(st_ok, n + 1)
                v.tensor_copy(s["pad"][:], s["ln_st"][:, 0, 0:1])
                for g in range(G):
                    last = v.bn_aggr(s["ln_mv"][:, g, :], s["ln_st"][:, g, :])
                last.then_inc(ag_ok, 1)
                dve.wait_ge(ag_ok, n + 1)
                v.tensor_scalar(s["ln_v"][:], s["ln_mv"][:, :, 1], 1e-5, None, ALU.add).then_inc(stats, 1)
                yield 3
                dve.wait_ge(rstd, n + 1)
                for g in range(G):
                    v.tensor_scalar(s["h"][:, g, :], s["x_in"][:, r, g, :], s["ln_mv"][:, g, 0:1], s["ln_r"][:, g:g + 1],
                                    ALU.subtract, ALU.mult).then_inc(normed, 1)
                yield 4
                dve.wait_ge(normed, (n + 1) * G)
                v.tensor_tensor(s["h"][:], s["h"][:], s["scale1"][:], ALU.mult).then_inc(scaled, 1)
                for j in range(1, TAPS):
                    yield (None, 13.5, 14.5, 16)[j]
                    dve.wait_ge(conv_tap, n * TAPS + j)
                    for m in range(M):
                        xin = s["conv_in"][:, m, :, j:j + C]
                        acc = s["conv_acc"][:, m, :].rearrange("p (b t) -> p b t", t=C)
                        last = v.scalar_tensor_tensor(acc, xin, s["conv_w"][:, m, j:j + 1], acc, ALU.mult, ALU.add)
                    last.then_inc(conv_tap, 1)
                    if j == 1:
                        yield 13.6
                        dve.wait_ge(small_ps, n + 1)
                        v.tensor_tensor(s["small"][:], ps[:, A_BANK[0], 0:G * P].rearrange("p (g e) -> p g e", g=G)[:, :, 0:2 * NH],
                                        bc(s["small_bias"][:].unsqueeze(1), [P, G, 2 * NH]), ALU.add).then_inc(small_sum, 1)
                first = lambda t: t.rearrange("p (q t) -> p q t", t=C)
                yield 18
                dve.wait_ge(th_decay, n + 1)
                v.tensor_scalar(s["gam"][:], s["th_decay"][:], 0.5, 0.5, ALU.mult, ALU.add)
                v.tensor_scalar(s["omg"][:], s["th_decay"][:], -0.5, 0.5, ALU.mult, ALU.add).then_inc(ema_in, 1)
                yield 21
                dve.wait_ge(ema_in, n + 1)
                dve.wait_ge(qkvT_ok, n + 1)
                v.tensor_tensor(s["omg"][:], s["omg"][:], both(s["qkvT"][:, r, 4:6, :]), ALU.mult)
                v.tensor_tensor(s["ema_hist"][:], first(s["gam"][:])[:, :, 0], first(both(s["ema_out"][:, 1 - r]))[:, :, C - 1],
                                ALU.mult).then_inc(ema_hist, 1)
                yield 22
                dve.wait_ge(ema_hist, n + 1)
                v.tensor_tensor(first(s["omg"][:])[:, :, 0], first(s["omg"][:])[:, :, 0], s["ema_hist"][:], ALU.add)
                v.memset(first(s["gam"][:])[:, :, 0], 0.0).then_inc(ema_first, 1)
                yield 23
                dve.wait_ge(ema_first, n + 1)
                v.tensor_tensor_scan(both(s["ema_out"][:, r]), s["gam"][:], s["omg"][:], 0.0, ALU.mult, ALU.add).then_inc(ema_ok, 1)

            def phase_b(n, r):
                yield 1
                dve.wait_ge(th_small, n + 1)
                once_positive(dve, mix_b, n * G)
                v.tensor_scalar(s["bm"][:], s["th_small"][:, r], 0.5, 0.5, ALU.mult, ALU.add)
                v.tensor_scalar(s["omm"][:, r], s["th_small"][:, r, :, NH:], -0.5, 0.5, ALU.mult, ALU.add).then_inc(beta_ok, 1)
                for g in range(G):
                    yield 2 + g
                    dve.wait_ge(sq_ok, n * G + g + 1)
                    v.tensor_reduce(s["ss"][:, g, :], heads(s["sq"][:, g, :]), AX_X, ALU.add).then_inc(ssq_ok, 1)
                    dve.wait_ge(ssq_ok, n * G + g + 1)
                    v.tensor_scalar(s["ss"][:, g, :], s["ss"][:, g, :], 1e-6, None, ALU.add).then_inc(eps_ok, 1)
                for g in range(G):
                    yield 5 + g
                    beta = bc(s["bm"][:, g, 0:NH].unsqueeze(2), [P, NH, DH])
                    dve.wait_ge(r_ok, n * G + g + 1)
                    once_positive(dve, kbd_ok, (n - 1) * G + g + 1)
                    v.tensor_tensor(heads(both(s["qkn"][:, g])), heads(ps[:, b_bank(g)[0], :]),
                                    bc(s["rqk"][:, g, :].unsqueeze(2), [P, 2 * NH, DH]), ALU.mult).then_inc(qkn_ok, 1)
                    dve.wait_ge(ema_rows, n * G + g + 1)
                    dve.wait_ge(beta_ok, n + 1)
                    v.tensor_tensor(heads(s["vb"][:, r, g, :]), heads(ps[:, b_bank(g)[1], 0:D]), beta, ALU.mult)
                    dve.wait_ge(qkn_ok, n * G + g + 1)
                    v.tensor_tensor(heads(s["kb"][:, r, g, :]), heads(s["qkn"][:, g, 1, :]), beta, ALU.mult).then_inc(kb_ok, 1)
                for g in range(G):
                    yield 10
                    dve.wait_ge(gram_ps, n * G + g + 1)
                    mask = bc(both(s["chunk_mask"][:]).unsqueeze(1), [P, PAIRS, 2 * P])
                    for par in range(2):
                        dst = s["LA"][:, r, g, par::2].rearrange("p m a b -> p m (a b)")
                        last = v.tensor_tensor(dst, ps[:, b_bank(g)[par], :].rearrange("p (m c) -> p m c", m=PAIRS), mask, ALU.mult)
                    last.then_inc(gram_ok, 1)
                for g in range(G):
                    yield 11
                    dve.wait_ge(gram_ok, n * G + g + 1)
                    for i in range(QB):
                        q = slice(i * C, (i + 1) * C)
                        last = v.transpose(s["Y"][q, g], s["LA"][q, r, g, :, 0, q])
                    last.then_inc(lc_ok, 1)
                for g in range(G):
                    yield 12
                    dve.wait_ge(lc_ok, n * G + g + 1)
                    v.tensor_tensor(s["Y0"][:, g], s["Y"][:, g], bc(s["levels"][:, 0, :].unsqueeze(1), [P, NH, C]), ALU.mult).then_inc(y0_ok, 1)
                for lev in range(LEVELS):
                    if lev:
                        for g in range(G):
                            yield level_tick(lev) + 1
                            dve.wait_ge(y_ps, (n * (LEVELS - 1) + lev - 1) * G + g + 1)
                            v.tensor_tensor(s["Y"][:, g], own(ps[:, b_bank(g)[0], :]),
                                            bc(s["levels"][:, lev, :].unsqueeze(1), [P, NH, C]), ALU.mult).then_inc(y_ok, 1)
                    for g in range(G):
                        yield level_tick(lev) + 3
                        if lev == 0:
                            dve.wait_ge(y0_ok, n * G + g + 1)
                            v.tensor_tensor(s["T"][:, g], bc(s["eye32"][:].unsqueeze(1), [P, NH, C]), s["Y0"][:, g],
                                            ALU.subtract).then_inc(t_ok, 1)
                        else:
                            dve.wait_ge(z_ps, (n * (LEVELS - 1) + lev - 1) * G + g + 1)
                            v.tensor_tensor(s["T"][:, g], s["T"][:, g], own(ps[:, b_bank(g)[1], :]),
                                            ALU.subtract).then_inc(t_ok, 1)
                    for g in range(G):
                        yield level_tick(lev) + 3
                        dve.wait_ge(t_ok, (n * LEVELS + lev) * G + g + 1)
                        for i in range(QB):
                            q = slice(i * C, (i + 1) * C)
                            last = v.transpose(s["TTbd"][q, r, g, :, q], s["T"][q, g])
                        last.then_inc(tt_ok, 1)

            def phase_c(n, r):
                for g in range(G):
                    t = c_tick(g)
                    yield t + 5
                    dve.wait_ge(o_ps, n * G + g + 1)
                    v.tensor_tensor(heads(s["mix_d"][:, g, :]), heads(ps[:, C_BANK[1], 0:D]),
                                    bc(s["omm"][:, r, g, :].unsqueeze(2), [P, NH, DH]), ALU.mult).then_inc(mix_a, 1)
                    yield t + 6
                    dve.wait_ge(mix_a, n * G + g + 1)
                    dve.wait_ge(mix_b, n * G + g + 1)
                    v.tensor_tensor(s["o"][:, g, :], s["mix_d"][:, g, :], s["mix_e"][:, r, g, :], ALU.add).then_inc(o_ok, 1)
                    for pair in range(PAIRS):
                        yield t + 6 + pair
                        dve.wait_ge(ds_ps, (n * G + g) * PAIRS + pair + 1)
                        for par, half in enumerate(HALVES):
                            st = s["state"][half, g * QB:(g + 1) * QB, pair, half]
                            last = v.tensor_tensor(st, st, ps[half, C_BANK[pair], :].rearrange("p (i c) -> p i c", i=QB)[:, :, half], ALU.add)
                    last.then_inc(s_ok, 1)
                    yield t + 8
                    dve.wait_ge(osq_ok, n * G + g + 1)
                    v.tensor_reduce(s["oss"][:, g, :], heads(s["osq"][:, g, :]), AX_X, ALU.add).then_inc(oss_ok, 1)
                    dve.wait_ge(oss_ok, n * G + g + 1)
                    v.tensor_scalar(s["oss"][:, g, :], s["oss"][:, g, :], 1.0 / DH, 1e-5, ALU.mult, ALU.add).then_inc(oeps_ok, 1)
                    yield t + 14
                    dve.wait_ge(wo_ps, n * G + g + 1)
                    v.tensor_tensor(s["y"][:, g, :], ps[:, C_BANK[1], 0:D], s["gate1"][:, g, :], ALU.mult).then_inc(gated, 1)

            over_steps(dve, phase_a, phase_b, phase_c, STEPS)


def plan_tiles(dve, v, s, planned):
    steps = [0]

    def link(ins):
        steps[0] += 1
        ins.then_inc(planned, 1)
        dve.wait_ge(planned, steps[0])

    spare = s["b_x1"][:].rearrange("p b d -> p (b d)")
    under = spare[:, 0:NEXP * (TOK // P)].rearrange("p (e k) -> p e k", e=NEXP)
    all_past = spare[:, NEXP * (TOK // P):NEXP * (TOK // P) + TILES * (NEXP - 1)].rearrange("p (i e) -> p i e", e=NEXP - 1)
    most = TOK // P
    link(v.tensor_tensor(s["p_count"][:], s["next_slot"][:], s["region"][:], ALU.subtract))
    link(v.tensor_tensor(under, bc(s["p_count"][:].unsqueeze(2), [P, NEXP, most]),
                         bc(s["slot_steps"][:, 0:most].unsqueeze(1), [P, NEXP, most]), ALU.is_gt))
    link(v.tensor_reduce(s["p_tiles"][:], under, AX_X, ALU.add))
    link(v.tensor_tensor_scan(s["p_until"][:], s["ones"][:, 0:NEXP], s["p_tiles"][:], 0.0, ALU.mult, ALU.add))
    past = [P, TILES, NEXP - 1]
    link(v.tensor_scalar(s["p_tile"][:], s["slot_steps"][:], 1.0 / P, None, ALU.mult))
    link(v.tensor_tensor(all_past, bc(s["p_tile"][:].unsqueeze(2), past),
                         bc(s["p_until"][:, 0:NEXP - 1].unsqueeze(1), past), ALU.is_ge))
    link(v.tensor_reduce(s["p_expert"][:], all_past, AX_X, ALU.add))
    link(v.tensor_tensor(all_past, all_past, bc(s["p_tiles"][:, 0:NEXP - 1].unsqueeze(1), past), ALU.mult))
    link(v.tensor_reduce(s["p_first"][:], all_past, AX_X, ALU.add))
    link(v.tensor_tensor(s["p_first"][:], s["p_tile"][:], s["p_first"][:], ALU.subtract))
    link(v.tensor_scalar(s["p_first"][:], s["p_first"][:], float(P), None, ALU.mult))
    link(v.tensor_copy(s["tile_expert"][:], s["p_expert"][:]))
    link(v.tensor_scalar(s["p_expert"][:], s["p_expert"][:], float(REGION), None, ALU.mult))
    link(v.tensor_tensor(s["p_first"][:], s["p_first"][:], s["p_expert"][:], ALU.add))
    link(v.tensor_copy(s["tile_slot"][:], s["p_first"][:]))


def pass_two(nc, ctx, x1, haa, x2n, table, mod_rows, d, weights_in, s, ps):
    sem = lambda name: ctx.enter_context(nc.semaphore(name))
    x1_in, st_ok, ag_ok, var_ok, r_ok = sem("b_x1_in"), sem("b_stats"), sem("b_aggregated"), sem("b_var"), sem("b_rstd")
    norm_ok, scaled_ok, h2_ok = sem("b_normed"), sem("b_scaled"), sem("b_h2_ready")
    nT_ps, nT_ok, qkv_ps, q_ok, kv_ok = (sem("b_nT_in_psum"), sem("b_nT_ready"), sem("b_qkv_in_psum"), sem("b_q_ready"),
                                         sem("b_kv_ready"))
    prod_ok, sc_ok, soft, exp_ok, attn_step = sem("b_products"), sem("b_scores"), sem("b_softmax"), sem("b_exp"), sem("b_attn_step")
    pv_prod, aT_ps, aT_ok, pr_ps, haa_ok = sem("b_pv_product"), sem("b_aT_in_psum"), sem("b_aT_ready"), sem("b_proj_in_psum"), sem("b_after_attn")
    lg_ps, route, gexp_ok, x2_out, haa_out = (sem("b_logits_in_psum"), sem("b_route"), sem("b_gate_exp"), sem("b_x2_out"), sem("b_after_attn_out"))
    loaded, filled = sem("b_loaded"), sem("b_filled")
    names = ["w_qkv2", "w_proj", "w_router", "ln_wb", "region", "next_slot", "slot_steps", "earlier", "b_ids_f", "scan_reset"]
    ALL_LOADED = 16 * (len(names) + 4)

    def constants_there(eng, n):
        if isinstance(n, int) and n == 0:
            eng.wait_ge(loaded, ALL_LOADED)

    pow_ok, planned = sem("b_power"), sem("b_planned")
    held = sem("b_wait_held")
    hot_ok, count_ps, place, ids_ok, slot_ok, listed = (sem("b_chosen"), sem("b_counts_in_psum"), sem("b_place"), sem("b_ids_ready"),
                                                      sem("b_slots_ready"), sem("b_listed"))
    v, gp, ac, te = nc.vector, nc.gpsimd, nc.scalar, nc.tensor
    ROUTE = 9
    ident = s["ident"]
    aT = s["b_attn"][:].rearrange("p b d -> p (b d)").rearrange("p (k t) -> p k t", k=KD)
    of_l = lambda ap: ap.rearrange("b l d -> l b d")
    x1_of, haa_of, x2n_of = of_l(x1), of_l(haa), of_l(x2n)

    def normed(n, l):
        if l < 2:
            return l + 1 if isinstance(n, int) and n == 0 else n * 3 + l
        return n * 3 + 3 if isinstance(n, int) and n == PT - 1 else n * 3 + 5

    def turned(n, c):
        if c:
            return n * 2 + 2 if isinstance(n, int) and n == PT - 1 else n * 2 + 3
        return 1 if isinstance(n, int) and n == 0 else n * 2

    def next_a(n):
        return min(n + 2, PT) if isinstance(n, int) else n + 2

    with nc.Block() as block:
        @block.sync
        def _(sp):
            def phase_a(n, r):
                yield 0
                if not (isinstance(n, int) and n == 0):
                    sp.wait_ge(norm_ok, normed(n - 1, 0) * B)
                sp.dma_start(s["b_x1"][:], x1_of[bass.ds(n * P, P)]).then_inc(x1_in, 16)
                if isinstance(n, int) and n == 0:
                    for name, which in (("scale2", 4), ("shift2", 3), ("gate2", 5)):
                        rows = mod_rows[:, which * D:(which + 1) * D].unsqueeze(0)
                        sp.dma_start(s[name][:], bc(rows, [P, B, D])).then_inc(loaded, 16)
                    for name in names:
                        sp.dma_start(s[name][:], d[name]).then_inc(loaded, 16)
                    sp.dma_start(table, d["empty_slots"]).then_inc(loaded, 16)
                if isinstance(n, int) and n == 1:
                    for name in ("w_up", "w_down"):
                        sp.dma_start(s[name][:], d[name]).then_inc(weights_in, 16)

            def phase_b(n, r):
                yield 0

            def phase_c(n, r):
                yield 1
                sp.wait_ge(haa_ok, n + 1)
                sp.dma_start(haa_of[bass.ds(n * P, P)], s["b_h2"][:, r]).then_inc(haa_out, 16)
                yield 3
                sp.wait_ge(norm_ok, normed(n, 2) * B)
                sp.dma_start(x2n_of[bass.ds(n * P, P)], s["b_n"][:]).then_inc(x2_out, 16)

            over_steps(sp, phase_a, phase_b, phase_c, PT)
            sp.wait_ge(haa_out, 16 * PT)
            sp.wait_ge(x2_out, 16 * PT)

        @block.gpsimd
        def _(pool):
            nc.gpsimd.memset(s["ones"][:], 1.0).then_inc(filled, 1)
            nc.gpsimd.memset(s["scores"][:], FMIN).then_inc(filled, 1)

            def power(n, l):
                pool.wait_ge(var_ok, normed(n, l))
                if not (isinstance(n, int) and n == 0):
                    pool.wait_ge(norm_ok, normed(n - 1, l) * B)
                gp.tensor_tensor(s["b_r"][:, l, :], s["b_var"][:, l, :], s["minus_half"][:], ALU.pow).then_inc(pow_ok, 1)
                pool.wait_ge(pow_ok, normed(n, l))
                gp.tensor_tensor(s["b_shift"][:, l, :], s["b_neg_mean"][:, l, :], s["b_r"][:, l, :], ALU.mult).then_inc(r_ok, 1)

            def phase_a(n, r):
                yield 6
                power(n, 0)
                yield 9
                constants_there(pool, n)
                pool.wait_ge(scaled_ok, n + 1)
                once_positive(pool, haa_out, (n - 1) * 16)
                gp.tensor_tensor(s["b_h2"][:, r], s["b_n"][:], s["shift2"][:], ALU.add).then_inc(h2_ok, 1)
                yield 12
                power(n, 1)

            def phase_b(n, r):
                yield 0

            def phase_c(n, r):
                yield 2
                power(n, 2)
                yield 13
                pool.wait_ge(ids_ok, n + 1)
                pool.wait_ge(slot_ok, n + 1)
                pool.sem_inc(held, 1)
                for c in range(TOPK):
                    for b in range(B):
                        k = c * B + b
                        gp.indirect_dma_start(table, bass.IndirectOffsetOnAxis(ap=s["b_slot"][:, k:k + 1], axis=0),
                                              s["b_ids"][:, c, b, :], None).then_inc(listed, 16)

            over_steps(pool, phase_a, phase_b, phase_c, PT)
            pool.wait_ge(listed, PT * 16 * TOPK * B)

        @block.scalar
        def _(act):
            def normalise(n, l, src):
                act.wait_ge(r_ok, normed(n, l))
                for b in range(B):
                    ac.activation(s["b_n"][:, b, :], src[:, b, :], ACT.Identity, bias=s["b_shift"][:, l, b:b + 1],
                                  scale=s["b_r"][:, l, b:b + 1]).then_inc(norm_ok, 1)

            def normed_out(n, c):
                for k in range(KD):
                    for q in range(2):
                        act.wait_ge(nT_ps, turned(n, c) * 4 - 3 + 2 * k + q)
                        ac.activation(s["b_nT"][:, k, q * 512:(q + 1) * 512], ps[:, 2 * k + q, :], ACT.Identity,
                                      bias=s["ln_wb"][:, k, 2 * c + 1:2 * c + 2], scale=s["ln_wb"][:, k, 2 * c:2 * c + 1]).then_inc(nT_ok, 1)

            def phase_a(n, r):
                yield 8
                once_positive(act, x2_out, (n - 1) * 16)
                normalise(n, 0, s["b_x1"])
                yield 13
                normalise(n, 1, s["b_h2"][:, r])
                yield 14
                constants_there(act, n)
                once_positive(act, lg_ps, n - 1)
                normed_out(n, 0)
                for i, b in enumerate(reversed(range(B))):
                    act.wait_ge(qkv_ps, n * B + i + 1)
                    if i == 0:
                        once_positive(act, prod_ok, n * B)
                        once_positive(act, pv_prod, (n - 1) * B)
                    bank = 4 + i % 4
                    ac.copy(s["b_q"][:, b, :], ps[:, bank, 0:QH * HD]).then_inc(q_ok, 1)
                    for kv, dst in enumerate((s["b_k"][:, b, :], s["b_v"][:, r, b, :])):
                        src = ps[:, bank, QH * HD + kv * KVH * HD:QH * HD + (kv + 1) * KVH * HD]
                        src = src.rearrange("p (j d) -> p j d", d=HD).unsqueeze(2)
                        last = ac.copy(dst.rearrange("p (j r d) -> p j r d", j=KVH, r=REP), bc(src, [P, KVH, REP, HD]))
                    last.then_inc(kv_ok, 1)

            def phase_b(n, r):
                yield 5
                act.wait_ge(soft, n * 5 + 2)
                ac.activation(s["scores_x"][:], s["scores_x"][:], ACT.Exp, scale=HD ** -0.5).then_inc(exp_ok, 1)

            def phase_c(n, r):
                yield 0
                act.wait_ge(aT_ps, (n + 1) * 4)
                for k in range(KD):
                    for q in range(2):
                        ac.copy(aT[:, k, q * 512:(q + 1) * 512], ps[:, 2 * k + q, :]).then_inc(aT_ok, 1)
                yield 3
                once_positive(act, x2_out, n * 16)
                normalise(n, 2, s["b_h2"][:, r])
                yield 4
                act.wait_ge(qkv_ps, next_a(n) * B)
                normed_out(n, 1)
                yield 7
                act.wait_ge(route, n * ROUTE + 2)
                ac.activation(s["b_gate"][:], s["b_gate"][:], ACT.Exp).then_inc(gexp_ok, 1)

            over_steps(act, phase_a, phase_b, phase_c, PT)

        @block.tensor
        def _(pe):
            def turn(src, arrived):
                for k in range(KD):
                    for q in range(2):
                        for b in range(4):
                            last = te.transpose(ps[:, 2 * k + q, b * P:(b + 1) * P], src[:, 4 * q + b, k * P:(k + 1) * P], ident[:])
                        last.then_inc(arrived, 1)

            def phase_a(n, r):
                yield 14
                pe.wait_ge(norm_ok, normed(n, 1) * B)
                turn(s["b_n"], nT_ps)
                pe.wait_ge(nT_ok, turned(n, 0) * 4)
                constants_there(pe, n)
                once_positive(pe, place, (n - 1) * 5)
                once_positive(pe, kv_ok, n * B)
                for i, b in enumerate(reversed(range(B))):
                    if i >= 4:
                        pe.wait_ge(kv_ok, n * B + i - 3)
                    for k in range(KD):
                        last = te.matmul(ps[:, 4 + i % 4, 0:QKV], s["b_nT"][:, k, b * P:(b + 1) * P], s["w_qkv2"][:, k, :],
                                         start=(k == 0), stop=(k == KD - 1))
                    last.then_inc(qkv_ps, 1)

            def phase_b(n, r):
                yield 0

            def phase_c(n, r):
                yield 0
                pe.wait_ge(attn_step, (n + 1) * (B - 1))
                turn(s["b_attn"], aT_ps)
                pe.wait_ge(aT_ok, (n + 1) * 4)
                pe.wait_ge(kv_ok, next_a(n) * B)
                once_positive(pe, place, n * 5)
                for b in range(B):
                    for k in range(KD):
                        last = te.matmul(ps[:, 4 + b // 2, (b % 2) * D:(b % 2 + 1) * D], aT[:, k, b * P:(b + 1) * P],
                                         s["w_proj"][:, k, :], start=(k == 0), stop=(k == KD - 1))
                    last.then_inc(pr_ps, 1)
                yield 4
                pe.wait_ge(norm_ok, normed(n, 2) * B)
                turn(s["b_n"], nT_ps)
                yield 5
                pe.wait_ge(nT_ok, turned(n, 1) * 4)
                for b in range(B):
                    for k in range(KD):
                        last = te.matmul(ps[:, 4, b * NEXP:(b + 1) * NEXP], s["b_nT"][:, k, b * P:(b + 1) * P], s["w_router"][:, k, :],
                                         start=(k == 0), stop=(k == KD - 1))
                last.then_inc(lg_ps, 1)
                yield 8
                pe.wait_ge(hot_ok, n + 1)
                te.matmul(ps[:, 5, 0:B * NEXP], s["ones"][:], s["b_chosen"][:], start=True, stop=True)
                te.matmul(ps[:, 5, B * NEXP:2 * B * NEXP], s["earlier"][:], s["b_chosen"][:], start=True, stop=True).then_inc(count_ps, 1)

            over_steps(pe, phase_a, phase_b, phase_c, PT)

        @block.vector
        def _(dve):
            def statistics(n, l, src):
                for b in range(B):
                    last = v.bn_stats(s["b_st"][:, b, :], src[:, b, :])
                last.then_inc(st_ok, 1)
                dve.wait_ge(st_ok, normed(n, l))
                v.tensor_copy(s["pad"][:], s["b_st"][:, 0, 0:1])
                for b in range(B):
                    last = v.bn_aggr(s["b_mv"][:, b, :], s["b_st"][:, b, :])
                last.then_inc(ag_ok, 1)
                dve.wait_ge(ag_ok, normed(n, l))
                v.tensor_scalar(s["b_neg_mean"][:, l, :], s["b_mv"][:, :, 0], -1.0, None, ALU.mult)
                v.tensor_scalar(s["b_var"][:, l, :], s["b_mv"][:, :, 1], 1e-5, None, ALU.add).then_inc(var_ok, 1)

            def phase_a(n, r):
                yield 5
                dve.wait_ge(x1_in, (n + 1) * 16)
                statistics(n, 0, s["b_x1"])
                yield 8
                constants_there(dve, n)
                dve.wait_ge(norm_ok, normed(n, 0) * B)
                v.tensor_tensor(s["b_n"][:], s["b_n"][:], s["scale2"][:], ALU.mult).then_inc(scaled_ok, 1)
                yield 11
                dve.wait_ge(h2_ok, n + 1)
                statistics(n, 1, s["b_h2"][:, r])

            def phase_b(n, r):
                def product(i):
                    u = B - 1 - i
                    dve.wait_ge(q_ok, n * B + i + 1)
                    dve.wait_ge(kv_ok, n * B + i + 1)
                    if i == 1:
                        once_positive(dve, attn_step, n * (B - 1))
                    if i >= 2:
                        dve.wait_ge(sc_ok, n * B + i - 1)
                    v.tensor_tensor(s["b_prod"][:, i % 2, 0:B - u, :], s["b_q"][:, u:, :],
                                    bc(s["b_k"][:, u, :].unsqueeze(1), [P, B - u, D]), ALU.mult).then_inc(prod_ok, 1)

                def score(i):
                    u = B - 1 - i
                    dve.wait_ge(prod_ok, n * B + i + 1)
                    v.tensor_reduce(s["scores"][:, u:, :, u], s["b_prod"][:, i % 2, 0:B - u, :].rearrange("p a (h d) -> p a h d", d=HD),
                                    AX_X, ALU.add).then_inc(sc_ok, 1)

                def weigh(u):
                    if u >= 3:
                        dve.wait_ge(attn_step, n * (B - 1) + u - 2)
                    dst = s["b_attn"][:] if u == 0 else s["b_prod"][:, u % 2, 0:B - u, :]
                    v.tensor_tensor(dst.rearrange("p a (h d) -> p a h d", d=HD),
                                    bc(s["b_v"][:, r, u, :].rearrange("p (h d) -> p h d", d=HD).unsqueeze(1), [P, B - u, QH, HD]),
                                    bc(probs[:, u:, :, u].unsqueeze(3), [P, B - u, QH, HD]), ALU.mult).then_inc(pv_prod, 1)

                def add(u):
                    dve.wait_ge(pv_prod, n * B + u + 1)
                    if u > 1:
                        dve.wait_ge(attn_step, n * (B - 1) + u - 1)
                    v.tensor_tensor(s["b_attn"][:, u:, :], s["b_attn"][:, u:, :], s["b_prod"][:, u % 2, 0:B - u, :],
                                    ALU.add).then_inc(attn_step, 1)

                rows = [P, B * QH, B]
                all_scores = s["scores"][:].rearrange("p a h u -> p (a h) u")
                sx = s["scores_x"][:].rearrange("p (q u) -> p q u", u=B)
                probs = s["scores_x"][:].rearrange("p (a h u) -> p a h u", a=B, h=QH)
                yield 0
                if isinstance(n, int) and n == 0:
                    dve.wait_ge(filled, 2)
                product(0)
                for i in range(1, B - 1):
                    product(i)
                    score(i - 1)
                yield 4
                product(B - 1)
                score(B - 2)
                score(B - 1)
                dve.wait_ge(sc_ok, (n + 1) * B)
                v.tensor_reduce(s["b_mx"][:], all_scores, AX_X, ALU.max).then_inc(soft, 1)
                dve.wait_ge(soft, n * 5 + 1)
                v.tensor_tensor(sx, all_scores, bc(s["b_mx"][:].unsqueeze(2), rows), ALU.subtract).then_inc(soft, 1)
                yield 6
                dve.wait_ge(exp_ok, n + 1)
                v.tensor_reduce(s["b_mx"][:], sx, AX_X, ALU.add).then_inc(soft, 1)
                dve.wait_ge(soft, n * 5 + 3)
                v.reciprocal(s["b_den"][:], s["b_mx"][:]).then_inc(soft, 1)
                yield 9
                dve.wait_ge(soft, n * 5 + 4)
                v.tensor_tensor(sx, sx, bc(s["b_den"][:].unsqueeze(2), rows), ALU.mult).then_inc(soft, 1)
                dve.wait_ge(soft, n * 5 + 5)
                once_positive(dve, pr_ps, n * B)
                weigh(0)
                weigh(1)
                yield 12
                weigh(2)
                add(1)
                yield 14
                for u in range(3, B):
                    weigh(u)
                    add(u - 1)
                add(B - 1)

            def phase_c(n, r):
                yield 1
                for half in range(2):
                    dve.wait_ge(pr_ps, n * B + (half + 1) * 4)
                    rows = s["b_h2"][:, r, half * 4:half * 4 + 4, :].rearrange("p (a c) d -> p a (c d)", c=2)
                    last = v.tensor_tensor(rows, ps[:, 4 + half * 2:6 + half * 2, :], rows, ALU.add)
                last.then_inc(haa_ok, 1)
                dve.wait_ge(haa_ok, n + 1)
                statistics(n, 2, s["b_h2"][:, r])
                yield 7
                routed = lambda c: dve.wait_ge(route, n * ROUTE + c)
                dve.wait_ge(lg_ps, n + 1)
                lg = ps[:, 4, 0:B * NEXP].rearrange("p (b e) -> p b e", e=NEXP)
                wide = [P, B, NEXP]
                v.tensor_reduce(s["b_gm"][:], lg, AX_X, ALU.max).then_inc(route, 1)
                routed(1)
                v.tensor_tensor(s["b_gate"][:], lg, bc(s["b_gm"][:].unsqueeze(2), wide), ALU.subtract).then_inc(route, 1)
                dve.wait_ge(gexp_ok, n + 1)
                v.tensor_reduce(s["b_gs"][:], s["b_gate"][:], AX_X, ALU.add).then_inc(route, 1)
                routed(3)
                v.reciprocal(s["b_gm"][:], s["b_gs"][:]).then_inc(route, 1)
                routed(4)
                v.tensor_tensor(s["b_gate"][:], s["b_gate"][:], bc(s["b_gm"][:].unsqueeze(2), wide), ALU.mult).then_inc(route, 1)
                routed(5)
                v.tensor_copy(s["pad"][:], s["b_gate"][:, 0, 0:1])
                for b in range(B):
                    last = v.max(s["b_top"][:, b, :], s["b_gate"][:, b, :])
                last.then_inc(route, 1)
                routed(6)
                v.tensor_copy(s["pad"][:], s["b_top"][:, 0, 0:1])
                for b in range(B):
                    last = v.max_index(s["b_idx"][:, b, :], s["b_top"][:, b, :], s["b_gate"][:, b, :])
                last.then_inc(route, 1)
                routed(7)
                v.tensor_copy(s["b_idf"][:], s["b_idx"][:, :, 0:TOPK]).then_inc(route, 1)
                routed(8)
                iota = bc(s["iota8"][:].unsqueeze(1), wide)
                for c in range(TOPK):
                    last = v.tensor_tensor(s["b_hot"][:, c], iota, bc(s["b_idf"][:, :, c:c + 1], wide), ALU.is_equal)
                last.then_inc(route, 1)
                routed(ROUTE)
                v.tensor_tensor(s["b_chosen"][:].rearrange("p (b e) -> p b e", e=NEXP), s["b_hot"][:, 0], s["b_hot"][:, 1], ALU.add).then_inc(hot_ok, 1)
                v.tensor_copy(s["wts"][:, bass.ds(n * B, B), :], s["b_top"][:, :, 0:TOPK])
                once_positive(dve, listed, n * (16 * TOPK * B))
                v.tensor_copy(s["b_ids"][:], s["b_ids_f"][:]).then_inc(ids_ok, 1)
                v.tensor_scalar(s["b_ids_f"][:], s["b_ids_f"][:], float(P), None, ALU.add)
                yield 12
                placed = lambda c: dve.wait_ge(place, n * 5 + c)
                dve.wait_ge(count_ps, n + 1)
                total = ps[:, 5, 0:B * NEXP].rearrange("p (b e) -> p e b", e=NEXP)
                before = ps[:, 5, B * NEXP:2 * B * NEXP].rearrange("p (b e) -> p b e", e=NEXP)
                v.tensor_copy(s["b_scan_in"][:, :, 0], s["next_slot"][:])
                v.tensor_copy(s["b_scan_in"][:, :, 1:], total[:, :, 0:B - 1]).then_inc(place, 1)
                placed(1)
                v.tensor_tensor_scan(s["b_scan"][:].rearrange("p e b -> p (e b)"), s["scan_reset"][:],
                                     s["b_scan_in"][:].rearrange("p e b -> p (e b)"), 0.0, ALU.mult, ALU.add).then_inc(place, 1)
                placed(2)
                v.tensor_tensor(s["next_slot"][:], s["b_scan"][:, :, B - 1], total[:, :, B - 1], ALU.add)
                v.tensor_tensor(s["b_pos"][:], before, s["b_scan"][:].rearrange("p e b -> p b e"), ALU.add).then_inc(place, 1)
                placed(3)
                v.tensor_tensor(s["b_hot"][:], s["b_hot"][:], bc(s["b_pos"][:].unsqueeze(1), [P, TOPK, B, NEXP]), ALU.mult).then_inc(place, 1)
                placed(4)
                v.tensor_reduce(s["b_slot_f"][:], s["b_hot"][:].rearrange("p r b e -> p (r b) e"), AX_X, ALU.add).then_inc(place, 1)
                placed(5)
                v.tensor_copy(s["b_slot"][:], s["b_slot_f"][:]).then_inc(slot_ok, 1)

            over_steps(dve, phase_a, phase_b, phase_c, PT)
            dve.wait_ge(place, PT * 5)
            plan_tiles(dve, v, s, planned)


def over_tiles(eng, body):
    for i in range(DEEP):
        body(i, i, 0)
    with eng.Fori(1, PT) as j:
        for r in range(DEEP):
            body(j * DEEP + r, r, j)
    with eng.Fori(PT, TILES // DEEP - 1) as j:
        for r in range(DEEP):
            body(j * DEEP + r, r, None)
    for i in range(TILES - DEEP, TILES):
        body(i, i % DEEP, None)


def exists(i):
    return not isinstance(i, int) or i < TILES


def pass_three(nc, ctx, x1, haa, x2n, table, y_rows, weights_in, s, ps):
    sem = lambda name: ctx.enter_context(nc.semaphore(name))
    ids_in, turn_loaded, ids_ok, x_in = sem("c_ids_in"), sem("c_turn_loaded"), sem("c_ids_ready"), [sem(f"c_x_in_{r}") for r in range(XDEEP)]
    loads = lambda i, r: (i - r % XDEEP) * (16 // XDEEP) + 16
    AHEAD = 5
    xT_ps, xT_ok, up_ps, gelu_ok, hT_ps, hT_ok, y_ps, y_ok, y_out = (
        sem("c_xT_in_psum"), sem("c_xT_ready"), sem("c_up_in_psum"), sem("c_gelu"),
        sem("c_hT_in_psum"), sem("c_hT_ready"), sem("c_y_in_psum"), sem("c_y_ready"), sem("c_y_out"))
    v, gp, ac, te = nc.vector, nc.gpsimd, nc.scalar, nc.tensor
    held = sem("c_wait_held")
    ident = s["ident"]
    X_BANK = 0
    UP_BANK, HT_BANK, Y_BANK = (1, 2), (3, 4), (5, 6)
    res_in, res_gated, res_ok = sem("c_residual_in"), sem("c_residual_gated"), sem("c_residual_ready")
    PARTS = 4
    x1_of, haa_of = x1.rearrange("b l d -> l b d"), haa.rearrange("b l d -> l b d")
    w_up = s["w_up"][:].rearrange("p e k f -> p (e k f)")
    w_down = s["w_down"][:].rearrange("p e f d -> p (e f d)")

    with nc.Block() as block:
        @block.sync
        def _(sp):
            with sp.Fori(0, TILES // DEEP) as j:
                for r in range(DEEP):
                    i = j * DEEP + r
                    first = sp.value_load(s["tile_slot"][0:1, bass.ds(i, 1)], min_val=0, max_val=SLOTS - P)
                    sp.dma_start(s["c_all_ids"][:, bass.ds(i, 1), :], table[bass.ds(first, P), :].unsqueeze(1)).then_inc(ids_in, 16)
                sp.wait_ge(ids_in, (j + 1) * (16 * DEEP))
                sp.sem_inc(turn_loaded, 1)

        @block.gpsimd
        def _(pool):
            def gather(i, r):
                pool.wait_ge(ids_ok, i + 1)
                once_positive(pool, xT_ps, i - XDEEP + 1)
                pool.sem_inc(held, 1)
                gp.indirect_dma_start(s["c_x"][:, r % XDEEP, :], None, x2n, bass.IndirectOffsetOnAxis(ap=s["c_ids"][:, r, 0:1], axis=0)).then_inc(x_in[r % XDEEP], 16)

            def step(i, r, t):
                if exists(i + XDEEP):
                    gather(i + XDEEP, (r + XDEEP) % DEEP)
                pool.wait_ge(y_ok, i + 1)
                once_positive(pool, y_out, i * 16)
                pool.sem_inc(held, 1)
                gp.indirect_dma_start(y_rows, bass.IndirectOffsetOnAxis(ap=s["c_ids"][:, r, 1:2], axis=0), s["c_y"][:, r % XDEEP, :], None).then_inc(y_out, 16)

            for i in range(XDEEP):
                gather(i, i)
            over_tiles(pool, step)
            pool.wait_ge(y_out, TILES * 16)

        @block.scalar
        def _(act):
            def turned(i, r):
                act.wait_ge(xT_ps, i + 1)
                once_positive(act, up_ps, i - 1)
                for k in range(KD):
                    last = ac.activation(s["c_xT"][:, r % 2, k, :], ps[:, X_BANK, k * P:(k + 1) * P], ACT.Identity,
                                         bias=s["ln_wb"][:, k, 3:4], scale=s["ln_wb"][:, k, 2:3])
                last.then_inc(xT_ok, 1)

            def gelu(i, r):
                act.wait_ge(up_ps, i + 1)
                once_positive(act, hT_ps, i - 1)
                ac.activation(s["c_h"][:, r % 2, :], ps[:, UP_BANK[r % 2], :], ACT.Gelu_apprx_tanh).then_inc(gelu_ok, 1)

            def load_residual(t, part):
                if part == 0:
                    once_positive(act, res_ok, t * PARTS)
                n, cols = B // PARTS, B * D // PARTS
                act.dma_start(s["c_x1"][:, part * n:(part + 1) * n], x1_of[bass.ds(t * P, P), part * n:(part + 1) * n]).then_inc(res_in, 16)
                act.dma_start(s["residual"][:, bass.ds(t * (B * D) + part * cols, cols)].rearrange("p (b d) -> p b d", b=n),
                              haa_of[bass.ds(t * P, P), part * n:(part + 1) * n]).then_inc(res_in, 16)

            def step(i, r, t):
                if t is not None and r < PARTS:
                    load_residual(t, r)
                if exists(i + 1):
                    gelu(i + 1, r + 1)
                if exists(i + 2):
                    turned(i + 2, r)

            turned(0, 0)
            gelu(0, 0)
            turned(1, 1)
            over_tiles(act, step)

        @block.tensor
        def _(pe):
            def turn_x(i, r):
                pe.wait_ge(x_in[r % XDEEP], loads(i, r))
                once_positive(pe, xT_ok, i)
                for k in range(KD):
                    last = te.transpose(ps[:, X_BANK, k * P:(k + 1) * P], s["c_x"][:, r % XDEEP, k * P:(k + 1) * P], ident[:])
                last.then_inc(xT_ps, 1)

            def up(i, r):
                expert = pe.value_load(s["tile_expert"][0:1, bass.ds(i, 1)], min_val=0, max_val=NEXP - 1)
                pe.wait_ge(xT_ok, i + 1)
                once_positive(pe, gelu_ok, i - 1)
                for k in range(KD):
                    last = te.matmul(ps[:, UP_BANK[r % 2], :], s["c_xT"][:, r % 2, k, :], w_up[:, bass.ds(expert * (KD * FF) + k * FF, FF)],
                                     start=(k == 0), stop=(k == KD - 1))
                last.then_inc(up_ps, 1)

            def turn_h(i, r):
                pe.wait_ge(gelu_ok, i + 1)
                once_positive(pe, hT_ok, i - 1)
                for f in range(FT):
                    last = te.transpose(ps[:, HT_BANK[r % 2], f * P:(f + 1) * P], s["c_h"][:, r % 2, f * P:(f + 1) * P], ident[:])
                last.then_inc(hT_ps, 1)

            def down(i, r):
                expert = pe.value_load(s["tile_expert"][0:1, bass.ds(i, 1)], min_val=0, max_val=NEXP - 1)
                pe.wait_ge(hT_ok, i + 1)
                once_positive(pe, y_ok, i - 1)
                for f in range(FT):
                    last = te.matmul(ps[:, Y_BANK[r % 2], 0:D], s["c_hT"][:, r % 2, f, :], w_down[:, bass.ds(expert * (FT * D) + f * D, D)],
                                     start=(f == 0), stop=(f == FT - 1))
                last.then_inc(y_ps, 1)

            def step(i, r, t):
                turn_h(i, r)
                if exists(i + 1):
                    up(i + 1, r + 1)
                if exists(i + 2):
                    turn_x(i + 2, (r + 2) % DEEP)
                down(i, r)

            pe.wait_ge(weights_in, 16 * 2)
            turn_x(0, 0)
            up(0, 0)
            turn_x(1, 1)
            over_tiles(pe, step)

        @block.vector
        def _(dve):
            def step(i, r, t):
                dve.wait_ge(hT_ps, i + 1)
                once_positive(dve, y_ps, i - 1)
                v.tensor_copy(s["c_hT"][:, r % 2].rearrange("p f t -> p (f t)"), ps[:, HT_BANK[r % 2], :]).then_inc(hT_ok, 1)
                if t is not None and r >= DEEP - PARTS:
                    make_residual(t, r - (DEEP - PARTS))
                dve.wait_ge(y_ps, i + 1)
                once_positive(dve, y_out, (i - XDEEP + 1) * 16)
                v.tensor_copy(s["c_y"][:, r % XDEEP, :], ps[:, Y_BANK[r % 2], 0:D]).then_inc(y_ok, 1)
                if exists(i + AHEAD):
                    hand_out(i + AHEAD, (r + AHEAD) % DEEP)

            def make_residual(t, part):
                cols = B * D // PARTS
                rows = s["residual"][:, bass.ds(t * (B * D) + part * cols, cols)]
                here = lambda x: x[:].rearrange("p b d -> p (b d)")[:, part * cols:(part + 1) * cols]
                if part == 0:
                    dve.wait_ge(res_in, (t + 1) * (32 * PARTS))
                v.tensor_tensor(rows, rows, here(s["gate2"]), ALU.mult).then_inc(res_gated, 1)
                dve.wait_ge(res_gated, t * PARTS + part + 1)
                v.tensor_tensor(rows, rows, here(s["c_x1"]), ALU.add).then_inc(res_ok, 1)

            def hand_out(i, r):
                if r == 0:
                    dve.wait_ge(ids_in, (i + DEEP) * 16)
                once_positive(dve, y_out, (i - DEEP + 1) * 16)
                v.tensor_copy(s["c_ids"][:, r, :], s["c_all_ids"][:, bass.ds(i, 1), :].rearrange("p i c -> p (i c)")).then_inc(ids_ok, 1)

            for i in range(AHEAD):
                hand_out(i, i)
            over_tiles(dve, step)


def pass_four(nc, ctx, y_rows, out, s):
    sem = lambda name: ctx.enter_context(nc.semaphore(name))
    y_in, stored = [[sem(f"{name}_{r}") for r in range(XDEEP)] for name in ("d_y_in", "d_stored")]
    weights_ok, first_ok, both_ok, gated, out_ok = sem("d_weights"), sem("d_first"), sem("d_both"), sem("d_gated"), sem("d_out_ready")
    v, ac = nc.vector, nc.scalar
    y_of = y_rows[0:TOPK * TOK].rearrange("(n l) d -> l n d", l=L)
    out_of = out.rearrange("b l d -> l b d")
    places = [s["w_up"][:].rearrange("p e k f -> p (e k f)"), s["w_down"][:].rearrange("p e f d -> p (e f d)")]
    rows_of = [place.rearrange("p (h n d) -> p h n d", h=2, d=D)[:, h] for place in places for h in range(2)]

    with nc.Block() as block:
        @block.sync
        def _(sp):
            for t in range(XDEEP):
                sp.dma_start(rows_of[t], y_of[t * P:(t + 1) * P]).then_inc(y_in[t], 16)
            for t in range(PT):
                r = t % XDEEP
                sp.wait_ge(out_ok, t + 1)
                sp.dma_start(out_of[t * P:(t + 1) * P], rows_of[r][:, B:]).then_inc(stored[r], 16)
                before = t - 1
                if before >= 0 and before + XDEEP < PT:
                    q = before % XDEEP
                    sp.wait_ge(stored[q], 16 * (before // XDEEP + 1))
                    sp.dma_start(rows_of[q], y_of[(before + XDEEP) * P:(before + XDEEP + 1) * P]).then_inc(y_in[q], 16)
            for r in range(XDEEP):
                sp.wait_ge(stored[r], PT // XDEEP * 16)

        @block.scalar
        def _(act):
            with act.Fori(0, PT // XDEEP) as j:
                for r in range(XDEEP):
                    act.wait_ge(weights_ok, j * XDEEP + r + 1)
                    act.wait_ge(y_in[r], (j + 1) * 16)
                    for b in range(B):
                        last = ac.activation(rows_of[r][:, b], rows_of[r][:, b], ACT.Identity, scale=s["d_w"][:, r, b, 0:1])
                    last.then_inc(first_ok, 1)

        @block.vector
        def _(dve):
            def weights(t, r):
                v.tensor_copy(s["d_w"][:, r], s["wts"][:, bass.ds(t * B, B), :]).then_inc(weights_ok, 1)

            with dve.Fori(0, PT // XDEEP) as j:
                for r in range(XDEEP):
                    weights(j * XDEEP + r, r)
                for r in range(XDEEP):
                    t = j * XDEEP + r
                    y0, y1 = rows_of[r][:, 0:B], rows_of[r][:, B:]
                    dve.wait_ge(first_ok, t + 1)
                    for b in range(B):
                        last = v.scalar_tensor_tensor(y0[:, b, :], y1[:, b, :], s["d_w"][:, r, b, 1:2], y0[:, b, :], ALU.mult, ALU.add)
                    last.then_inc(both_ok, 1)
                    dve.wait_ge(both_ok, t + 1)
                    v.tensor_tensor(y0, y0, s["gate2"][:], ALU.mult).then_inc(gated, 1)
                    dve.wait_ge(gated, t + 1)
                    residual = s["residual"][:, bass.ds(t * (B * D), B * D)]
                    v.tensor_tensor(y1.rearrange("p b d -> p (b d)"), y0.rearrange("p b d -> p (b d)"), residual, ALU.add).then_inc(out_ok, 1)


SHAPES = {
    "quad_mask": [P, QB],    "eye32": [P, C], "levels": [P, LEVELS, C], "chunk_mask": [P, 2, P],
    "w_qkv": [P, KD, 3 * D], "w_beta_mix": [P, KD, P], "w_decay": [P, KD, D], "w_out": [P, KD, D],
    "conv_w": [P, M, TAPS], "onorm": [P, 1], "small_bias": [P, 2 * NH], "cT": [P, KD, B], "wmod": [P, KD, 6 * D],
}
SHARED = dict(ident=[P, P], iota8=[P, NEXP], pad=[P, 1], wts=[P, PT * B, TOPK], minus_half=[P, 8])
SHARED2 = dict(
    next_slot=[P, NEXP], region=[P, NEXP], slot_steps=[P, TILES], ones=[P, P], ln_wb=[P, KD, 4], w_up=[P, NEXP, KD, FF], w_down=[P, NEXP, FT, D],
    shift2=[P, B, D], scale2=[P, B, D], gate2=[P, B, D])
PASS2 = dict(
    w_qkv2=[P, KD, QKV], w_proj=[P, KD, D], w_router=[P, KD, NEXP],
    b_x1=[P, B, D], b_n=[P, B, D], b_h2=[P, 2, B, D], b_nT=[P, KD, B * P], b_st=[P, B, 6], b_mv=[P, B, 2], b_var=[P, 3, B], b_neg_mean=[P, 3, B], b_shift=[P, 3, B], b_r=[P, 3, B],
    b_q=[P, B, D], b_k=[P, B, D], b_v=[P, 2, B, D], b_prod=[P, 2, B, D], scores=[P, B, QH, B], scores_x=[P, B * QH * B],
    b_mx=[P, B * QH], b_den=[P, B * QH], b_attn=[P, B, D],
    b_gate=[P, B, NEXP], b_gm=[P, B], b_gs=[P, B], b_top=[P, B, 8], b_idf=[P, B, 2], b_hot=[P, TOPK, B, NEXP],
    b_chosen=[P, B * NEXP], earlier=[P, P], b_ids_f=[P, TOPK, B, 2], b_scan_in=[P, NEXP, B], b_scan=[P, NEXP, B], scan_reset=[P, NEXP * B],
    b_pos=[P, B, NEXP], b_slot_f=[P, TOPK * B])
PLAN = dict(p_count=[P, NEXP], p_tiles=[P, NEXP], p_until=[P, NEXP], p_tile=[P, TILES],
            p_expert=[P, TILES], p_first=[P, TILES])
PASS3 = dict(c_x1=[P, B, D], c_x=[P, XDEEP, D], c_xT=[P, 2, KD, P], c_h=[P, 2, FF], c_hT=[P, 2, FT, P], c_y=[P, XDEEP, D])
PASS4 = dict(d_w=[P, XDEEP, B, TOPK])
INTEGERS = dict(tile_expert=[P, TILES], tile_slot=[P, TILES])
SETUP = dict(mod=[B, 6 * D], scT=[P, KD, B], gate_sign=[B, D])
PASS1 = dict(
    shift1=[P, G, D], scale1=[P, G, D], gate1=[P, G, D],
    state=[P, B, PAIRS, P], x_in=[P, 2, G, D], x_res=[P, G, D], x1_rows=[P, G, D], y=[P, G, D], ln_st=[P, G, 6], ln_mv=[P, G, 2],
    ln_v=[P, G], ln_r=[P, G], h=[P, G, D], hT=[P, KD, COLS], conv_in=[P, M, B, C + TAPS - 1], conv_acc=[P, M, COLS],
    qkvT=[P, 2, M, COLS], th_decay=[P, PAIRS * COLS], gam=[P, PAIRS * COLS], omg=[P, PAIRS * COLS], ema_hist=[P, PAIRS * B],
    ema_out=[P, 2, PAIRS, COLS], small=[P, G, 2 * NH], th_small=[P, 2, G, 2 * NH], bm=[P, G, 2 * NH], omm=[P, 2, G, NH],
    sq=[P, G, 2 * D], ss=[P, G, 2 * NH], rqk=[P, G, 2 * NH], ema_rows=[P, G, D], mix_e=[P, 2, G, D], mix_d=[P, G, D],
    qkn=[P, G, 2, D], kb=[P, 2, G, D], vb=[P, 2, G, D], k_bd=[P, 2, G, QB, D], knT=[P, G, 2, PAIRS, P], kqT=[P, 2, G, PAIRS, 2, P],
    LA=[P, 2, G, NH, 2, P], Y=[P, G, NH, C], Y0=[P, G, NH, C], T=[P, G, NH, C], TTbd=[P, 2, G, NH, P],
    wT=[P, G, PAIRS, P], un=[P, G, D], o=[P, G, D], osq=[P, G, D], oss=[P, G, NH], orr=[P, G, NH], on=[P, G, D], onT=[P, G, KD, P])


def program(nc, d, x, out):
    x1 = nc.dram_tensor("x1_rows_dram", (B, L, D), F32, kind="Internal").ap()
    haa = nc.dram_tensor("after_attention_dram", (B, L, D), F32, kind="Internal").ap()
    x2n = nc.dram_tensor("x2n_dram", (TOK, D), F32, kind="Internal").ap()
    y_rows = nc.dram_tensor("y_rows_dram", (TOPK * TOK + P, D), F32, kind="Internal").ap()
    table = nc.dram_tensor("table_dram", (SLOTS, 2), U32, kind="Internal").ap()
    mod_rows = nc.dram_tensor("modulation_dram", (B, 6 * D), F32, kind="Internal").ap()
    with ExitStack() as ctx:
        ps = ctx.enter_context(nc.psum_tensor("ps", [P, 8, 512], F32))
        zeroed = ctx.enter_context(nc.semaphore("zeroed"))
        s = {k: ctx.enter_context(nc.sbuf_tensor(k, v, F32)) for k, v in SHARED.items()}
        with ExitStack() as c1:
            s |= {k: c1.enter_context(nc.sbuf_tensor(k, v, F32)) for k, v in {**SHAPES, **SETUP, **PASS1, }.items()}
            setup_constants(nc, ctx, d, s, ps, mod_rows, zeroed)
            pass_one(nc, ctx, x, x1, s, ps)
        s |= {k: ctx.enter_context(nc.sbuf_tensor(k, v, F32)) for k, v in SHARED2.items()}
        s |= {k: ctx.enter_context(nc.sbuf_tensor(k, v, U32)) for k, v in INTEGERS.items()}
        weights_in = ctx.enter_context(nc.semaphore("c_weights_in"))
        with ExitStack() as c2:
            s |= {k: c2.enter_context(nc.sbuf_tensor(k, v, F32)) for k, v in {**PASS2, **PLAN}.items()}
            s["b_idx"] = c2.enter_context(nc.sbuf_tensor("b_idx", [P, B, 8], U32))
            s["b_ids"] = c2.enter_context(nc.sbuf_tensor("b_ids", [P, TOPK, B, 2], U32))
            s["b_slot"] = c2.enter_context(nc.sbuf_tensor("b_slot", [P, TOPK * B], U32))
            pass_two(nc, ctx, x1, haa, x2n.rearrange("(b l) d -> b l d", b=B), table, mod_rows, d, weights_in, s, ps)
        s["residual"] = ctx.enter_context(nc.sbuf_tensor("residual", [P, PT * B * D], F32))
        with ExitStack() as c4:
            s |= {k: c4.enter_context(nc.sbuf_tensor(k, v, F32)) for k, v in PASS3.items()}
            s["c_all_ids"] = c4.enter_context(nc.sbuf_tensor("c_all_ids", [P, TILES, 2], U32))
            s["c_ids"] = c4.enter_context(nc.sbuf_tensor("c_ids", [P, DEEP, 2], U32))
            pass_three(nc, ctx, x1, haa, x2n, table, y_rows, weights_in, s, ps)
        with ExitStack() as c5:
            s |= {k: c5.enter_context(nc.sbuf_tensor(k, v, F32)) for k, v in PASS4.items()}
            pass_four(nc, ctx, y_rows, out, s)
    return x1


def constants():
    p = np.arange(P)
    same = (p[:, None] // C) == (p[None, :] // C)
    row, col = (p % C)[:, None], np.arange(C)[None, :]
    levels = np.stack([((row >> k) & 1 == 1) & ((col >> k) == (row >> k) - 1) for k in range(LEVELS)], 1)
    mask = np.stack([same & (p[None, :] > p[:, None]), same & (p[None, :] >= p[:, None])], 1)
    f = np.float32
    slot, token = np.arange(SLOTS), np.arange(B)[None, None, :] * L + p[:, None, None]
    region = np.tile(np.arange(NEXP, dtype=f) * REGION, (P, 1))
    number = np.stack([np.broadcast_to(token, (P, TOPK, B)), token + np.arange(TOPK)[None, :, None] * TOK], 3)
    return {
            "empty_slots": np.stack([slot % P, TOPK * TOK + slot % P], 1).astype(np.uint32),
            "region": region, "next_slot": region.copy(), "slot_steps": np.tile(np.arange(TILES, dtype=f) * P, (P, 1)),
            "earlier": (p[:, None] < p[None, :]).astype(f), "b_ids_f": np.ascontiguousarray(number.astype(f)),
            "scan_reset": np.tile((np.arange(NEXP * B) % B > 0).astype(f), (P, 1)),
            "ident": np.eye(P, dtype=f), "eye32": np.tile(np.eye(C, dtype=f), (P // C, 1)), "levels": levels.astype(f),
            "chunk_mask": mask.astype(f),
            "quad_mask": (p[:, None] // C == np.arange(QB)[None, :]).astype(f), "iota8": np.tile(np.arange(NEXP, dtype=f), (P, 1))}


def tiles(a):
    a = np.asarray(a)
    return np.ascontiguousarray(a.reshape(-1, P, *a.shape[1:]).swapaxes(0, 1))


def lay_out(i):
    a = {k: np.asarray(v) for k, v in i.items()}
    d = constants()
    d["w_qkv"] = tiles(np.concatenate([a["L0_attn_Wq"], a["L0_attn_Wk"], a["L0_attn_Wv"]], 0).T)
    pad = np.zeros((P - 2 * NH, D), np.float32)
    d["w_beta_mix"] = tiles(np.concatenate([a["L0_attn_Wb"], a["L0_attn_Wmix"], pad], 0).T)
    d["w_decay"] = tiles(np.repeat(a["L0_attn_Wdec"], DH, axis=0).T)
    d["w_out"] = tiles(a["L0_attn_Wo"].T)
    d["conv_w"] = tiles(np.concatenate([a["L0_attn_wq_conv"], a["L0_attn_wk_conv"], a["L0_attn_wv_conv"]], 0))
    d["onorm"] = np.ascontiguousarray(np.tile(a["L0_attn_onorm_w"], P // DH)[:, None])
    d["small_bias"] = np.ascontiguousarray(np.tile(np.concatenate([np.zeros(NH, np.float32), a["L0_attn_mix_bias"]])[None], (P, 1)))
    d["w_qkv2"] = tiles(a["L0_ffn_qkv_weight"].T)
    d["w_proj"] = tiles(a["L0_ffn_proj_weight"].T)
    d["w_router"] = tiles(a["L0_ffn_router_weight"].T)
    d["ln_wb"] = tiles(np.stack([a["L0_ffn_ln1_weight"], a["L0_ffn_ln1_bias"], a["L0_ffn_ln2_weight"], a["L0_ffn_ln2_bias"]], 1))
    d["w_up"] = np.ascontiguousarray(a["L0_ffn_moe_w1"].reshape(NEXP, KD, P, FF).transpose(2, 0, 1, 3))
    d["w_down"] = np.ascontiguousarray(a["L0_ffn_moe_w2"].reshape(NEXP, FT, P, D).transpose(2, 0, 1, 3))
    d["cT"] = tiles(a["L0_c"].T)
    d["wmod"] = tiles(a["L0_wmod"])
    return d, np.ascontiguousarray(a["L0_attn_hidden_states"])


def kernel(**inputs):
    import concourse.bacc as bacc
    from concourse.bass_utils import run_bass_kernel_spmd

    nc = bacc.Bacc("TRN2", target_bir_lowering=False, num_devices=1)
    d, x = lay_out(inputs)
    arrays = {f"{name}_dram": a for name, a in d.items()} | {"x_dram": x}
    aps = {name: nc.dram_tensor(f"{name}_dram", a.shape, mybir.dt.from_np(a.dtype), kind="ExternalInput").ap() for name, a in d.items()}
    x_ap = nc.dram_tensor("x_dram", x.shape, F32, kind="ExternalInput").ap()
    out = nc.dram_tensor("out_0_dram", (B, L, D), F32, kind="ExternalOutput").ap()
    program(nc, aps, x_ap, out)
    r = run_bass_kernel_spmd(nc, [arrays], core_ids=[0])
    return r.results[0]["out_0_dram"]
```
